# Optimizing a Trainium2 kernel written in Bass

```python
import numpy as np
import jax
import jax.numpy as jnp

def _softmax(x, axis=-1):
    return jax.nn.softmax(x, axis=axis)

def _gelu(x):
    return jax.nn.gelu(x, approximate=True)

def _silu(x):
    return jax.nn.silu(x)

def _sigmoid(x):
    return jax.nn.sigmoid(x)

def _layernorm(x, axis=-1, eps=1e-05):
    m = jnp.mean(x, axis=axis, keepdims=True)
    v = jnp.var(x, axis=axis, keepdims=True)
    return (x - m) / jnp.sqrt(v + eps)

def _scatter_add(tgt, idx, src, axis=0):
    return tgt.at[idx].add(src)

def _segment_sum(src, seg, n):
    return jax.ops.segment_sum(src, seg, n)
kernel_name = 'mk_recurrent_d1_jaxref_r8_437048'

def setup_inputs(seed: int=0):
    np.random.seed(seed)
    _w = jnp.asarray

    def _L0_attn_setup():
        import jax, jax.numpy as jnp
        import numpy as np
        import math
        H = 16
        KV = 8
        D = 128
        HID = 256
        LAYER_IDX = 1
        LAMBDA_INIT = 0.8 - 0.6 * math.exp(-0.3 * LAYER_IDX)
        EPS = 1e-05
        key = jax.random.key(seed)
        ks = jax.random.split(key, 8)
        B, S = (2, 256)
        op_size = H * D + 2 * KV * D
        return {'hidden_states': jax.random.normal(ks[0], (B, S, HID), jnp.float32), 'Wqkv_w': jax.random.normal(ks[1], (op_size, HID), jnp.float32) * 0.02, 'Wqkv_b': jnp.zeros((op_size,), jnp.float32), 'lambda_q1': jax.random.normal(ks[2], (D,), jnp.float32) * 0.1, 'lambda_k1': jax.random.normal(ks[3], (D,), jnp.float32) * 0.1, 'lambda_q2': jax.random.normal(ks[4], (D,), jnp.float32) * 0.1, 'lambda_k2': jax.random.normal(ks[5], (D,), jnp.float32) * 0.1, 'subln_w': jnp.ones((2 * D,), jnp.float32), 'out_w': jax.random.normal(ks[6], (HID, H * D), jnp.float32) * 0.02, 'out_b': jnp.zeros((HID,), jnp.float32)}
    _L0_attn_in = _L0_attn_setup()

    def _L0_ffn_setup():
        import jax, jax.numpy as jnp
        import numpy as np
        HIDDEN = 256
        FFN = 704
        N_EXPERTS = 8
        TOP_K = 2
        BATCH, SEQ = (2, 256)
        key = jax.random.key(seed)
        ks = jax.random.split(key, 6)
        s_in = 1.0 / np.sqrt(HIDDEN)
        s_ffn = 1.0 / np.sqrt(FFN)
        return {'hidden_states': jax.random.normal(ks[0], (BATCH, SEQ, HIDDEN), jnp.float32), 'gate_w': jax.random.normal(ks[1], (N_EXPERTS, HIDDEN), jnp.float32) * s_in, 'w_in_gate': jax.random.normal(ks[2], (N_EXPERTS, FFN, HIDDEN), jnp.float32) * s_in, 'w_in_up': jax.random.normal(ks[3], (N_EXPERTS, FFN, HIDDEN), jnp.float32) * s_in, 'w_out': jax.random.normal(ks[4], (N_EXPERTS, HIDDEN, FFN), jnp.float32) * s_ffn, 'bias': jax.random.normal(ks[5], (HIDDEN,), jnp.float32) * 0.02}
    _L0_ffn_in = _L0_ffn_setup()
    _d = {'L0_attn_hidden_states': _L0_attn_in['hidden_states'], 'L0_attn_Wqkv_w': _L0_attn_in['Wqkv_w'], 'L0_attn_Wqkv_b': _L0_attn_in['Wqkv_b'], 'L0_attn_lambda_q1': _L0_attn_in['lambda_q1'], 'L0_attn_lambda_k1': _L0_attn_in['lambda_k1'], 'L0_attn_lambda_q2': _L0_attn_in['lambda_q2'], 'L0_attn_lambda_k2': _L0_attn_in['lambda_k2'], 'L0_attn_subln_w': _L0_attn_in['subln_w'], 'L0_attn_out_w': _L0_attn_in['out_w'], 'L0_attn_out_b': _L0_attn_in['out_b'], 'L0_ffn_gate_w': _L0_ffn_in['gate_w'], 'L0_ffn_w_in_gate': _L0_ffn_in['w_in_gate'], 'L0_ffn_w_in_up': _L0_ffn_in['w_in_up'], 'L0_ffn_w_out': _L0_ffn_in['w_out'], 'L0_ffn_bias': _L0_ffn_in['bias']}
    _x0 = _d['L0_attn_hidden_states']
    _d['L0_attn_hidden_states'] = jax.random.normal(jax.random.fold_in(jax.random.key(seed), 1), (8, 256, 256), dtype=_x0.dtype)
    del _x0
    return _d

def reference(L0_attn_hidden_states, L0_attn_Wqkv_w, L0_attn_Wqkv_b, L0_attn_lambda_q1, L0_attn_lambda_k1, L0_attn_lambda_q2, L0_attn_lambda_k2, L0_attn_subln_w, L0_attn_out_w, L0_attn_out_b, L0_ffn_gate_w, L0_ffn_w_in_gate, L0_ffn_w_in_up, L0_ffn_w_out, L0_ffn_bias):

    def _L0_attn_ref(hidden_states, Wqkv_w, Wqkv_b, lambda_q1, lambda_k1, lambda_q2, lambda_k2, subln_w, out_w, out_b):
        import jax, jax.numpy as jnp
        import numpy as np
        import math
        H = 16
        KV = 8
        D = 128
        HID = 256
        LAYER_IDX = 1
        LAMBDA_INIT = 0.8 - 0.6 * math.exp(-0.3 * LAYER_IDX)
        EPS = 1e-05
        B, S, _ = hidden_states.shape
        qkv = hidden_states @ Wqkv_w.T + Wqkv_b
        q, k, v = jnp.split(qkv, [H * D, H * D + KV * D], axis=-1)
        q = q.reshape(B, S, H // 2, 2, D)
        k = k.reshape(B, S, KV // 2, 2, D)
        v = v.reshape(B, S, KV // 2, 2 * D)
        rep = H // KV
        k = jnp.repeat(k, rep, axis=2)
        v = jnp.repeat(v, rep, axis=2)
        scale = D ** (-0.5)
        causal = jnp.tril(jnp.ones((S, S), bool))
        neg = jnp.finfo(jnp.float32).min

        def attn_map(qi, ki):
            s = jnp.einsum('bqhd,bkhd->bhqk', qi, ki) * scale
            s = jnp.where(causal, s, neg)
            return jax.nn.softmax(s, axis=-1)
        p1 = attn_map(q[:, :, :, 0], k[:, :, :, 0])
        p2 = attn_map(q[:, :, :, 1], k[:, :, :, 1])
        lam1 = jnp.exp(jnp.sum(lambda_q1 * lambda_k1))
        lam2 = jnp.exp(jnp.sum(lambda_q2 * lambda_k2))
        lam = lam1 - lam2 + LAMBDA_INIT
        p = p1 - lam * p2
        o = jnp.einsum('bhqk,bkhe->bqhe', p, v)
        rms = jax.lax.rsqrt(jnp.mean(o * o, axis=-1, keepdims=True) + EPS)
        o = o * rms * subln_w
        o = o * (1.0 - LAMBDA_INIT)
        o = o.reshape(B, S, H * D)
        return o @ out_w.T + out_b

    def _L0_ffn_ref(hidden_states, gate_w, w_in_gate, w_in_up, w_out, bias):
        import jax, jax.numpy as jnp
        import numpy as np
        HIDDEN = 256
        FFN = 704
        N_EXPERTS = 8
        TOP_K = 2
        BATCH, SEQ = (2, 256)
        B, S, D = hidden_states.shape
        x = hidden_states.reshape(-1, D)
        T = x.shape[0]
        logits = jnp.einsum('td,ed->te', x, gate_w)
        top_vals, top_idx = jax.lax.top_k(logits, TOP_K)
        top_w = jax.nn.softmax(top_vals, axis=-1)
        routes = jnp.zeros((T, N_EXPERTS), dtype=x.dtype)
        routes = routes.at[jnp.arange(T)[:, None], top_idx].set(top_w)
        out = jnp.zeros_like(x)
        for e in range(N_EXPERTS):
            g = jnp.einsum('td,fd->tf', x, w_in_gate[e])
            u = jnp.einsum('td,fd->tf', x, w_in_up[e])
            h = jax.nn.silu(g) * u
            y = jnp.einsum('tf,df->td', h, w_out[e])
            out = out + routes[:, e, None] * y
        out = out + bias
        return out.reshape(B, S, D)
    x = L0_attn_hidden_states
    xn = _layernorm(x, axis=-1)
    s = _L0_attn_ref(xn, L0_attn_Wqkv_w, L0_attn_Wqkv_b, L0_attn_lambda_q1, L0_attn_lambda_k1, L0_attn_lambda_q2, L0_attn_lambda_k2, L0_attn_subln_w, L0_attn_out_w, L0_attn_out_b)
    g = _silu(_L0_ffn_ref(xn, L0_ffn_gate_w, L0_ffn_w_in_gate, L0_ffn_w_in_up, L0_ffn_w_out, L0_ffn_bias))
    x = x + s * g
    return x

_drawn_inputs = setup_inputs


def setup_inputs(seed=0):
    import zlib

    import numpy as np

    out = dict(_drawn_inputs(seed))
    spreads = {'L0_attn_Wqkv_b': (0.0, 0.1),
     'L0_attn_subln_w': (1.0, 0.59),
     'L0_attn_out_b': (0.0, 0.362)}
    factors = {'L0_attn_lambda_q1': 8.0,
     'L0_attn_lambda_k1': 64.0,
     'L0_attn_lambda_q2': 64.0,
     'L0_attn_lambda_k2': 8.0,
     'L0_ffn_bias': 8.0}
    for name, (base, spread) in spreads.items():
        noise = np.random.default_rng([zlib.crc32(name.encode()), seed]).standard_normal(out[name].shape)
        drawn = base * np.exp(spread * noise) if base else spread * noise
        out[name] = jnp.asarray(drawn.astype(out[name].dtype))
    for name, factor in factors.items():
        out[name] = (out[name] * factor).astype(out[name].dtype)
    return out
```

```python
import math
from contextlib import ExitStack

import concourse.bass as bass
from concourse import mybir

F32 = mybir.dt.float32
F16 = mybir.dt.float16
I32 = mybir.dt.int32
U32 = mybir.dt.uint32
ALU = mybir.AluOpType
ACT = mybir.ActivationFunctionType
AX = mybir.AxisListType.X
ds = bass.ds

P = 128
B, S, D = 8, 256, 256
T = B * S
NT = T // P
DK = D // P
NH = 8
HD = 128
VD = 256
NG = 4
NU = B * NG
NN = B * NH
NE = 8
FF = 704
FB = FF // P
FR = FF - FB * P
GUW = 2 * FF
NS = 2 * T // P + NE - 1
SLOTS = NS * P
ROW = 516
LAMBDA_INIT = 0.8 - 0.6 * math.exp(-0.3)
EPS = 1e-5
WS = 64.0
ES = 32.0
HS = 16.0
SCALE = HD ** -0.5 / (WS * WS)
MASK = 65504.0


def build(nc, x, wqkv, qkb, vb, lam_in, sub, wo, outb, gw, wgu, wd, fbias, out):
    xrow_dram = nc.dram_tensor("xrow_dram", (SLOTS, ROW // 2), F32, kind="Internal").ap()
    y_dram = nc.dram_tensor("y_dram", (2 * T + SLOTS, D), F32, kind="Internal").ap()
    xT_dram = nc.dram_tensor("xT_dram", (B * P, 4 * S), F16, kind="Internal").ap()
    s_dram = nc.dram_tensor("s_dram", (T, D), F32, kind="Internal").ap()

    with ExitStack() as ctx:
        def sb(name, shape, dt):
            return ctx.enter_context(nc.sbuf_tensor(name, shape, dt))

        def sem(name):
            return ctx.enter_context(nc.semaphore(name))

        GU = sb("GU", [P, NE, DK, 2, GUW], F16)
        gu32 = GU[:, :, :, :, :].rearrange("p e k h n -> p (e k h n)").bitcast(F32)
        EXP32 = DK * GUW
        WQ = gu32[:, 0:8192].rearrange("p (k n) -> p k n", k=DK)
        X0 = gu32[:, 3 * EXP32:3 * EXP32 + NT * D].rearrange("p (t d) -> p t d", t=NT)
        XR0 = 3 * EXP32 + NT * D
        XROW = gu32[:, XR0:XR0 + NT * 2 * ROW // 2].rearrange("p (t k w) -> p t k w", t=NT, k=2)
        XROWH = XROW.bitcast(F16)
        FX = gu32[:, 0:4096].rearrange("p (t d) -> p t d", t=NT)
        FSA = gu32[:, 4096:8192].rearrange("p (t d) -> p t d", t=NT)
        FY = gu32[:, 8192:16384].rearrange("p (k t d) -> p k t d", k=2, t=NT)
        W2 = sb("W2", [P, 24576], F16)
        wqh = W2[:, 0:8192].rearrange("p (k n) -> p k n", k=DK)
        wql = W2[:, 8192:16384].rearrange("p (k n) -> p k n", k=DK)
        woh = W2[:, 16384:20480].rearrange("p (t n) -> p t n", t=16)
        wol = W2[:, 20480:24576].rearrange("p (t n) -> p t n", t=16)
        WD = W2[:, :].rearrange("p (e h b n) -> p e h b n", e=NE, h=2, b=FB + 1)
        stage = sb("stage", [P, 2, 1536], F32)
        WK = sb("WK", [P, 11264], F32)
        at = [0]

        def view(words, dt=F32):
            v = WK[:, at[0]:at[0] + words]
            at[0] += words
            assert at[0] <= 11264
            return v if dt == F32 else v.bitcast(dt)

        xT2 = view(1024, F16).rearrange("p (b k h t) -> p b k h t", b=2, k=DK, h=2)
        rt = view(4096)
        at[0] = 0
        xT = view(512, F16).rearrange("p (k h t) -> p k h t", k=DK, h=2)
        qh = view(1024, F16).rearrange("p (u m t) -> p u m t", u=2, m=4)
        ql = view(1024, F16).rearrange("p (u m t) -> p u m t", u=2, m=4)
        kh = view(512, F16).rearrange("p (u m t) -> p u m t", u=2, m=2)
        kl = view(512, F16).rearrange("p (u m t) -> p u m t", u=2, m=2)
        vh = view(512, F16).rearrange("p (u t n) -> p u t n", u=2, t=2)
        vl = view(512, F16).rearrange("p (u t n) -> p u t n", u=2, t=2)
        v32 = view(512)
        ee = view(2 * 2 * 384).rearrange("p (b m n) -> p b m n", b=2, m=2)
        pc = view(2 * 384).rearrange("p (b n) -> p b n", b=2)
        pth = view(384, F16).rearrange("p (b n) -> p b n", b=2)
        ptl = view(384, F16).rearrange("p (b n) -> p b n", b=2)
        on = view(1024).rearrange("p (b q n) -> p b q n", b=2, q=2)
        oth = view(512, F16).rearrange("p (b n) -> p b n", b=2)
        otl = view(512, F16).rearrange("p (b n) -> p b n", b=2)
        junk = view(512).rearrange("p (q n) -> p q n", q=2)
        so = view(512)
        at[0] = 0
        xg = view(4 * ROW // 2).rearrange("p (b w) -> p b w", b=4)
        xgh = xg.bitcast(F16)
        xgT = view(512, F16).rearrange("p (b n) -> p b n", b=2)
        sg = view(2 * 768).rearrange("p (b n) -> p b n", b=2)
        h32 = view(2 * 768).rearrange("p (b n) -> p b n", b=2)
        hh = view(768, F16).rearrange("p (b n) -> p b n", b=2)
        hl = view(768, F16).rearrange("p (b n) -> p b n", b=2)
        yy = view(1024).rearrange("p (b n) -> p b n", b=4)

        ident16 = sb("ident16", [P, P], F16)
        ident32 = sb("ident32", [P, P], F32)
        maskl = sb("maskl", [P, P], F16)
        maskr = sb("maskr", [P, P], F16)
        sut = sb("sut", [P, P], F16)
        ones16 = sb("ones16", [P, P], F16)
        es_c = sb("es_c", [P, 1], F32)
        half_c = sb("half_c", [P, 4], F32)
        zrow = sb("zrow", [P, 256], F32)
        padf = sb("padf", [P, NS, 2], I32)
        rev = sb("rev", [P, NE], F32)
        revi = sb("revi", [P, NE], I32)
        ti = sb("ti", [P, NS], I32)
        tf = sb("tf", [P, NS], F32)
        qkb_s = sb("qkb_s", [P, 24], F32)
        qkb64 = sb("qkb64", [P, 24], F32)
        vb_s = sb("vb_s", [P, NG, VD], F32)
        ob_s = sb("ob_s", [P, D], F32)
        fb_s = sb("fb_s", [P, D], F32)
        lam_s = sb("lam_s", [P, 4, HD], F32)
        sub_s = sb("sub_s", [P, 2], F32)
        gw_s = sb("gw_s", [P, DK, NE], F32)
        gwh = sb("gwh", [P, DK, NE], F16)
        gwl = sb("gwl", [P, DK, NE], F16)
        sm = sb("sm", [P, 64], F32)
        cf = sb("cf", [P, 2, 2], F32)
        co = sb("co", [P, 1], F32)
        mean = sb("mean", [P, NT], F32)
        rstd = sb("rstd", [P, NT], F32)
        mx = sb("mx", [P, 2, 2, 2], F32)
        ngm = sb("ngm", [P, 2, 2, 2], F32)
        rs = sb("rs", [P, 2, 2, 2], F32)
        ri = sb("ri", [P, 2, 2, 2], F32)
        al = sb("al", [P, 2, 2, 2], F32)
        ss = sb("ss", [P, 2, 2], F32)
        ms = sb("ms", [P, 2, 2], F32)
        rm = sb("rm", [P, 2, 2], F32)
        rc = sb("rc", [P, 2, 2], F32)

        ra = [0]

        def rview(*shape):
            n = int(math.prod(shape))
            v = rt[:, ra[0]:ra[0] + n]
            ra[0] += n
            if len(shape) == 2:
                v = v.rearrange("p (a b) -> p a b", a=shape[0])
            return v

        L = rview(NT, NE)
        L2 = rview(NT, NE)
        m1 = rview(NT)
        m2 = rview(NT)
        km = rview(NT)
        km2 = rview(NT)
        eq = rview(NT, NE)
        eq2 = rview(NT, NE)
        key = rview(NT, NE)
        key2 = rview(NT, NE)
        oh1 = rview(NT, NE)
        oh2 = rview(NT, NE)
        M16 = rview(64).bitcast(F16)
        pre = rview(NT, NE)
        tot = rview(NT, NE)
        scA = [rview(NT, NE) for _ in range(4)]
        cnt = rview(NE)
        cnti = rview(NE).bitcast(I32)
        cnts = rview(NE).bitcast(I32)
        tls = rview(NE)
        scE = [rview(NE) for _ in range(3)]
        base = rview(NE)
        slot = rview(NT, NE)
        slot2 = rview(NT, NE)
        ps1 = rview(NT, NE)
        ps2 = rview(NT, NE)
        slf = rview(2, NT)
        dd = rview(NT)
        ex = rview(NT)
        ex1 = rview(NT)
        w1 = rview(NT)
        w2 = rview(NT)
        te = rview(NS, NE - 1)
        tef = rview(NS)
        texp = sb("texp", [P, NS], I32)
        sli = sb("sli", [P, 2, NT], I32)

        PS = ctx.enter_context(nc.psum_tensor("PS", [P, 8, 512], F32))
        PSH = [PS[:, i, :].bitcast(F16) for i in range(8)]
        bPJ = [PS[:, 0, :], PS[:, 1, :]]
        bS = PS[:, 2:4, :]
        bPT, bPV, bOT, bOUT = (PS[:, i, :] for i in (4, 5, 6, 7))

        s_x_in = sem("s_x_in")
        s_wq_in = sem("s_wq_in")
        s_small_in = sem("s_small_in")
        s_wo_in = [sem(f"s_wo_in{i}") for i in range(2)]
        s_consts = sem("s_consts")
        s_xchain = sem("s_xchain")
        s_xn_ready = sem("s_xn_ready")
        s_xrow_ready = sem("s_xrow_ready")
        s_pt0_ready = sem("s_pt0_ready")
        s_xTev = sem("s_xTev")
        s_xT_out = [sem(f"s_xT_out{i}") for i in range(2)]
        s_gw_ready = sem("s_gw_ready")
        s_lg_ready = sem("s_lg_ready")
        s_route = sem("s_route")
        s_dd_ready = sem("s_dd_ready")
        s_M_ready = sem("s_M_ready")
        s_pre_ready = sem("s_pre_ready")
        s_slots_ready = sem("s_slots_ready")
        s_texp_ready = sem("s_texp_ready")
        s_fields = sem("s_fields")
        s_pads_ready = sem("s_pads_ready")
        s_zpad_out = sem("s_zpad_out")
        s_scat_out = sem("s_scat_out")
        s_wqhi = sem("s_wqhi")
        s_wqlo = sem("s_wqlo")
        s_wo_scaled = sem("s_wo_scaled")
        s_wohi = sem("s_wohi")
        s_wolo = sem("s_wolo")
        s_achain = sem("s_achain")
        s_lam_ready = sem("s_lam_ready")
        s_prep_done = sem("s_prep_done")
        s_expw = sem("s_expw")
        s_xT_in = sem("s_xT_in")
        s_proj = sem("s_proj")
        s_projhi = sem("s_projhi")
        s_projlo = sem("s_projlo")
        s_v32_ready = sem("s_v32_ready")
        s_vhi_ready = sem("s_vhi_ready")
        s_vlo_ready = sem("s_vlo_ready")
        s_scores = sem("s_scores")
        s_maxed = sem("s_maxed")
        s_negm = sem("s_negm")
        s_exped = sem("s_exped")
        s_rsum_inv = sem("s_rsum_inv")
        s_coef = sem("s_coef")
        s_pscaled = sem("s_pscaled")
        s_pcomb = sem("s_pcomb")
        s_pT = sem("s_pT")
        s_pThi = sem("s_pThi")
        s_pTlo = sem("s_pTlo")
        s_pv = sem("s_pv")
        s_sumsq = sem("s_sumsq")
        s_meansq = sem("s_meansq")
        s_rms = sem("s_rms")
        s_ocoef = sem("s_ocoef")
        s_onorm = sem("s_onorm")
        s_oT = sem("s_oT")
        s_oThi = sem("s_oThi")
        s_oTlo = sem("s_oTlo")
        s_heads_out = sem("s_heads_out")
        s_so_ready = sem("s_so_ready")
        s_s_out = sem("s_s_out")
        s_gu_in = [sem(f"s_gu_in{i}") for i in range(2)]
        s_gu_mul = sem("s_gu_mul")
        s_gu_split = sem("s_gu_split")
        s_wd_in = [sem(f"s_wd_in{i}") for i in range(2)]
        s_wdhi = sem("s_wdhi")
        s_wdlo = sem("s_wdlo")
        s_xg_in = [sem(f"s_xg_in{i}") for i in range(4)]
        s_xgTp = sem("s_xgTp")
        s_xgT_ready = sem("s_xgT_ready")
        s_gup = sem("s_gup")
        s_silu = sem("s_silu")
        s_hmul = sem("s_hmul")
        s_hhi = sem("s_hhi")
        s_hlo = sem("s_hlo")
        s_yp = sem("s_yp")
        s_yev = sem("s_yev")
        s_y_out = [sem(f"s_y_out{i}") for i in range(4)]
        s_scatter_turn = sem("s_scatter_turn")
        s_fin_in = sem("s_fin_in")
        s_fin_sum = sem("s_fin_sum")
        s_fin_add = sem("s_fin_add")
        s_fin_mul = sem("s_fin_mul")
        s_fin_silu = sem("s_fin_silu")
        s_fin_done = sem("s_fin_done")
        s_fin_out = sem("s_fin_out")

        def pos(value):
            return not isinstance(value, int) or value > 0

        block = ctx.enter_context(nc.Block())

        def steps(eng, step):
            for j in range(NH):
                step(0, j)
            with eng.Fori(1, B - 1) as b:
                for j in range(NH):
                    step(b, j)
            for j in range(NH + 2):
                step(B - 1, j)

        def has(n, lag):
            return not isinstance(n, int) or 0 <= n - lag < NN

        def has_proj(n):
            return not isinstance(n, int) or n < NN - 2

        def ahead(b, j):
            u = b * NG + (j + 2) // 2
            return u, (j + 2) // 2 % NG, (j + 2) // 2 % 2

        def tiles(eng, step):
            for j in range(4):
                step(0, j)
            with eng.Fori(1, NS // 4) as t:
                for j in range(4):
                    step(t, j)
            for j in range(NS % 4 + 1):
                step(NS // 4, j)

        def prepared(eng):
            eng.wait_ge(s_prep_done, 1)
            eng.wait_ge(s_lg_ready, NT)
            eng.wait_ge(s_xT_out[0], 16 * B // 2)
            eng.wait_ge(s_xT_out[1], 16 * B // 2)

        @block.sync
        def _(eng):
            eng.dma_start(X0, x.rearrange("(t p) d -> p t d", p=P)).then_inc(s_x_in, 16)
            eng.dma_start(gw_s[:, :, :], gw).then_inc(s_small_in, 16)
            eng.dma_start(qkb_s[:, :], qkb).then_inc(s_small_in, 16)
            eng.dma_start(sub_s[:, :], sub).then_inc(s_small_in, 16)
            eng.dma_start(lam_s[:, :, :].rearrange("p a b -> p (a b)"), lam_in.partition_broadcast(P)).then_inc(s_small_in, 16)
            eng.dma_start(vb_s[:, :, :].rearrange("p a b -> p (a b)"), vb.partition_broadcast(P)).then_inc(s_small_in, 16)
            eng.dma_start(ob_s[:, :], outb.partition_broadcast(P)).then_inc(s_small_in, 16)
            eng.dma_start(fb_s[:, :], fbias.partition_broadcast(P)).then_inc(s_small_in, 16)
            eng.dma_start(WQ, wqkv).then_inc(s_wq_in, 16)
            for c in range(2):
                eng.dma_start(stage[:, c, 0:1024], wo[:, 1024 * c:1024 * c + 1024]).then_inc(s_wo_in[c], 16)
            eng.wait_ge(s_pads_ready, 1)
            for t in range(NS):
                eng.dma_start(xrow_dram[t * P:t * P + P, 0:256], zrow[:, :]).then_inc(s_zpad_out, 16)
            eng.dma_start(xrow_dram.rearrange("(t p) w -> p t w", p=P)[:, :, 256:258], padf[:, :, :].bitcast(F32)).then_inc(s_zpad_out, 16)
            for c in range(2, 4):
                eng.wait_ge(s_wohi, c - 1)
                eng.wait_ge(s_wolo, c - 1)
                eng.dma_start(stage[:, c % 2, 0:1024], wo[:, 1024 * c:1024 * c + 1024]).then_inc(s_wo_in[c % 2], 16)

            def load_xT(b):
                eng.dma_start(xT.rearrange("p k h t -> p (k h t)"), xT_dram[ds(b * P, P), :]).then_inc(s_xT_in, 16)

            def load_gu(e, k):
                if pos(e * 8 + k * 4 - 4):
                    eng.wait_ge(s_gu_split, e * 8 + k * 4 - 4)
                src = wgu[ds(e, 1), :, k, :].rearrange("a p n -> (a p) n")
                eng.dma_start(stage[:, k, 0:GUW], src).then_inc(s_gu_in[k], 16)

            def store_s(b):
                eng.wait_ge(s_so_ready, b + 1)
                eng.dma_start(s_dram[ds(b * S, S), :].rearrange("(q p) d -> p q d", p=P),
                              so.rearrange("p (q d) -> p q d", q=2)).then_inc(s_s_out, 16)

            prepared(eng)
            load_xT(0)
            eng.wait_ge(s_wohi, 4)
            eng.wait_ge(s_wolo, 4)
            load_gu(0, 0)
            load_gu(0, 1)
            load_gu(1, 0)
            with eng.Fori(1, B - 1) as b:
                if pos(b * 16):
                    eng.wait_ge(s_proj, b * 16)
                load_xT(b)
                load_gu(b, 1)
                store_s(b - 1)
                load_gu(b + 1, 0)
            eng.wait_ge(s_proj, (B - 1) * 16)
            load_xT(B - 1)
            load_gu(B - 1, 1)
            store_s(B - 2)
            store_s(B - 1)
            eng.wait_ge(s_s_out, 16 * B)
            eng.wait_ge(s_gu_split, 8 * NE)
            for e in range(NE):
                if e >= 2:
                    if pos(e - 1):
                        eng.wait_ge(s_wdhi, e - 1)
                    if pos(e - 1):
                        eng.wait_ge(s_wdlo, e - 1)
                st = stage[:, e % 2, :].rearrange("p (b n) -> p b n", b=FB + 1)
                eng.dma_start(st[:, 0:FB, :], wd[e, 0:FB * P, :].rearrange("(b p) n -> p b n", p=P)).then_inc(s_wd_in[e % 2], 16)
                eng.dma_start(st[0:FR, FB, :], wd[e, FB * P:FF, :]).then_inc(s_wd_in[e % 2], 16)

            def load(t, j):
                if isinstance(t, int) and 4 * t + j >= NS:
                    return
                if pos(t * 16):
                    eng.wait_ge(s_y_out[j], t * 16)
                eng.dma_start(xg[:, j, :], xrow_dram[ds(t * (4 * P) + j * P, P), :]).then_inc(s_xg_in[j], 16)

            eng.wait_ge(s_scat_out, 16 * 2 * NT)
            tiles(eng, load)
            for j in range(4):
                eng.wait_ge(s_y_out[j], 16 * ((NS + 3 - j) // 4))
            eng.dma_start(FX, x.rearrange("(t p) d -> p t d", p=P)).then_inc(s_fin_in, 16)
            eng.dma_start(FSA, s_dram.rearrange("(t p) d -> p t d", p=P)).then_inc(s_fin_in, 16)
            for k in range(2):
                eng.dma_start(FY[:, k, :, :], y_dram[k * T:k * T + T, :].rearrange("(t p) d -> p t d", p=P)).then_inc(s_fin_in, 16)
            for q in range(4):
                eng.wait_ge(s_fin_done, 2 * q + 2)
                eng.dma_start(out[q * 512:q * 512 + 512, :].rearrange("(t p) d -> p t d", p=P), FX[:, 4 * q:4 * q + 4, :]).then_inc(s_fin_out, 16)
            eng.wait_ge(s_fin_out, 64)

        @block.gpsimd
        def _(eng):
            eng.memset(ident16[:, :], 0.0).then_inc(s_consts, 1)
            eng.memset(ident32[:, :], 0.0).then_inc(s_consts, 1)
            eng.memset(maskl[:, :], 0.0).then_inc(s_consts, 1)
            eng.memset(maskr[:, :], 0.0).then_inc(s_consts, 1)
            eng.memset(sut[:, :], 1.0).then_inc(s_consts, 1)
            eng.wait_ge(s_consts, 5)
            for m, v in ((ident16, 1.0), (ident32, 1.0), (maskl, MASK)):
                eng.affine_select(out=m[:, :], in_=m[:, :], compare_op=ALU.not_equal, fill=v, base=0,
                                  pattern=[[-1, P]], channel_multiplier=1).then_inc(s_consts, 1)
            eng.affine_select(out=maskr[:, :], in_=maskr[:, :], compare_op=ALU.is_ge, fill=-MASK, base=0,
                              pattern=[[-1, P]], channel_multiplier=1).then_inc(s_consts, 1)
            eng.affine_select(out=sut[:, :], in_=sut[:, :], compare_op=ALU.is_ge, fill=0.0, base=-1,
                              pattern=[[1, P]], channel_multiplier=-1).then_inc(s_consts, 1)
            eng.memset(ones16[:, :], 1.0).then_inc(s_consts, 1)
            eng.memset(es_c[:, :], ES).then_inc(s_consts, 1)
            eng.memset(half_c[:, :], -0.5).then_inc(s_consts, 1)
            eng.memset(zrow[:, :], 0.0).then_inc(s_consts, 1)
            eng.memset(padf[:, :, 1], 0).then_inc(s_consts, 1)
            eng.iota(padf[:, :, 0], pattern=[[P, NS]], base=2 * T, channel_multiplier=1).then_inc(s_consts, 1)
            eng.iota(revi[:, :], pattern=[[-1, NE]], base=NE, channel_multiplier=0).then_inc(s_consts, 1)
            eng.iota(ti[:, :], pattern=[[1, NS]], base=0, channel_multiplier=0).then_inc(s_consts, 1)
            eng.wait_ge(s_consts, 18)
            eng.tensor_copy(rev[:, :], revi[:, :]).then_inc(s_pads_ready, 1)
            eng.iota(XROW[:, :, :, 256].bitcast(I32), pattern=[[P, NT], [T, 2]], base=0, channel_multiplier=1).then_inc(s_fields, 1)
            for b in range(B):
                eng.wait_ge(s_xTev, 2 * b + 2)
                eng.dma_start(xT_dram[b * P:b * P + P, :],
                              xT2[:, b % 2, :, :, :].rearrange("p k h t -> p (k h t)")).then_inc(s_xT_out[b % 2], 16)

            def dispatch(t):
                for k in range(2):
                    eng.indirect_dma_start(xrow_dram, bass.IndirectOffsetOnAxis(ap=sli[:, k, t:t + 1].bitcast(U32), axis=0),
                                           XROW[:, t, k, :], None).then_inc(s_scat_out, 16)

            def value_lo(b, j):
                u, _, up = ahead(b, j)
                if not has_proj(b * NH + j) or j % 2 == 0:
                    return
                eng.wait_ge(s_vhi_ready, u + 1)
                eng.tensor_tensor(vl[:, up, :, :].rearrange("p t n -> p (t n)"), v32,
                                  vh[:, up, :, :].rearrange("p t n -> p (t n)"), ALU.subtract).then_inc(s_vlo_ready, 1)

            def split(b, j):
                if j >= NH:
                    return
                k, q = j // 4, j % 4
                c = slice(q * GUW // 4, (q + 1) * GUW // 4)
                w = stage[:, k, c]
                hi = GU[:, ds(b, 1), k, 0, c].rearrange("p a n -> p (a n)")
                lo = GU[:, ds(b, 1), k, 1, c].rearrange("p a n -> p (a n)")
                sc = es_c[:, 0:1].to_broadcast([P, GUW // 4])
                eng.wait_ge(s_gu_in[k], b * 16 + 16)
                eng.tensor_tensor(hi, w, sc, ALU.mult).then_inc(s_gu_mul, 1)
                eng.tensor_tensor(w, w, sc, ALU.mult).then_inc(s_gu_mul, 1)
                eng.wait_ge(s_gu_mul, b * 16 + (2 * j + 2))
                eng.tensor_tensor(lo, w, hi, ALU.subtract).then_inc(s_gu_split, 1)

            def root(b, j, lag):
                n, par = b * NH + j, (j + lag) % 2
                if not has(n, lag):
                    return
                eng.wait_ge(s_meansq, n - lag + 1)
                eng.tensor_tensor(rm[:, par, :], ms[:, par, :], half_c[:, 0:2], ALU.pow).then_inc(s_rms, 1)

            def step(b, j):
                root(b, j, 1)
                value_lo(b, j)
                if isinstance(b, int) and b == 0:
                    dispatch(2 * j)
                    dispatch(2 * j + 1)
                    if j == NH - 1:
                        eng.wait_ge(s_scat_out, 16 * 2 * NT)
                split(b, j)

            prepared(eng)
            value_lo(0, -1)
            eng.wait_ge(s_slots_ready, 1)
            eng.wait_ge(s_fields, 3)
            eng.wait_ge(s_xrow_ready, 2)
            eng.wait_ge(s_zpad_out, 16 * (NS + 1))
            eng.wait_ge(s_wqlo, 1)
            steps(eng, step)

            def scatter(t, j):
                i = t * 4 + j
                if isinstance(i, int) and i == 0:
                    return
                if pos(i):
                    eng.wait_ge(s_yev, i)
                eng.sem_inc(s_scatter_turn, 1)
                q = (j + 3) % 4
                eng.indirect_dma_start(y_dram, bass.IndirectOffsetOnAxis(ap=xg[:, q, 256:257].bitcast(U32), axis=0),
                                       yy[:, q, :], None).then_inc(s_y_out[q], 16)

            tiles(eng, scatter)
            for j in range(4):
                eng.wait_ge(s_y_out[j], 16 * ((NS + 3 - j) // 4))

        def three(o, ah, al_, bh, bl, first, last, **kw):
            nc.tensor.matmul(o, ah, bh, start=first, stop=False, **kw)
            nc.tensor.matmul(o, al_, bh, start=False, stop=False, **kw)
            return nc.tensor.matmul(o, ah, bl, start=False, stop=last, **kw)

        @block.tensor
        def _(eng):
            eng.wait_ge(s_consts, 18)
            eng.wait_ge(s_xrow_ready, 1)
            eng.wait_ge(s_gw_ready, 2)

            def logits(t):
                b, tt = t // 2, t % 2
                eng.wait_ge(s_xTev, t + 1)
                for k in range(DK):
                    xs = [xT2[:, b % 2, k, h, tt * P:tt * P + P] for h in range(2)]
                    l = three(PS[:, 6, t * NE:t * NE + NE], xs[0], xs[1], gwh[:, k, :], gwl[:, k, :], k == 0, k == DK - 1)
                l.then_inc(s_lg_ready, 1)

            for t in range(NT):
                if t >= 2:
                    if pos(t - 1):
                        eng.wait_ge(s_xTev, t - 1)
                for q in range(4):
                    l = nc.tensor.transpose(PSH[t % 2][:, q * P:q * P + P], XROWH[:, t, 0, q * P:q * P + P], ident16[:, :])
                l.then_inc(s_pt0_ready, 1)
                if t >= 1:
                    logits(t - 1)
            logits(NT - 1)
            eng.wait_ge(s_M_ready, 1)
            nc.tensor.matmul(PS[:, 7, 0:P], sut[:, :], M16, start=True, stop=True)
            nc.tensor.matmul(PS[:, 7, P:2 * P], ones16[:, :], M16, start=True, stop=True).then_inc(s_pre_ready, 1)

            def proj(b, j, i):
                u, g, _ = ahead(b, j)
                if not has_proj(b * NH + j):
                    return
                if g == 0 and j % 2 == 0 and i == 0:
                    eng.wait_ge(s_xT_in, (b * 16 if j < 0 else b * 16 + 16) + 16)
                bank = bPJ[i]
                if j % 2 == 0 and i == 1:
                    if pos(u):
                        eng.wait_ge(s_v32_ready, u)
                elif pos(u * 3 + (i + 1 if j % 2 else 0)):
                    eng.wait_ge(s_projhi, u * 3 + (i + 1 if j % 2 else 0))
                    eng.wait_ge(s_projlo, u * 3 + (i + 1 if j % 2 else 0))
                if j % 2 == 1 and i == 1:
                    vc = slice(3072 + g * VD, 3072 + g * VD + VD)
                    for tt in range(2):
                        tk = slice(tt * P, tt * P + P)
                        for k in range(DK):
                            l = three(bank[:, tt * VD:tt * VD + VD], xT[:, k, 0, tk], xT[:, k, 1, tk],
                                      wqh[:, k, vc], wql[:, k, vc], k == 0, k == DK - 1)
                else:
                    c0 = (g * 512 + i * 256) if j % 2 == 0 else 2048 + g * 256
                    for m in range(2):
                        c = c0 + m * P
                        for k in range(DK):
                            l = three(bank[:, m * S:m * S + S], wqh[:, k, c:c + P], wql[:, k, c:c + P],
                                      xT[:, k, 0, :], xT[:, k, 1, :], k == 0, k == DK - 1)
                l.then_inc(s_proj, 1)

            def score(b, j):
                n = b * NH + j
                if not has(n, 0):
                    return
                up, h = (j // 2) % 2, j % 2
                eng.wait_ge(s_projhi, (b * NG + j // 2) * 3 + 3)
                eng.wait_ge(s_projlo, (b * NG + j // 2) * 3 + 3)
                if pos(n):
                    eng.wait_ge(s_exped, n)
                for m in range(2):
                    q0, q1 = slice(0, P), slice(P, 2 * P)
                    hm = 2 * h + m
                    three(bS[:, m, 0:P], qh[:, up, hm, q0], ql[:, up, hm, q0], kh[:, up, m, q0], kl[:, up, m, q0], True, False)
                    nc.tensor.matmul(bS[:, m, 0:P], maskl[:, :], maskr[:, :], start=False, stop=True)
                    three(bS[:, m, P:3 * P], qh[:, up, hm, q1], ql[:, up, hm, q1], kh[:, up, m, :], kl[:, up, m, :], True, False)
                    l = nc.tensor.matmul(bS[:, m, 2 * P:3 * P], maskl[:, :], maskr[:, :], start=False, stop=True)
                l.then_inc(s_scores, 1)

            def transpose_p(b, j):
                n, par = b * NH + j, (j + 1) % 2
                if not has(n, 1):
                    return
                eng.wait_ge(s_pcomb, n)
                if pos(n - 1):
                    eng.wait_ge(s_pThi, n - 1)
                    eng.wait_ge(s_pTlo, n - 1)
                for q in range(3):
                    l = nc.tensor.transpose(bPT[:, q * P:q * P + P], pc[:, par, q * P:q * P + P], ident32[:, :])
                l.then_inc(s_pT, 1)

            def weigh_values(b, j):
                n, par, up = b * NH + j, (j + 1) % 2, (j - 1) // 2 % 2
                if not has(n, 1):
                    return
                eng.wait_ge(s_pThi, n)
                eng.wait_ge(s_pTlo, n)
                eng.wait_ge(s_vlo_ready, b * NG + (j - 1) // 2 + 1)
                if pos(n - 1):
                    eng.wait_ge(s_onorm, n - 1)
                v = [(vh[:, up, t, :], vl[:, up, t, :]) for t in range(2)]
                three(bPV[:, 0:VD], pth[:, par, 0:P], ptl[:, par, 0:P], *v[0], True, True)
                three(bPV[:, VD:2 * VD], pth[:, par, P:2 * P], ptl[:, par, P:2 * P], *v[0], True, False)
                l = three(bPV[:, VD:2 * VD], pth[:, par, 2 * P:3 * P], ptl[:, par, 2 * P:3 * P], *v[1], False, True)
                l.then_inc(s_pv, 1)

            def transpose_o(b, j):
                n, par = b * NH + j, j % 2
                if not has(n, 2):
                    return
                eng.wait_ge(s_onorm, n - 1)
                if pos(n - 2):
                    eng.wait_ge(s_oThi, n - 2)
                    eng.wait_ge(s_oTlo, n - 2)
                for q in range(2):
                    for eb in range(2):
                        l = nc.tensor.transpose(bOT[:, (q * 2 + eb) * P:(q * 2 + eb + 1) * P], on[:, par, q, eb * P:eb * P + P], ident32[:, :])
                l.then_inc(s_oT, 1)

            def project_out(b, j):
                n, par, hd = b * NH + j, j % 2, (j + NH - 2) % NH
                if not has(n, 2):
                    return
                eng.wait_ge(s_oThi, n - 1)
                eng.wait_ge(s_oTlo, n - 1)
                if hd == 0 and pos(b):
                    eng.wait_ge(s_so_ready, b)
                for q in range(2):
                    for eb in range(2):
                        c = (q * 2 + eb) * P
                        l = three(bOUT[:, q * D:q * D + D], oth[:, par, c:c + P], otl[:, par, c:c + P],
                                  woh[:, 2 * hd + eb, :], wol[:, 2 * hd + eb, :],
                                  hd == 0 and q == 0 and eb == 0, hd == NH - 1 and q == 1 and eb == 1, skip_group_check=True)
                l.then_inc(s_heads_out, 1)

            def step(b, j):
                score(b, j)
                transpose_p(b, j)
                proj(b, j, 0)
                transpose_o(b, j)
                weigh_values(b, j)
                proj(b, j, 1)
                project_out(b, j)

            eng.wait_ge(s_wqhi, 1)
            eng.wait_ge(s_wqlo, 1)
            eng.wait_ge(s_slots_ready, 1)
            for j in (-2, -1):
                proj(0, j, 0)
                proj(0, j, 1)
            eng.wait_ge(s_wohi, 4)
            eng.wait_ge(s_wolo, 4)
            steps(eng, step)

            def xt(t, j):
                t, j = t + j // 4, j % 4
                eng.wait_ge(s_xg_in[j], t * 16 + 16)
                if pos(t * 4 + j):
                    eng.wait_ge(s_xgT_ready, t * 4 + j)
                for q in range(4):
                    l = nc.tensor.transpose(PSH[7][:, q * P:q * P + P], xgh[:, j, q * P:q * P + P], ident16[:, :])
                l.then_inc(s_xgTp, 1)

            GUC = [(0, 0), (0, 128), (0, 256), (0, 384), (1, 0), (1, 128), (1, 256), (2, 0), (2, 128), (2, 256), (2, 384)]

            def tile(t, j):
                i = t * 4 + j
                if not isinstance(i, int) or i < NS:
                    e = eng.value_load(texp[0:1, ds(i, 1)], min_val=0, max_val=NE - 1)
                if not isinstance(i, int) or i >= 1:
                    e1 = eng.value_load(texp[0:1, ds(i - 1, 1)], min_val=0, max_val=NE - 1)
                if not isinstance(i, int) or i < NS:
                    par = j % 2
                    eng.wait_ge(s_xgT_ready, i + 1)
                    if pos(i - 1):
                        eng.wait_ge(s_hmul, i - 1)
                    for c, (bank, col) in enumerate(GUC):
                        o = PS[:, 3 * par + bank, col:col + P]
                        for k in range(DK):
                            w = [GU[:, ds(e, 1), k, h, c * P:c * P + P].rearrange("p a n -> p (a n)") for h in range(2)]
                            xs = [xgT[:, par, (k * 2 + h) * P:(k * 2 + h + 1) * P] for h in range(2)]
                            nc.tensor.matmul(o, w[0], xs[0], start=k == 0, stop=False)
                            nc.tensor.matmul(o, w[0], xs[1], start=False, stop=False)
                            l = nc.tensor.matmul(o, w[1], xs[0], start=False, stop=k == DK - 1)
                    l.then_inc(s_gup, 1)
                    if not isinstance(i, int) or i + 1 < NS:
                        xt(t, j + 1)
                if not isinstance(i, int) or i >= 1:
                    par = (j + 1) % 2
                    if pos(i):
                        eng.wait_ge(s_hhi, i)
                    if pos(i):
                        eng.wait_ge(s_hlo, i)
                    if pos(i - 1):
                        eng.wait_ge(s_yev, i - 1)
                    for c in range(FB + 1):
                        r = P if c < FB else FR
                        w = [WD[0:r, ds(e1, 1), h, c, :].rearrange("p a n -> p (a n)") for h in range(2)]
                        l = three(PS[:, 6, 0:D], hh[0:r, par, c * P:c * P + P], hl[0:r, par, c * P:c * P + P], w[0], w[1], c == 0, c == FB)
                    l.then_inc(s_yp, 1)

            eng.wait_ge(s_gu_split, 8 * NE)
            eng.wait_ge(s_texp_ready, 1)
            eng.wait_ge(s_so_ready, B)
            xt(0, 0)
            eng.wait_ge(s_wdhi, NE)
            eng.wait_ge(s_wdlo, NE)
            tiles(eng, tile)

        @block.scalar
        def _(eng):
            act = eng.activation
            eng.wait_ge(s_small_in, 16 * 7)
            act(gwh[:, :, :], gw_s[:, :, :], ACT.Copy, scale=WS).then_inc(s_gw_ready, 1)
            act(qkb64[:, :], qkb_s[:, :], ACT.Copy, scale=WS).then_inc(s_lam_ready, 1)
            eng.wait_ge(s_wq_in, 16)
            act(wqh, WQ, ACT.Copy, scale=WS).then_inc(s_wqhi, 1)
            eng.wait_ge(s_xn_ready, 1)
            act(XROWH[:, :, 0, 0:512].rearrange("p t (k h d) -> p t k h d", k=DK, h=2)[:, :, :, 0, :],
                X0.rearrange("p t (k d) -> p t k d", k=DK), ACT.Copy).then_inc(s_xn_ready, 1)
            for t in range(NT):
                b, tt = t // 2, t % 2
                eng.wait_ge(s_pt0_ready, t + 1)
                if tt == 0 and b >= 2:
                    if pos(16 * (b // 2)):
                        eng.wait_ge(s_xT_out[b % 2], 16 * (b // 2))
                if t >= 2:
                    if pos(t - 1):
                        eng.wait_ge(s_lg_ready, t - 1)
                act(xT2[:, b % 2, :, :, tt * P:tt * P + P], PSH[t % 2][:, 0:512].rearrange("p (k h t) -> p k h t", k=DK, h=2),
                    ACT.Copy).then_inc(s_xTev, 1)
                if t % 4 == 3:
                    c = t // 4
                    eng.wait_ge(s_wo_scaled, c + 1)
                    act(woh[:, 4 * c:4 * c + 4, :], stage[:, c % 2, 0:1024].rearrange("p (a n) -> p a n", a=4), ACT.Copy).then_inc(s_wohi, 1)
            eng.wait_ge(s_achain, 2)
            act(sm[:, 2:3], sm[:, 0:1], ACT.Exp).then_inc(s_lam_ready, 1)
            act(sm[:, 3:4], sm[:, 1:2], ACT.Exp).then_inc(s_lam_ready, 1)
            eng.wait_ge(s_dd_ready, 1)
            act(ex, dd, ACT.Exp).then_inc(s_expw, 1)

            def project_hi(b, j, i):
                n = b * NH + j
                u, g, up = ahead(b, j)
                if not has_proj(n):
                    return
                if j % 2 == 1 and i == 1:
                    eng.wait_ge(s_v32_ready, u + 1)
                    if pos(n - 1):
                        eng.wait_ge(s_pv, n - 1)
                    act(vh[:, up, :, :].rearrange("p t n -> p (t n)"), v32, ACT.Copy).then_inc(s_vhi_ready, 1)
                    return
                eng.wait_ge(s_proj, n * 2 + (5 + i))
                if pos(n - j % 2):
                    eng.wait_ge(s_scores, n - j % 2)
                for m in range(2):
                    dst = qh[:, up, 2 * i + m, :] if j % 2 == 0 else kh[:, up, m, :]
                    col = (4 * g + 2 * i + m) if j % 2 == 0 else 16 + 2 * g + m
                    l = act(dst, bPJ[i][:, m * S:m * S + S], ACT.Identity, bias=qkb64[:, col:col + 1])
                l.then_inc(s_projhi, 1)

            def exponentials(b, j):
                n, par = b * NH + j, j % 2
                if not has(n, 0):
                    return
                eng.wait_ge(s_negm, n + 1)
                if pos(n - 1):
                    eng.wait_ge(s_pcomb, n - 1)
                for m in range(2):
                    for q in range(2):
                        c = slice(0, P) if q == 0 else slice(P, 3 * P)
                        l = act(ee[:, par, m, c], bS[:, m, c], ACT.Exp, bias=ngm[:, par, q, m:m + 1], scale=SCALE,
                                accum_out=rs[:, par, m, q:q + 1])
                l.then_inc(s_exped, 1)

            def o_hi(b, j):
                n, par = b * NH + j, j % 2
                if not has(n, 2):
                    return
                eng.wait_ge(s_oT, n - 1)
                if pos(n - 3):
                    eng.wait_ge(s_heads_out, n - 3)
                act(oth[:, par, :], bOT, ACT.Copy).then_inc(s_oThi, 1)

            def p_hi(b, j):
                n, par = b * NH + j, (j + 1) % 2
                if not has(n, 1):
                    return
                eng.wait_ge(s_pT, n)
                if pos(n - 2):
                    eng.wait_ge(s_pv, n - 2)
                act(pth[:, par, :], bPT[:, 0:384], ACT.Copy).then_inc(s_pThi, 1)

            def squares(b, j):
                n, par = b * NH + j, (j + 1) % 2
                if not has(n, 1):
                    return
                eng.wait_ge(s_pv, n)
                if pos(n - 1):
                    eng.wait_ge(s_sumsq, n - 1)
                if pos(n - 2):
                    eng.wait_ge(s_meansq, n - 2)
                for q in range(2):
                    l = act(junk[:, q, :], bPV[:, q * VD:q * VD + VD], ACT.Square, scale=co[:, 0:1],
                            accum_out=ss[:, par, q:q + 1])
                l.then_inc(s_sumsq, 1)

            def normalise(b, j, lag):
                n, par = b * NH + j, (j + lag) % 2
                if not has(n, lag):
                    return
                eng.wait_ge(s_ocoef, n - lag + 1)
                if pos(n - lag - 1):
                    eng.wait_ge(s_oT, n - lag - 1)
                for q in range(2):
                    l = act(on[:, par, q, :], bPV[:, q * VD:q * VD + VD], ACT.Copy, scale=rc[:, par, q:q + 1])
                l.then_inc(s_onorm, 1)

            def step(b, j):
                normalise(b, j, 2)
                p_hi(b, j)
                exponentials(b, j)
                o_hi(b, j)
                project_hi(b, j, 0)
                squares(b, j)
                project_hi(b, j, 1)

            prepared(eng)
            eng.wait_ge(s_lam_ready, 4)
            for j in (-2, -1):
                project_hi(0, j, 0)
                project_hi(0, j, 1)
            steps(eng, step)

            for e in range(NE):
                st = stage[:, e % 2, :].rearrange("p (b n) -> p b n", b=FB + 1)
                eng.wait_ge(s_wd_in[e % 2], 32 * (e // 2 + 1))
                act(WD[:, e, 0, 0:FB, :], st[:, 0:FB, :], ACT.Copy, scale=ES)
                act(WD[0:FR, e, 0, FB, :], st[0:FR, FB, :], ACT.Copy, scale=ES).then_inc(s_wdhi, 1)

            def tile(t, j):
                i, par = t * 4 + j, j % 2
                if not isinstance(i, int) or i < NS:
                    eng.wait_ge(s_gup, i + 1)
                    if pos(i - 1):
                        eng.wait_ge(s_hmul, i - 1)
                    act(sg[:, par, 0:512], PS[:, 3 * par, :], ACT.Silu, scale=1.0 / ES)
                    act(sg[:, par, 512:640], PS[:, 3 * par + 1, 0:P], ACT.Silu, scale=1.0 / ES)
                    act(sg[FR:P, par, 640:768], PS[0:FR, 3 * par + 1, P:2 * P], ACT.Silu, scale=1.0 / ES).then_inc(s_silu, 1)
                    eng.wait_ge(s_hmul, i + 1)
                    if pos(i - 1):
                        eng.wait_ge(s_yp, i - 1)
                    act(hh[:, par, 0:640], h32[:, par, 0:640], ACT.Copy)
                    act(hh[0:FR, par, 640:768], h32[0:FR, par, 640:768], ACT.Copy).then_inc(s_hhi, 1)
                if not isinstance(i, int) or i >= 1:
                    q = (j + 3) % 4
                    if pos(i):
                        eng.wait_ge(s_yp, i)
                    if pos((t + (j + 3) // 4 - 1) * 16):
                        eng.wait_ge(s_y_out[q], (t + (j + 3) // 4 - 1) * 16)
                    act(yy[:, q, :], PS[:, 6, 0:D], ACT.Copy, scale=xg[:, q, 257:258]).then_inc(s_yev, 1)

            tiles(eng, tile)
            for b in range(8):
                eng.wait_ge(s_fin_add, b + 1)
                act(FY[:, 1, 2 * b:2 * b + 2, :], FY[:, 0, 2 * b:2 * b + 2, :], ACT.Silu).then_inc(s_fin_silu, 1)

        @block.vector
        def _(eng):
            v = nc.vector
            def link(ins, chain):
                chain[1] += 1
                ins.then_inc(chain[0], 1)
                eng.wait_ge(chain[0], chain[1])

            norm = [s_xchain, 0]
            rows = [s_xrow_ready, 0]
            coefs = [s_achain, 0]
            wos = [s_wo_scaled, 0]
            routing = [s_route, 0]
            fsum = [s_fin_sum, 0]
            fmul = [s_fin_mul, 0]

            eng.wait_ge(s_x_in, 16)
            link(v.tensor_reduce(mean[:, :], X0, AX, ALU.add), norm)
            link(v.tensor_scalar(mean[:, :], mean[:, :], 1.0 / D, None, ALU.mult), norm)
            link(v.tensor_tensor(X0, X0, mean[:, :].unsqueeze(2).to_broadcast([P, NT, D]), ALU.subtract), norm)
            for t in range(NT):
                last = v.scalar_tensor_tensor(out=XROW[:, t, 1, 0:256], in0=X0[:, t, :], scalar=1.0, in1=X0[:, t, :], op0=ALU.mult, op1=ALU.mult,
                                              accum_out=rstd[:, t:t + 1])
            link(last, norm)
            link(v.tensor_scalar(rstd[:, :], rstd[:, :], 1.0 / D, EPS, ALU.mult, ALU.add), norm)

            def rsqrt(y, val, tmp, name):
                link(v.tensor_scalar(tmp.bitcast(I32), val.bitcast(I32), 1, None, ALU.logical_shift_right), name)
                link(v.tensor_scalar(y.bitcast(I32), tmp.bitcast(I32), -1.0, float(0x5F3759DF), ALU.mult, ALU.add), name)
                for _ in range(4):
                    link(v.tensor_tensor(tmp, y, val, ALU.mult), name)
                    link(v.scalar_tensor_tensor(out=tmp, in0=tmp, scalar=-0.5, in1=y, op0=ALU.mult, op1=ALU.mult), name)
                    link(v.scalar_tensor_tensor(out=y, in0=tmp, scalar=1.5, in1=y, op0=ALU.add, op1=ALU.mult), name)

            rsqrt(m2, rstd[:, :], m1, norm)
            v.tensor_tensor(X0, X0, m2.unsqueeze(2).to_broadcast([P, NT, D]), ALU.mult).then_inc(s_xn_ready, 1)
            eng.wait_ge(s_gw_ready, 1)
            v.scalar_tensor_tensor(out=gwl[:, :, :], in0=gw_s[:, :, :], scalar=WS, in1=gwh[:, :, :], op0=ALU.mult, op1=ALU.subtract).then_inc(s_gw_ready, 1)
            eng.wait_ge(s_xn_ready, 2)
            hi = XROWH[:, :, 0, 0:512].rearrange("p t (k h d) -> p t k h d", k=DK, h=2)
            for k in range(DK):
                last = v.tensor_tensor(hi[:, :, k, 1, :], X0[:, :, k * P:k * P + P], hi[:, :, k, 0, :], ALU.subtract)
            link(last, rows)
            v.tensor_copy(XROW[:, :, 1, 0:256], XROW[:, :, 0, 0:256]).then_inc(s_xrow_ready, 1)
            eng.wait_ge(s_wqhi, 1)
            v.scalar_tensor_tensor(out=wql, in0=WQ, scalar=WS, in1=wqh, op0=ALU.mult, op1=ALU.subtract).then_inc(s_wqlo, 1)
            eng.wait_ge(s_small_in, 16 * 7)
            for i in range(2):
                v.tensor_tensor_reduce(out=rt[:, 3900 - 128 * i:4028 - 128 * i], in0=lam_s[:, 2 * i, :], in1=lam_s[:, 2 * i + 1, :], scale=1.0, scalar=0.0,
                                       op0=ALU.mult, op1=ALU.add, accum_out=sm[:, i:i + 1]).then_inc(s_achain, 1)
            coefs[1] = 2
            link(v.tensor_scalar(sub_s[:, :], sub_s[:, :], (1.0 - LAMBDA_INIT) * WS, None, ALU.mult), coefs)
            for c in range(4):
                eng.wait_ge(s_wo_in[c % 2], 16 * (c // 2 + 1))
                st = stage[:, c % 2, 0:1024].rearrange("p (a e n) -> p a e n", a=2, e=2)
                for eb in range(2):
                    last = v.tensor_scalar(st[:, :, eb, :], st[:, :, eb, :], sub_s[:, eb:eb + 1], None, ALU.mult)
                link(last, wos)
                eng.wait_ge(s_wohi, c + 1)
                v.tensor_tensor(wol[:, 4 * c:4 * c + 4, :], stage[:, c % 2, 0:1024].rearrange("p (a n) -> p a n", a=4),
                                woh[:, 4 * c:4 * c + 4, :], ALU.subtract).then_inc(s_wolo, 1)
            eng.wait_ge(s_lg_ready, NT)
            r = lambda ins: link(ins, routing)
            eng.wait_ge(s_pads_ready, 1)
            r(v.tensor_scalar(L, PS[:, 6, 0:P].rearrange("p (t e) -> p t e", t=NT), 1.0 / WS, None, ALU.mult))

            def bc(a):
                return a.unsqueeze(2).to_broadcast([P, NT, NE])

            def be(a):
                return a.unsqueeze(1).to_broadcast([P, NT, NE])

            for src, mm, q, kk, kmx, oh in ((L, m1, eq, key, km, oh1), (L2, m2, eq2, key2, km2, oh2)):
                r(v.tensor_reduce(mm, src, AX, ALU.max))
                r(v.tensor_tensor(q, src, bc(mm), ALU.is_equal))
                r(v.tensor_tensor(kk, q, be(rev[:, :]), ALU.mult))
                r(v.tensor_reduce(kmx, kk, AX, ALU.max))
                r(v.tensor_tensor(oh, kk, bc(kmx), ALU.is_equal))
                if src is L:
                    r(v.scalar_tensor_tensor(out=L2, in0=oh1, scalar=-3e38, in1=L, op0=ALU.mult, op1=ALU.add))
            v.tensor_tensor(dd, m2, m1, ALU.subtract).then_inc(s_dd_ready, 1)
            v.tensor_tensor(M16.rearrange("p (t e) -> p t e", t=NT), oh1, oh2, ALU.add).then_inc(s_M_ready, 1)
            eng.wait_ge(s_pre_ready, 1)
            r(v.tensor_copy(pre, PS[:, 7, 0:P].rearrange("p (t e) -> p t e", t=NT)))
            r(v.tensor_copy(tot, PS[:, 7, P:2 * P].rearrange("p (t e) -> p t e", t=NT)))
            src = tot
            for n, sh in enumerate((1, 2, 4, 8)):
                d_ = scA[n]
                r(v.tensor_copy(d_[:, 0:sh, :], src[:, 0:sh, :]))
                r(v.tensor_tensor(d_[:, sh:NT, :], src[:, sh:NT, :], src[:, 0:NT - sh, :], ALU.add))
                src = d_
            incl = src
            r(v.tensor_scalar(cnti, incl[:, NT - 1, :], float(P - 1), None, ALU.add))
            r(v.tensor_scalar(cnts, cnti, 7, None, ALU.logical_shift_right))
            r(v.tensor_copy(tls, cnts))
            srce = tls
            for n, sh in enumerate((1, 2, 4)):
                d_ = scE[n]
                r(v.tensor_copy(d_[:, 0:sh], srce[:, 0:sh]))
                r(v.tensor_tensor(d_[:, sh:NE], srce[:, sh:NE], srce[:, 0:NE - sh], ALU.add))
                srce = d_
            ends = srce
            r(v.tensor_tensor(base, ends, tls, ALU.subtract))
            r(v.tensor_scalar(base, base, float(P), None, ALU.mult))
            r(v.tensor_tensor(slot, incl, tot, ALU.subtract))
            r(v.tensor_tensor(slot2, slot, pre, ALU.add))
            r(v.tensor_tensor(slot, slot2, be(base), ALU.add))
            r(v.tensor_tensor(ps1, oh1, slot, ALU.mult))
            r(v.tensor_tensor(ps2, oh2, slot, ALU.mult))
            r(v.tensor_reduce(slf[:, 0, :], ps1, AX, ALU.add))
            r(v.tensor_reduce(slf[:, 1, :], ps2, AX, ALU.add))
            v.tensor_copy(sli[:, :, :], slf).then_inc(s_slots_ready, 1)
            r(v.tensor_copy(tf[:, :], ti[:, :]))
            r(v.tensor_tensor(te, tf[:, :].unsqueeze(2).to_broadcast([P, NS, NE - 1]),
                              ends[:, 0:NE - 1].unsqueeze(1).to_broadcast([P, NS, NE - 1]), ALU.is_ge))
            r(v.tensor_reduce(tef, te, AX, ALU.add))
            v.tensor_copy(texp[:, :], tef).then_inc(s_texp_ready, 1)
            eng.wait_ge(s_expw, 1)
            r(v.tensor_scalar(ex1, ex, 1.0, None, ALU.add))
            r(v.reciprocal(w1, ex1))
            r(v.tensor_tensor(w2, ex, w1, ALU.mult))
            v.tensor_scalar(XROW[:, :, 0, 257], w1, 1.0 / (HS * ES), None, ALU.mult).then_inc(s_fields, 1)
            v.tensor_scalar(XROW[:, :, 1, 257], w2, 1.0 / (HS * ES), None, ALU.mult).then_inc(s_fields, 1)
            a = lambda ins: link(ins, coefs)
            eng.wait_ge(s_lam_ready, 3)
            a(v.tensor_tensor(sm[:, 4:5], sm[:, 2:3], sm[:, 3:4], ALU.subtract))
            a(v.tensor_scalar(sm[:, 5:6], sm[:, 4:5], LAMBDA_INIT, None, ALU.add))
            a(v.tensor_scalar(sm[:, 6:7].bitcast(I32), sm[:, 5:6].bitcast(I32), 0x7F800000, None, ALU.bitwise_and))
            a(v.tensor_scalar(sm[:, 7:8], sm[:, 6:7], 1.0, None, ALU.max))
            a(v.reciprocal(sm[:, 8:9], sm[:, 7:8]))
            a(v.scalar_tensor_tensor(out=sm[:, 9:10], in0=sm[:, 5:6], scalar=-1.0, in1=sm[:, 8:9], op0=ALU.mult, op1=ALU.mult))
            for q in range(2):
                a(v.tensor_copy(cf[:, 0, q:q + 1], sm[:, 8:9]))
                a(v.tensor_copy(cf[:, 1, q:q + 1], sm[:, 9:10]))
            v.tensor_scalar(co[:, :], sm[:, 7:8], 1.0 / WS, None, ALU.mult).then_inc(s_lam_ready, 1)
            a(v.tensor_scalar(vb_s[:, :, :], vb_s[:, :, :], WS, None, ALU.mult))
            v.memset(sm[:, 10:11], 0.0).then_inc(s_prep_done, 1)

            def project_lo(b, j, i):
                u, g, up = ahead(b, j)
                if not has_proj(b * NH + j):
                    return
                if j % 2 == 1 and i == 1:
                    eng.wait_ge(s_proj, u * 4 + 4)
                    if pos(u):
                        eng.wait_ge(s_vlo_ready, u)
                    v.tensor_tensor(v32.rearrange("p (t n) -> p t n", t=2), bPJ[1].rearrange("p (t n) -> p t n", t=2),
                                    vb_s[:, g, :].unsqueeze(1).to_broadcast([P, 2, VD]), ALU.add).then_inc(s_v32_ready, 1)
                    return
                eng.wait_ge(s_projhi, u * 3 + (i + 1 if j % 2 == 0 else 3))
                for m in range(2):
                    dst = ql[:, up, 2 * i + m, :] if j % 2 == 0 else kl[:, up, m, :]
                    hi_ = qh[:, up, 2 * i + m, :] if j % 2 == 0 else kh[:, up, m, :]
                    col = (4 * g + 2 * i + m) if j % 2 == 0 else 16 + 2 * g + m
                    last = v.scalar_tensor_tensor(out=dst, in0=bPJ[i][:, m * S:m * S + S], scalar=qkb64[:, col:col + 1],
                                                  in1=hi_, op0=ALU.add, op1=ALU.subtract)
                last.then_inc(s_projlo, 1)

            def maxima(b, j):
                n, par = b * NH + j, j % 2
                if not has(n, 0):
                    return
                eng.wait_ge(s_scores, n + 1)
                if pos(n - 1):
                    eng.wait_ge(s_exped, n - 1)
                for q in range(2):
                    c = slice(0, P) if q == 0 else slice(P, 3 * P)
                    last = v.tensor_reduce(mx[:, par, q, :], bS[:, :, c], AX, ALU.max)
                last.then_inc(s_maxed, 1)
                eng.wait_ge(s_maxed, n + 1)
                v.tensor_scalar(ngm[:, par, :, :], mx[:, par, :, :], -SCALE, None, ALU.mult).then_inc(s_negm, 1)

            def o_lo(b, j):
                n, par = b * NH + j, j % 2
                if not has(n, 2):
                    return
                eng.wait_ge(s_oThi, n - 1)
                if pos(n - 3):
                    eng.wait_ge(s_heads_out, n - 3)
                v.tensor_tensor(otl[:, par, :], bOT, oth[:, par, :], ALU.subtract).then_inc(s_oTlo, 1)

            def p_lo(b, j):
                n, par = b * NH + j, (j + 1) % 2
                if not has(n, 1):
                    return
                eng.wait_ge(s_pThi, n)
                if pos(n - 2):
                    eng.wait_ge(s_pv, n - 2)
                v.tensor_tensor(ptl[:, par, :], bPT[:, 0:384], pth[:, par, :], ALU.subtract).then_inc(s_pTlo, 1)

            def combine(b, j):
                n, par = b * NH + j, j % 2
                if not has(n, 0):
                    return
                eng.wait_ge(s_exped, n + 1)
                if pos(n - 1):
                    eng.wait_ge(s_coef, n - 1)
                v.reciprocal(ri[:, par, :, :], rs[:, par, :, :]).then_inc(s_rsum_inv, 1)
                eng.wait_ge(s_rsum_inv, n + 1)
                if pos(n - 1):
                    eng.wait_ge(s_pcomb, n - 1)
                v.tensor_tensor(al[:, par, :, :], ri[:, par, :, :], cf[:, :, :], ALU.mult).then_inc(s_coef, 1)
                eng.wait_ge(s_coef, n + 1)
                for q in range(2):
                    c = slice(0, P) if q == 0 else slice(P, 3 * P)
                    last = v.tensor_scalar(ee[:, par, 0, c], ee[:, par, 0, c], al[:, par, 0, q:q + 1], None, ALU.mult)
                last.then_inc(s_pscaled, 1)
                eng.wait_ge(s_pscaled, n + 1)
                if pos(n - 1):
                    eng.wait_ge(s_pT, n - 1)
                for q in range(2):
                    c = slice(0, P) if q == 0 else slice(P, 3 * P)
                    last = v.scalar_tensor_tensor(out=pc[:, par, c], in0=ee[:, par, 1, c], scalar=al[:, par, 1, q:q + 1],
                                                  in1=ee[:, par, 0, c], op0=ALU.mult, op1=ALU.add)
                last.then_inc(s_pcomb, 1)

            def mean_square(b, j, lag):
                n, par = b * NH + j, (j + lag) % 2
                if not has(n, lag):
                    return
                eng.wait_ge(s_sumsq, n - lag + 1)
                if pos(n - lag - 1):
                    eng.wait_ge(s_rms, n - lag - 1)
                v.tensor_scalar(ms[:, par, :], ss[:, par, :], 1.0 / VD, EPS, ALU.mult, ALU.add).then_inc(s_meansq, 1)

            def out_coef(b, j, lag):
                n, par = b * NH + j, (j + lag) % 2
                if not has(n, lag):
                    return
                eng.wait_ge(s_rms, n - lag + 1)
                if pos(n - lag - 1):
                    eng.wait_ge(s_onorm, n - lag - 1)
                v.tensor_scalar(rc[:, par, :], rm[:, par, :], co[:, 0:1], None, ALU.mult).then_inc(s_ocoef, 1)

            def rows_out(b, j):
                if j % NH != 1 or (isinstance(b, int) and b * NH + j < NH):
                    return
                bb = b + j // NH
                eng.wait_ge(s_heads_out, bb * NH)
                if pos((bb - 1) * 16):
                    eng.wait_ge(s_s_out, (bb - 1) * 16)
                v.scalar_tensor_tensor(out=so.rearrange("p (q d) -> p q d", q=2), in0=bOUT.rearrange("p (q d) -> p q d", q=2),
                                       scalar=1.0 / WS, in1=ob_s[:, :].unsqueeze(1).to_broadcast([P, 2, D]),
                                       op0=ALU.mult, op1=ALU.add).then_inc(s_so_ready, 1)

            def step(b, j):
                out_coef(b, j, 2)
                maxima(b, j)
                p_lo(b, j)
                o_lo(b, j)
                combine(b, j)
                project_lo(b, j, 0)
                mean_square(b, j, 1)
                project_lo(b, j, 1)
                rows_out(b, j)

            prepared(eng)
            for j in (-2, -1):
                project_lo(0, j, 0)
                project_lo(0, j, 1)
            steps(eng, step)

            for e in range(NE):
                st = stage[:, e % 2, :].rearrange("p (b n) -> p b n", b=FB + 1)
                eng.wait_ge(s_wdhi, e + 1)
                v.scalar_tensor_tensor(out=WD[:, e, 1, 0:FB, :], in0=st[:, 0:FB, :], scalar=ES, in1=WD[:, e, 0, 0:FB, :], op0=ALU.mult, op1=ALU.subtract)
                v.scalar_tensor_tensor(out=WD[0:FR, e, 1, FB, :], in0=st[0:FR, FB, :], scalar=ES, in1=WD[0:FR, e, 0, FB, :], op0=ALU.mult, op1=ALU.subtract).then_inc(s_wdlo, 1)

            def xev(i, j):
                eng.wait_ge(s_xgTp, i + 1)
                if pos(i - 1):
                    eng.wait_ge(s_gup, i - 1)
                v.tensor_copy(xgT[:, j % 2, :], PSH[7][:, 0:512]).then_inc(s_xgT_ready, 1)

            xev(0, 0)

            def tile(t, j):
                i, par = t * 4 + j, j % 2
                if isinstance(i, int) and i >= NS:
                    return
                if not isinstance(i, int) or i + 1 < NS:
                    xev(i + 1, j + 1)
                eng.wait_ge(s_silu, i + 1)
                if pos(i - 1):
                    eng.wait_ge(s_hhi, i - 1)
                if pos(i - 1):
                    eng.wait_ge(s_hlo, i - 1)
                f = HS / ES
                v.scalar_tensor_tensor(out=h32[:, par, 0:512], in0=PS[:, 3 * par + 2, :], scalar=f, in1=sg[:, par, 0:512], op0=ALU.mult, op1=ALU.mult)
                v.scalar_tensor_tensor(out=h32[:, par, 512:640], in0=PS[:, 3 * par + 1, 2 * P:3 * P], scalar=f, in1=sg[:, par, 512:640], op0=ALU.mult, op1=ALU.mult)
                v.scalar_tensor_tensor(out=h32[0:FR, par, 640:768], in0=PS[FR:P, 3 * par + 1, P:2 * P], scalar=f, in1=sg[FR:P, par, 640:768],
                                       op0=ALU.mult, op1=ALU.mult).then_inc(s_hmul, 1)
                eng.wait_ge(s_hhi, i + 1)
                if pos(i - 1):
                    eng.wait_ge(s_yp, i - 1)
                v.tensor_tensor(hl[:, par, 0:640], h32[:, par, 0:640], hh[:, par, 0:640], ALU.subtract)
                v.tensor_tensor(hl[0:FR, par, 640:768], h32[0:FR, par, 640:768], hh[0:FR, par, 640:768], ALU.subtract).then_inc(s_hlo, 1)

            tiles(eng, tile)
            eng.wait_ge(s_fin_in, 64)
            bias = fb_s[:, :].unsqueeze(1).to_broadcast([P, 2, D])
            for b in range(8):
                t = slice(2 * b, 2 * b + 2)
                link(v.tensor_tensor(FY[:, 0, t, :], FY[:, 0, t, :], FY[:, 1, t, :], ALU.add), fsum)
                v.tensor_tensor(FY[:, 0, t, :], FY[:, 0, t, :], bias, ALU.add).then_inc(s_fin_add, 1)
            for b in range(8):
                t = slice(2 * b, 2 * b + 2)
                eng.wait_ge(s_fin_silu, b + 1)
                link(v.tensor_tensor(FSA[:, t, :], FSA[:, t, :], FY[:, 1, t, :], ALU.mult), fmul)
                v.tensor_tensor(FX[:, t, :], FX[:, t, :], FSA[:, t, :], ALU.add).then_inc(s_fin_done, 1)


def kernel(**inputs):
    import numpy as np
    import concourse.bacc as bacc
    from concourse.bass_utils import run_bass_kernel_spmd

    g = {k[3:]: np.asarray(a) for k, a in inputs.items()}
    c = np.ascontiguousarray
    wg = g["ffn_w_in_gate"].transpose(0, 2, 1).reshape(NE, DK, P, FF).transpose(0, 2, 1, 3)
    wu = g["ffn_w_in_up"].transpose(0, 2, 1).reshape(NE, DK, P, FF).transpose(0, 2, 1, 3)
    wgu = np.concatenate([wg[..., 0:640], wg[..., 640:704], wu[..., 640:704], wu[..., 512:640], wu[..., 0:512]], axis=-1)
    arrays = {
        "x": c(g["attn_hidden_states"].reshape(T, D)),
        "wqkv": c(g["attn_Wqkv_w"].T.reshape(DK, P, 4096).transpose(1, 0, 2)),
        "qkb": c(g["attn_Wqkv_b"][:3072].reshape(24, P).T),
        "vb": c(g["attn_Wqkv_b"][3072:]),
        "lam_in": np.concatenate([g["attn_lambda_q1"], g["attn_lambda_k1"], g["attn_lambda_q2"], g["attn_lambda_k2"]]),
        "sub": c(g["attn_subln_w"].reshape(2, P).T),
        "wo": c(g["attn_out_w"].T.reshape(16, P, D).transpose(1, 0, 2).reshape(P, 16 * D)),
        "outb": c(g["attn_out_b"]),
        "gw": c(g["ffn_gate_w"].T.reshape(DK, P, NE).transpose(1, 0, 2)),
        "wgu": c(wgu),
        "wd": c(g["ffn_w_out"].transpose(0, 2, 1)),
        "fbias": c(g["ffn_bias"]),
    }
    nc = bacc.Bacc("TRN2", target_bir_lowering=False, num_devices=1)
    aps = {k: nc.dram_tensor(f"in_{k}", a.shape, mybir.dt.from_np(a.dtype), kind="ExternalInput").ap() for k, a in arrays.items()}
    out = nc.dram_tensor("out_0", (T, D), F32, kind="ExternalOutput").ap()
    build(nc, out=out, **aps)
    r = run_bass_kernel_spmd(nc, [{f"in_{k}": a for k, a in arrays.items()}], core_ids=[0])
    return r.results[0]["out_0"].reshape(B, S, D)
```

```python
import math
from contextlib import ExitStack

import concourse.bass as bass
from concourse import mybir

F32 = mybir.dt.float32
F16 = mybir.dt.float16
I32 = mybir.dt.int32
U32 = mybir.dt.uint32
ALU = mybir.AluOpType
ACT = mybir.ActivationFunctionType
AX = mybir.AxisListType.X
ds = bass.ds

P = 128
B, S, D = 8, 256, 256
T = B * S
NT = T // P
DK = D // P
NH = 8
HD = 128
VD = 256
NG = 4
NU = B * NG
NN = B * NH
NE = 8
FF = 704
FB = -(-FF // P)
H0 = [min(c * P, FF - P) for c in range(FB)]
GUW = 2 * FF
EB = 3
NS = 2 * T // P + NE - 1
NQ = NS // 4 + 1
SLOTS = NS * P
NPAD = (SLOTS - 2 * T) // P
XG = 4
XT = NT // XG
WGC = 4096 // NG
ROW = 516
LAMBDA_INIT = 0.8 - 0.6 * math.exp(-0.3)
EPS = 1e-5
WS = 64.0
ES = 32.0
HS = 16.0
SCALE = HD ** -0.5 / (WS * WS)
MASK = 65504.0


def build(nc, x, wqkv, qkb, vb, lam_in, sub, wo, outb, gw, wgu, wd, fbias, out):
    xrow_dram = nc.dram_tensor("xrow_dram", (SLOTS, ROW // 2), F32, kind="Internal").ap()
    y_dram = nc.dram_tensor("y_dram", (2 * T + NPAD * P, D), F32, kind="Internal").ap()
    xT_dram = nc.dram_tensor("xT_dram", (B * P, 4 * S), F16, kind="Internal").ap()
    s_dram = nc.dram_tensor("s_dram", (T, D), F32, kind="Internal").ap()

    with ExitStack() as ctx:
        def sb(name, shape, dt):
            return ctx.enter_context(nc.sbuf_tensor(name, shape, dt))

        def sem(name):
            return ctx.enter_context(nc.semaphore(name))

        GU = sb("GU", [P, NE, DK, 2, GUW], F16)
        gu32 = GU[:, :, :, :, :].rearrange("p e k h n -> p (e k h n)").bitcast(F32)
        EXP32 = DK * GUW
        WQ = gu32[:, 0:8192].rearrange("p (k n) -> p k n", k=DK)
        X0 = gu32[:, 3 * EXP32:3 * EXP32 + NT * D].rearrange("p (t d) -> p t d", t=NT)
        XR0 = 3 * EXP32 + NT * D
        XROW = gu32[:, XR0:XR0 + NT * 2 * ROW // 2].rearrange("p (t k w) -> p t k w", t=NT, k=2)
        XROWH = XROW.bitcast(F16)
        WO3 = gu32[:, XR0 + NT * ROW:XR0 + NT * ROW + 1024]
        PADR = gu32[:, 5632:5632 + NPAD * ROW // 2].rearrange("p (k w) -> p k w", k=NPAD)
        FX = gu32[:, 0:4096].rearrange("p (t d) -> p t d", t=NT)
        FSA = gu32[:, 4096:8192].rearrange("p (t d) -> p t d", t=NT)
        FY = gu32[:, 8192:16384].rearrange("p (k t d) -> p k t d", k=2, t=NT)
        W2 = sb("W2", [P, 24576], F16)
        wqh = W2[:, 0:8192].rearrange("p (k n) -> p k n", k=DK)
        wql = W2[:, 8192:16384].rearrange("p (k n) -> p k n", k=DK)
        woh = W2[:, 16384:20480].rearrange("p (t n) -> p t n", t=16)
        wol = W2[:, 20480:24576].rearrange("p (t n) -> p t n", t=16)
        WD = W2[:, :].rearrange("p (e h b n) -> p e h b n", e=NE, h=2, b=FB)
        stage = sb("stage", [P, 2, 1536], F32)
        stg = stage[:, :, :].rearrange("p a n -> p (a n)")
        WOC = [stg[:, 0:1024], stg[:, 1024:2048], stg[:, 2048:3072], WO3]
        WK = sb("WK", [P, 11264], F32)
        at = [0]

        def view(words, dt=F32):
            v = WK[:, at[0]:at[0] + words]
            at[0] += words
            assert at[0] <= 11264
            return v if dt == F32 else v.bitcast(dt)

        xT2 = WK[:, 11264 - 7 * 512:11264].bitcast(F16).rearrange("p (b k h t) -> p b k h t", b=B - 1, k=DK, h=2)
        rt = X0.rearrange("p t d -> p (t d)")
        at[0] = 0
        xT = view(512, F16).rearrange("p (k h t) -> p k h t", k=DK, h=2)
        qh = view(1024, F16).rearrange("p (u m t) -> p u m t", u=2, m=4)
        ql = view(1024, F16).rearrange("p (u m t) -> p u m t", u=2, m=4)
        kh = view(512, F16).rearrange("p (u m t) -> p u m t", u=2, m=2)
        kl = view(512, F16).rearrange("p (u m t) -> p u m t", u=2, m=2)
        vh = view(512, F16).rearrange("p (u t n) -> p u t n", u=2, t=2)
        vl = view(512, F16).rearrange("p (u t n) -> p u t n", u=2, t=2)
        v32 = view(512)
        ee = view(2 * 2 * 384).rearrange("p (b m n) -> p b m n", b=2, m=2)
        pc = view(2 * 384).rearrange("p (b n) -> p b n", b=2)
        pth = view(384, F16).rearrange("p (b n) -> p b n", b=2)
        ptl = view(384, F16).rearrange("p (b n) -> p b n", b=2)
        on = view(1024).rearrange("p (b q n) -> p b q n", b=2, q=2)
        oth = view(512, F16).rearrange("p (b n) -> p b n", b=2)
        otl = view(512, F16).rearrange("p (b n) -> p b n", b=2)
        junk = view(512).rearrange("p (q n) -> p q n", q=2)
        so = view(512)
        at[0] = 0
        xg = view(4 * ROW // 2).rearrange("p (b w) -> p b w", b=4)
        xgh = xg.bitcast(F16)
        xgT = view(512, F16).rearrange("p (b n) -> p b n", b=2)
        sg = view(2 * 768).rearrange("p (b n) -> p b n", b=2)
        h32 = view(2 * 768).rearrange("p (b n) -> p b n", b=2)
        hh = view(768, F16).rearrange("p (b n) -> p b n", b=2)
        hl = view(768, F16).rearrange("p (b n) -> p b n", b=2)
        yy = view(1024).rearrange("p (b n) -> p b n", b=4)

        ident16 = sb("ident16", [P, P], F16)
        ident32 = sb("ident32", [P, P], F32)
        maskl = sb("maskl", [P, P], F16)
        maskr = sb("maskr", [P, P], F16)
        sut = sb("sut", [P, P], F16)
        ones16 = sb("ones16", [P, P], F16)
        es_c = sb("es_c", [P, 1], F32)
        half_c = sb("half_c", [P, NT // 2], F32)
        ki = sb("ki", [P, NPAD], I32)
        kf = sb("kf", [P, NPAD], F32)
        sp = sb("sp", [P, NPAD], I32)
        rev = sb("rev", [P, NE], F32)
        revi = sb("revi", [P, NE], I32)
        ti = sb("ti", [P, NS], I32)
        tf = sb("tf", [P, NS], F32)
        qkb_s = sb("qkb_s", [P, 24], F32)
        qkb64 = sb("qkb64", [P, 24], F32)
        vb_s = sb("vb_s", [P, NG, VD], F32)
        ob_s = sb("ob_s", [P, D], F32)
        fb_s = sb("fb_s", [P, D], F32)
        lam_s = sb("lam_s", [P, 4, HD], F32)
        sub_s = sb("sub_s", [P, 2], F32)
        gw_s = sb("gw_s", [P, DK, NE], F32)
        gwh = sb("gwh", [P, DK, NE], F16)
        gwl = sb("gwl", [P, DK, NE], F16)
        sm = sb("sm", [P, 64], F32)
        lc = sb("lc", [P, 2, 2], F32)
        bn = sb("bn", [P, NT, 6], F32)
        mv = sb("mv", [P, NT, 2], F32)
        ve = sb("ve", [P, NT], F32)
        rstd = sb("rstd", [P, NT], F32)
        mx = sb("mx", [P, 2, 2, 2], F32)
        ngm = sb("ngm", [P, 2, 2, 2], F32)
        rs = sb("rs", [P, 2, 2, 2], F32)
        ri = sb("ri", [P, 2, 2, 2], F32)
        al = sb("al", [P, 2, 2, 2], F32)
        ss = sb("ss", [P, 2, 2], F32)
        ms = sb("ms", [P, 2, 2], F32)
        rm = sb("rm", [P, 2, 2], F32)
        rc = sb("rc", [P, 2, 2], F32)

        ra = [0]

        def rview(*shape):
            n = int(math.prod(shape))
            v = rt[:, ra[0]:ra[0] + n]
            ra[0] += n
            if len(shape) == 2:
                v = v.rearrange("p (a b) -> p a b", a=shape[0])
            return v

        L = rview(NT, NE)
        L2 = rview(NT, NE)
        m1 = rview(NT)
        m2 = rview(NT)
        km = rview(NT)
        km2 = rview(NT)
        eq = rview(NT, NE)
        eq2 = rview(NT, NE)
        key = rview(NT, NE)
        key2 = rview(NT, NE)
        oh1 = rview(NT, NE)
        oh2 = rview(NT, NE)
        M16 = rview(64).bitcast(F16)
        cnt = rview(NE)
        cnti = rview(NE).bitcast(I32)
        cnts = rview(NE).bitcast(I32)
        tc = rview(2, NE)
        scE = [rview(2, NE) for _ in range(3)]
        tcx = rview(2, NE)
        base = rview(NE)
        free = rview(NE)
        pg = rview(NPAD, NE)
        pg2 = rview(NPAD, NE)
        pr = rview(NPAD)
        prs = rview(NPAD)
        slot = rview(NT, NE)
        ps1 = rview(NT, NE)
        ps2 = rview(NT, NE)
        slf = rview(2, NT)
        dd = rview(NT)
        ex = rview(NT)
        ex1 = rview(NT)
        w1 = rview(NT)
        w2 = rview(NT)
        te = rview(NS, NE - 1)
        tef = rview(NQ + 1, 4)
        tefs = tef.rearrange("p a b -> p (a b)")
        tep = [rview(NQ) for _ in range(4)]
        texp = sb("texp", [P, NQ], I32)
        sli = sb("sli", [P, 2, NT], I32)

        PS = ctx.enter_context(nc.psum_tensor("PS", [P, 8, 512], F32))
        PSH = [PS[:, i, :].bitcast(F16) for i in range(8)]
        bPJ = [PS[:, 0, :], PS[:, 1, :]]
        bS = PS[:, 2:4, :]
        GUP = PS[:, 0:6, :].rearrange("p (a b) n -> p a (b n)", a=2)
        bPT, bPV, bOT, bOUT = (PS[:, i, :] for i in (4, 5, 6, 7))

        s_x_in = [sem(f"s_x_in{i}") for i in range(XG)]
        s_wq_in = [sem(f"s_wq_in{i}") for i in range(NG)]
        s_small_in = sem("s_small_in")
        s_bias_in = sem("s_bias_in")
        s_wo_in = [sem(f"s_wo_in{i}") for i in range(4)]
        s_consts = sem("s_consts")
        s_stats = sem("s_stats")
        s_moments = sem("s_moments")
        s_var_ready = sem("s_var_ready")
        s_rstd_ready = sem("s_rstd_ready")
        s_xhi_ready = sem("s_xhi_ready")
        s_xn_ready = sem("s_xn_ready")
        s_xrow_ready = sem("s_xrow_ready")
        s_pt0_ready = sem("s_pt0_ready")
        s_xTev = sem("s_xTev")
        s_xT_out = sem("s_xT_out")
        s_gw_ready = sem("s_gw_ready")
        s_lg_ready = sem("s_lg_ready")
        s_route = sem("s_route")
        s_dd_ready = sem("s_dd_ready")
        s_M_ready = sem("s_M_ready")
        s_pre_ready = sem("s_pre_ready")
        s_slots_ready = sem("s_slots_ready")
        s_texp_ready = sem("s_texp_ready")
        s_fields = sem("s_fields")
        s_kf_ready = sem("s_kf_ready")
        s_pad_zero = sem("s_pad_zero")
        s_pad_rows = sem("s_pad_rows")
        s_pad_slots = sem("s_pad_slots")
        s_copied = sem("s_copied")
        s_sub_ready = sem("s_sub_ready")
        s_scat_out = sem("s_scat_out")
        s_wqhi = sem("s_wqhi")
        s_wqlo = sem("s_wqlo")
        s_wo_scaled = sem("s_wo_scaled")
        s_wohi = sem("s_wohi")
        s_wolo = sem("s_wolo")
        s_achain = sem("s_achain")
        s_lam_ready = sem("s_lam_ready")
        s_expw = sem("s_expw")
        s_xT_in = sem("s_xT_in")
        s_proj = sem("s_proj")
        s_projhi = sem("s_projhi")
        s_projlo = sem("s_projlo")
        s_v32_ready = sem("s_v32_ready")
        s_vhi_ready = sem("s_vhi_ready")
        s_vlo_ready = sem("s_vlo_ready")
        s_scores = sem("s_scores")
        s_maxed = sem("s_maxed")
        s_negm = sem("s_negm")
        s_exped = sem("s_exped")
        s_rsum_inv = sem("s_rsum_inv")
        s_coef = sem("s_coef")
        s_oscale = sem("s_oscale")
        s_pcomb = sem("s_pcomb")
        s_pT = sem("s_pT")
        s_pThi = sem("s_pThi")
        s_pTlo = sem("s_pTlo")
        s_pv = sem("s_pv")
        s_sumsq = sem("s_sumsq")
        s_meansq = sem("s_meansq")
        s_rms = sem("s_rms")
        s_ocoef = sem("s_ocoef")
        s_onorm = sem("s_onorm")
        s_oT = sem("s_oT")
        s_oThi = sem("s_oThi")
        s_oTlo = sem("s_oTlo")
        s_heads_out = sem("s_heads_out")
        s_so_ready = sem("s_so_ready")
        s_s_out = sem("s_s_out")
        s_gu_in = [sem(f"s_gu_in{i}") for i in range(2)]
        s_gu_mul = sem("s_gu_mul")
        s_gu_split = sem("s_gu_split")
        s_wd_in = [sem(f"s_wd_in{i}") for i in range(2)]
        s_wdhi = sem("s_wdhi")
        s_wdlo = sem("s_wdlo")
        s_xg_in = [sem(f"s_xg_in{i}") for i in range(4)]
        s_xgTp = sem("s_xgTp")
        s_xgT_ready = sem("s_xgT_ready")
        s_gup = sem("s_gup")
        s_silu = sem("s_silu")
        s_hmul = sem("s_hmul")
        s_hTp = sem("s_hTp")
        s_hhi = sem("s_hhi")
        s_hlo = sem("s_hlo")
        s_yp = sem("s_yp")
        s_yev = sem("s_yev")
        s_y_out = [sem(f"s_y_out{i}") for i in range(4)]
        s_scatter_turn = sem("s_scatter_turn")
        s_fin_in = sem("s_fin_in")
        s_fin_sum = sem("s_fin_sum")
        s_fin_add = sem("s_fin_add")
        s_fin_mul = sem("s_fin_mul")
        s_fin_silu = sem("s_fin_silu")
        s_fin_done = sem("s_fin_done")
        s_fin_out = sem("s_fin_out")

        def pos(value):
            return not isinstance(value, int) or value > 0

        block = ctx.enter_context(nc.Block())

        def steps(eng, step):
            for j in range(NH):
                step(0, j)
            with eng.Fori(1, B - 1) as b:
                for j in range(NH):
                    step(b, j)
            for j in range(NH + 2):
                step(B - 1, j)

        def has(n, lag):
            return not isinstance(n, int) or 0 <= n - lag < NN

        def has_proj(n):
            return not isinstance(n, int) or n < NN - 2

        def ahead(b, j):
            u = b * NG + (j + 2) // 2
            return u, (j + 2) // 2 % NG, (j + 2) // 2 % 2

        def tiles(eng, step):
            for j in range(4):
                step(0, j)
            with eng.Fori(1, NS // 4) as t:
                for j in range(4):
                    step(t, j)
            for j in range(NS % 4 + 1):
                step(NS // 4, j)

        @block.sync
        def _(eng):
            for c in range(XG):
                rows = slice(c * XT * P, (c + 1) * XT * P)
                eng.dma_start(X0[:, c * XT:(c + 1) * XT, :], x[rows, :].rearrange("(t p) d -> p t d", p=P)).then_inc(s_x_in[c], 16)
            for g in range(NG):
                cols = slice(g * WGC, (g + 1) * WGC)
                eng.dma_start(WQ[:, :, cols], wqkv[:, :, cols]).then_inc(s_wq_in[g], 16)
            for c in range(4):
                eng.dma_start(WOC[c], wo[:, 1024 * c:1024 * c + 1024]).then_inc(s_wo_in[c], 16)
            for b in range(1, B):
                eng.wait_ge(s_xTev, 2 * b + 2)
                eng.dma_start(xT_dram[b * P:b * P + P, :],
                              xT2[:, b - 1, :, :, :].rearrange("p k h t -> p (k h t)")).then_inc(s_xT_out, 16)

            def load_xT(b):
                eng.dma_start(xT.rearrange("p k h t -> p (k h t)"), xT_dram[ds(b * P, P), :]).then_inc(s_xT_in, 16)

            def load_gu(e, k):
                if pos(e * 8 + k * 4 - 4):
                    eng.wait_ge(s_gu_split, e * 8 + k * 4 - 4)
                src = wgu[ds(e, 1), :, k, :].rearrange("a p n -> (a p) n")
                eng.dma_start(stage[:, k, 0:GUW], src).then_inc(s_gu_in[k], 16)

            def store_s(b):
                eng.wait_ge(s_so_ready, b + 1)
                eng.dma_start(s_dram[ds(b * S, S), :].rearrange("(q p) d -> p q d", p=P),
                              so.rearrange("p (q d) -> p q d", q=2)).then_inc(s_s_out, 16)

            eng.wait_ge(s_wohi, 4)
            eng.wait_ge(s_wolo, 4)
            load_gu(0, 0)
            load_gu(0, 1)
            load_gu(1, 0)
            eng.wait_ge(s_xT_out, 16 * (B - 1))
            with eng.Fori(1, B - 1) as b:
                if pos(b * 16):
                    eng.wait_ge(s_proj, b * 16)
                load_xT(b)
                load_gu(b, 1)
                store_s(b - 1)
                load_gu(b + 1, 0)
            eng.wait_ge(s_proj, (B - 1) * 16)
            load_xT(B - 1)
            load_gu(B - 1, 1)
            store_s(B - 2)
            store_s(B - 1)
            eng.wait_ge(s_s_out, 16 * B)
            eng.wait_ge(s_gu_split, 8 * NE)
            for e in range(NE):
                if e >= 2:
                    if pos(e - 1):
                        eng.wait_ge(s_wdhi, e - 1)
                    if pos(e - 1):
                        eng.wait_ge(s_wdlo, e - 1)
                st = stage[:, e % 2, :].rearrange("p (b n) -> p b n", b=FB)
                eng.dma_start(st, wd[e]).then_inc(s_wd_in[e % 2], 16)

            def load(t, j):
                if isinstance(t, int) and 4 * t + j >= NS:
                    return
                if pos(t * 16):
                    eng.wait_ge(s_y_out[j], t * 16)
                eng.dma_start(xg[:, j, :], xrow_dram[ds(t * (4 * P) + j * P, P), :]).then_inc(s_xg_in[j], 16)

            eng.wait_ge(s_scat_out, 16 * (2 * NT + NPAD))
            tiles(eng, load)
            for j in range(4):
                eng.wait_ge(s_y_out[j], 16 * ((NS + 3 - j) // 4))
            eng.dma_start(FX, x.rearrange("(t p) d -> p t d", p=P)).then_inc(s_fin_in, 16)
            eng.dma_start(FSA, s_dram.rearrange("(t p) d -> p t d", p=P)).then_inc(s_fin_in, 16)
            for k in range(2):
                eng.dma_start(FY[:, k, :, :], y_dram[k * T:k * T + T, :].rearrange("(t p) d -> p t d", p=P)).then_inc(s_fin_in, 16)
            for q in range(4):
                eng.wait_ge(s_fin_done, 2 * q + 2)
                eng.dma_start(out[q * 512:q * 512 + 512, :].rearrange("(t p) d -> p t d", p=P), FX[:, 4 * q:4 * q + 4, :]).then_inc(s_fin_out, 16)
            eng.wait_ge(s_fin_out, 64)

        @block.gpsimd
        def _(eng):
            eng.memset(ident16[:, :], 0.0).then_inc(s_consts, 1)
            eng.memset(ident32[:, :], 0.0).then_inc(s_consts, 1)
            eng.memset(maskl[:, :], 0.0).then_inc(s_consts, 1)
            eng.memset(maskr[:, :], 0.0).then_inc(s_consts, 1)
            eng.memset(sut[:, :], 1.0).then_inc(s_consts, 1)
            eng.wait_ge(s_consts, 5)
            for m, v in ((ident16, 1.0), (ident32, 1.0), (maskl, MASK)):
                eng.affine_select(out=m[:, :], in_=m[:, :], compare_op=ALU.not_equal, fill=v, base=0,
                                  pattern=[[-1, P]], channel_multiplier=1).then_inc(s_consts, 1)
            eng.affine_select(out=maskr[:, :], in_=maskr[:, :], compare_op=ALU.is_ge, fill=-MASK, base=0,
                              pattern=[[-1, P]], channel_multiplier=1).then_inc(s_consts, 1)
            eng.affine_select(out=sut[:, :], in_=sut[:, :], compare_op=ALU.is_ge, fill=0.0, base=-1,
                              pattern=[[1, P]], channel_multiplier=-1).then_inc(s_consts, 1)
            eng.memset(ones16[:, :], 1.0).then_inc(s_consts, 1)
            eng.memset(es_c[:, :], ES).then_inc(s_consts, 1)
            eng.memset(half_c[:, :], -0.5).then_inc(s_consts, 1)
            eng.iota(ki[:, :], pattern=[[P, NPAD]], base=0, channel_multiplier=1).then_inc(s_consts, 1)
            eng.iota(revi[:, :], pattern=[[-1, NE]], base=NE, channel_multiplier=0).then_inc(s_consts, 1)
            eng.iota(ti[:, :], pattern=[[1, NS]], base=0, channel_multiplier=0).then_inc(s_consts, 1)
            eng.wait_ge(s_consts, 16)
            eng.tensor_copy(rev[:, :], revi[:, :]).then_inc(s_kf_ready, 1)
            eng.tensor_copy(kf[:, :], ki[:, :]).then_inc(s_kf_ready, 1)
            for h in range(2):
                c = slice(h * NT // 2, (h + 1) * NT // 2)
                eng.wait_ge(s_var_ready, h + 1)
                eng.tensor_tensor(rstd[:, c], ve[:, c], half_c[:, :], ALU.pow).then_inc(s_rstd_ready, 1)
            eng.iota(XROW[:, :, :, 256].bitcast(I32), pattern=[[P, NT], [T, 2]], base=0, channel_multiplier=1).then_inc(s_fields, 1)
            eng.wait_ge(s_sub_ready, 1)
            for c in range(4):
                w4 = WOC[c].rearrange("p (a e n) -> p a e n", a=2, e=2)
                eng.wait_ge(s_wo_in[c], 16)
                for eb in range(2):
                    last = eng.tensor_tensor(w4[:, :, eb, :], w4[:, :, eb, :], sub_s[:, eb:eb + 1].unsqueeze(2).to_broadcast([P, 2, D]), ALU.mult)
                last.then_inc(s_wo_scaled, 1)

            def wo_lo(c):
                t = slice(4 * c, 4 * c + 4)
                eng.wait_ge(s_wohi, c + 1)
                eng.tensor_tensor(wol[:, t, :].rearrange("p a n -> p (a n)"), WOC[c],
                                  woh[:, t, :].rearrange("p a n -> p (a n)"), ALU.subtract).then_inc(s_wolo, 1)

            def dispatch(t):
                for k in range(2):
                    eng.indirect_dma_start(xrow_dram, bass.IndirectOffsetOnAxis(ap=sli[:, k, t:t + 1].bitcast(U32), axis=0),
                                           XROW[:, t, k, :], None).then_inc(s_scat_out, 16)

            def dispatch_pads():
                eng.memset(PADR, 0.0).then_inc(s_pad_zero, 1)
                eng.wait_ge(s_pad_zero, 1)
                eng.iota(PADR[:, :, 256].bitcast(I32), pattern=[[P, NPAD]], base=2 * T, channel_multiplier=1).then_inc(s_pad_rows, 1)
                eng.wait_ge(s_pad_slots, 1)
                eng.wait_ge(s_pad_rows, 1)
                for k in range(NPAD):
                    eng.indirect_dma_start(xrow_dram, bass.IndirectOffsetOnAxis(ap=sp[:, k:k + 1].bitcast(U32), axis=0),
                                           PADR[:, k, :], None).then_inc(s_scat_out, 16)

            def value_lo(b, j):
                u, _, up = ahead(b, j)
                if not has_proj(b * NH + j) or j % 2 == 0:
                    return
                eng.wait_ge(s_vhi_ready, u + 1)
                eng.tensor_tensor(vl[:, up, :, :].rearrange("p t n -> p (t n)"), v32,
                                  vh[:, up, :, :].rearrange("p t n -> p (t n)"), ALU.subtract).then_inc(s_vlo_ready, 1)

            def split(b, j):
                if j >= NH:
                    return
                k, q = j // 4, j % 4
                c = slice(q * GUW // 4, (q + 1) * GUW // 4)
                w = stage[:, k, c]
                hi = GU[:, ds(b, 1), k, 0, c].rearrange("p a n -> p (a n)")
                lo = GU[:, ds(b, 1), k, 1, c].rearrange("p a n -> p (a n)")
                sc = es_c[:, 0:1].to_broadcast([P, GUW // 4])
                eng.wait_ge(s_gu_in[k], b * 16 + 16)
                if isinstance(b, int) and b == 0 and j == 0:
                    eng.wait_ge(s_wqlo, NG)
                eng.tensor_tensor(hi, w, sc, ALU.mult).then_inc(s_gu_mul, 1)
                eng.tensor_tensor(w, w, sc, ALU.mult).then_inc(s_gu_mul, 1)
                eng.wait_ge(s_gu_mul, b * 16 + (2 * j + 2))
                eng.tensor_tensor(lo, w, hi, ALU.subtract).then_inc(s_gu_split, 1)

            def root(b, j, lag):
                n, par = b * NH + j, (j + lag) % 2
                if not has(n, lag):
                    return
                eng.wait_ge(s_meansq, n - lag + 1)
                eng.tensor_tensor(rm[:, par, :], ms[:, par, :], half_c[:, 0:2], ALU.pow).then_inc(s_rms, 1)

            def step(b, j):
                root(b, j, 1)
                split(b, j)
                value_lo(b, j)
                if isinstance(b, int) and b == 0:
                    dispatch(2 * j)
                    dispatch(2 * j + 1)
                    if j == NH - 1:
                        dispatch_pads()
                        eng.wait_ge(s_scat_out, 16 * (2 * NT + NPAD))

            value_lo(0, -1)
            for c in range(4):
                wo_lo(c)
            eng.wait_ge(s_slots_ready, 1)
            eng.wait_ge(s_fields, 3)
            eng.wait_ge(s_copied, 1)
            steps(eng, step)

            def scatter(t, j):
                i = t * 4 + j
                if isinstance(i, int) and i == 0:
                    return
                if pos(i):
                    eng.wait_ge(s_yev, i)
                eng.sem_inc(s_scatter_turn, 1)
                q = (j + 3) % 4
                eng.indirect_dma_start(y_dram, bass.IndirectOffsetOnAxis(ap=xg[:, q, 256:257].bitcast(U32), axis=0),
                                       yy[:, q, :], None).then_inc(s_y_out[q], 16)

            tiles(eng, scatter)
            for j in range(4):
                eng.wait_ge(s_y_out[j], 16 * ((NS + 3 - j) // 4))

        def three(o, ah, al_, bh, bl, first, last, **kw):
            nc.tensor.matmul(o, ah, bh, start=first, stop=False, **kw)
            nc.tensor.matmul(o, al_, bh, start=False, stop=False, **kw)
            return nc.tensor.matmul(o, ah, bl, start=False, stop=last, **kw)

        @block.tensor
        def _(eng):
            eng.wait_ge(s_consts, 16)
            eng.wait_ge(s_gw_ready, 2)

            def logits(t):
                b, tt = t // 2, t % 2
                eng.wait_ge(s_xTev, t + 1)
                for k in range(DK):
                    xs = [(xT2[:, b - 1, k, h, :] if b else xT[:, k, h, :])[:, tt * P:tt * P + P] for h in range(2)]
                    l = three(PS[:, 6, t * NE:t * NE + NE], xs[0], xs[1], gwh[:, k, :], gwl[:, k, :], k == 0, k == DK - 1)
                l.then_inc(s_lg_ready, 1)

            for t in range(NT):
                eng.wait_ge(s_xrow_ready, t // XT + 1)
                if t >= 4:
                    eng.wait_ge(s_xTev, t - 3)
                for q in range(4):
                    l = nc.tensor.transpose(PSH[2 + t % 4][:, q * P:q * P + P], XROWH[:, t, 0, q * P:q * P + P], ident16[:, :])
                l.then_inc(s_pt0_ready, 1)
                if t >= 2:
                    logits(t - 2)
            logits(NT - 2)
            logits(NT - 1)

            def proj(b, j, i):
                u, g, _ = ahead(b, j)
                if not has_proj(b * NH + j):
                    return
                if g == 0 and j == NH - 2 and i == 0:
                    eng.wait_ge(s_xT_in, b * 16 + 16)
                if isinstance(b, int) and u < NG and j % 2 == 0 and i == 0:
                    eng.wait_ge(s_wqhi, g + 1)
                    eng.wait_ge(s_wqlo, g + 1)
                bank = bPJ[i]
                if j % 2 == 0 and i == 1:
                    if pos(u):
                        eng.wait_ge(s_v32_ready, u)
                elif pos(u * 3 + (i + 1 if j % 2 else 0)):
                    eng.wait_ge(s_projhi, u * 3 + (i + 1 if j % 2 else 0))
                    eng.wait_ge(s_projlo, u * 3 + (i + 1 if j % 2 else 0))
                if j % 2 == 1 and i == 1:
                    vc = slice(g * WGC + 768, g * WGC + 768 + VD)
                    for tt in range(2):
                        tk = slice(tt * P, tt * P + P)
                        for k in range(DK):
                            l = three(bank[:, tt * VD:tt * VD + VD], xT[:, k, 0, tk], xT[:, k, 1, tk],
                                      wqh[:, k, vc], wql[:, k, vc], k == 0, k == DK - 1)
                else:
                    c0 = g * WGC + (i * 256 if j % 2 == 0 else 512)
                    for m in range(2):
                        c = c0 + m * P
                        for k in range(DK):
                            l = three(bank[:, m * S:m * S + S], wqh[:, k, c:c + P], wql[:, k, c:c + P],
                                      xT[:, k, 0, :], xT[:, k, 1, :], k == 0, k == DK - 1)
                l.then_inc(s_proj, 1)

            def score(b, j):
                n = b * NH + j
                if not has(n, 0):
                    return
                up, h = (j // 2) % 2, j % 2
                eng.wait_ge(s_projhi, (b * NG + j // 2) * 3 + 3)
                eng.wait_ge(s_projlo, (b * NG + j // 2) * 3 + 3)
                if pos(n):
                    eng.wait_ge(s_exped, n)
                for m in range(2):
                    q0, q1 = slice(0, P), slice(P, 2 * P)
                    hm = 2 * h + m
                    three(bS[:, m, 0:P], qh[:, up, hm, q0], ql[:, up, hm, q0], kh[:, up, m, q0], kl[:, up, m, q0], True, False)
                    nc.tensor.matmul(bS[:, m, 0:P], maskl[:, :], maskr[:, :], start=False, stop=True)
                    three(bS[:, m, P:3 * P], qh[:, up, hm, q1], ql[:, up, hm, q1], kh[:, up, m, :], kl[:, up, m, :], True, False)
                    l = nc.tensor.matmul(bS[:, m, 2 * P:3 * P], maskl[:, :], maskr[:, :], start=False, stop=True)
                l.then_inc(s_scores, 1)

            def transpose_p(b, j):
                n, par = b * NH + j, (j + 1) % 2
                if not has(n, 1):
                    return
                eng.wait_ge(s_pcomb, n)
                if pos(n - 1):
                    eng.wait_ge(s_pThi, n - 1)
                    eng.wait_ge(s_pTlo, n - 1)
                for q in range(3):
                    l = nc.tensor.transpose(bPT[:, q * P:q * P + P], pc[:, par, q * P:q * P + P], ident32[:, :])
                l.then_inc(s_pT, 1)

            def weigh_values(b, j):
                n, par, up = b * NH + j, (j + 1) % 2, (j - 1) // 2 % 2
                if not has(n, 1):
                    return
                eng.wait_ge(s_pThi, n)
                eng.wait_ge(s_pTlo, n)
                eng.wait_ge(s_vlo_ready, b * NG + (j - 1) // 2 + 1)
                if pos(n - 1):
                    eng.wait_ge(s_onorm, n - 1)
                v = [(vh[:, up, t, :], vl[:, up, t, :]) for t in range(2)]
                three(bPV[:, 0:VD], pth[:, par, 0:P], ptl[:, par, 0:P], *v[0], True, True)
                three(bPV[:, VD:2 * VD], pth[:, par, P:2 * P], ptl[:, par, P:2 * P], *v[0], True, False)
                l = three(bPV[:, VD:2 * VD], pth[:, par, 2 * P:3 * P], ptl[:, par, 2 * P:3 * P], *v[1], False, True)
                l.then_inc(s_pv, 1)

            def transpose_o(b, j):
                n, par = b * NH + j, j % 2
                if not has(n, 2):
                    return
                eng.wait_ge(s_onorm, n - 1)
                if pos(n - 2):
                    eng.wait_ge(s_oThi, n - 2)
                    eng.wait_ge(s_oTlo, n - 2)
                for q in range(2):
                    for eb in range(2):
                        l = nc.tensor.transpose(bOT[:, (q * 2 + eb) * P:(q * 2 + eb + 1) * P], on[:, par, q, eb * P:eb * P + P], ident32[:, :])
                l.then_inc(s_oT, 1)

            def project_out(b, j):
                n, par, hd = b * NH + j, j % 2, (j + NH - 2) % NH
                if not has(n, 2):
                    return
                eng.wait_ge(s_oThi, n - 1)
                eng.wait_ge(s_oTlo, n - 1)
                if isinstance(n, int) and n == 2:
                    eng.wait_ge(s_wolo, 4)
                if hd == 0 and pos(b):
                    eng.wait_ge(s_so_ready, b)
                for q in range(2):
                    for eb in range(2):
                        c = (q * 2 + eb) * P
                        l = three(bOUT[:, q * D:q * D + D], oth[:, par, c:c + P], otl[:, par, c:c + P],
                                  woh[:, 2 * hd + eb, :], wol[:, 2 * hd + eb, :],
                                  hd == 0 and q == 0 and eb == 0, hd == NH - 1 and q == 1 and eb == 1, skip_group_check=True)
                l.then_inc(s_heads_out, 1)

            def step(b, j):
                score(b, j)
                transpose_p(b, j)
                proj(b, j, 0)
                transpose_o(b, j)
                weigh_values(b, j)
                proj(b, j, 1)
                project_out(b, j)

            proj(0, -2, 0)
            proj(0, -2, 1)
            eng.wait_ge(s_M_ready, 1)
            for sh in range(1, NT):
                nc.tensor.matmul(PS[:, 7, sh * NE:P], ones16[:, :], M16[:, 0:P - sh * NE], start=sh == 1, stop=False, skip_group_check=True)
            nc.tensor.matmul(PS[:, 7, 0:P], sut[:, :], M16, start=False, stop=True, skip_group_check=True)
            for t in range(NT):
                l = nc.tensor.matmul(PS[:, 7, P:P + NE], ones16[:, :], M16[:, t * NE:t * NE + NE], start=t == 0, stop=t == NT - 1)
            l.then_inc(s_pre_ready, 1)
            proj(0, -1, 0)
            proj(0, -1, 1)
            steps(eng, step)

            def xt(t, j):
                t, j = t + j // 4, j % 4
                eng.wait_ge(s_xg_in[j], t * 16 + 16)
                if pos(t * 4 + j):
                    eng.wait_ge(s_xgT_ready, t * 4 + j)
                for q in range(4):
                    l = nc.tensor.transpose(PSH[7][:, q * P:q * P + P], xgh[:, j, q * P:q * P + P], ident16[:, :])
                l.then_inc(s_xgTp, 1)

            packed = [None]

            def tile(t, j):
                i = t * 4 + j
                par, last = j % 2, (j + 1) % 2
                if j == 0:
                    packed[0] = eng.value_load(texp[0:1, ds(t, 1)], min_val=0, max_val=(1 << 5 * EB) - 1)
                e = (packed[0] >> (EB * (j + 1))) & (NE - 1)
                e1 = (packed[0] >> (EB * j)) & (NE - 1)

                def gate_up(c):
                    cols = slice(c * 512, min(c * 512 + 512, GUW))
                    for k in range(DK):
                        w = [GU[:, ds(e, 1), k, h, cols].rearrange("p a n -> p (a n)") for h in range(2)]
                        xs = [xgT[:, par, (k * 2 + h) * P:(k * 2 + h + 1) * P] for h in range(2)]
                        l = three(GUP[:, par, cols], xs[0], xs[1], w[0], w[1], k == 0, k == DK - 1)
                    return l

                if not isinstance(i, int) or i < NS:
                    eng.wait_ge(s_xgT_ready, i + 1)
                    if pos(i - 1):
                        eng.wait_ge(s_hhi, i - 1)
                        eng.wait_ge(s_hlo, i - 1)
                    gate_up(0)
                if not isinstance(i, int) or i >= 1:
                    if pos(i):
                        eng.wait_ge(s_hmul, i)
                    for c in range(FB):
                        l = nc.tensor.transpose(GUP[:, last, c * P:c * P + P], h32[:, last, H0[c]:H0[c] + P], ident32[:, :])
                    l.then_inc(s_hTp, 1)
                if not isinstance(i, int) or i < NS:
                    gate_up(1)
                    gate_up(2).then_inc(s_gup, 1)
                    if not isinstance(i, int) or i + 1 < NS:
                        xt(t, j + 1)
                if not isinstance(i, int) or i >= 1:
                    if pos(i):
                        eng.wait_ge(s_hhi, i)
                        eng.wait_ge(s_hlo, i)
                    if pos(i - 1):
                        eng.wait_ge(s_yev, i - 1)
                    for c in range(FB):
                        w = [WD[:, ds(e1, 1), h, c, :].rearrange("p a n -> p (a n)") for h in range(2)]
                        l = three(PS[:, 6, 0:D], hh[:, last, c * P:c * P + P], hl[:, last, c * P:c * P + P], w[0], w[1], c == 0, c == FB - 1)
                    l.then_inc(s_yp, 1)

            eng.wait_ge(s_gu_split, 8 * NE)
            eng.wait_ge(s_texp_ready, 1)
            eng.wait_ge(s_so_ready, B)
            xt(0, 0)
            eng.wait_ge(s_wdhi, NE)
            eng.wait_ge(s_wdlo, NE)
            tiles(eng, tile)

        @block.scalar
        def _(eng):
            act = eng.activation
            eng.dma_start(lam_s[:, :, :].rearrange("p a b -> p (a b)"), lam_in.partition_broadcast(P)).then_inc(s_small_in, 16)
            eng.dma_start(gw_s[:, :, :], gw).then_inc(s_small_in, 16)
            eng.dma_start(qkb_s[:, :], qkb).then_inc(s_small_in, 16)
            eng.dma_start(sub_s[:, :], sub).then_inc(s_small_in, 16)
            eng.wait_ge(s_small_in, 16 * 4)
            act(gwh[:, :, :], gw_s[:, :, :], ACT.Copy, scale=WS).then_inc(s_gw_ready, 1)
            act(qkb64[:, :], qkb_s[:, :], ACT.Copy, scale=WS).then_inc(s_lam_ready, 1)
            eng.dma_start(vb_s[:, :, :].rearrange("p a b -> p (a b)"), vb.partition_broadcast(P)).then_inc(s_bias_in, 16)
            eng.dma_start(ob_s[:, :], outb.partition_broadcast(P)).then_inc(s_bias_in, 16)
            eng.dma_start(fb_s[:, :], fbias.partition_broadcast(P)).then_inc(s_bias_in, 16)
            eng.wait_ge(s_achain, 2)
            act(sm[:, 2:3], sm[:, 0:1], ACT.Exp).then_inc(s_lam_ready, 1)
            act(sm[:, 3:4], sm[:, 1:2], ACT.Exp).then_inc(s_lam_ready, 1)

            def rows_hi(c):
                t = slice(c * XT, (c + 1) * XT)
                eng.wait_ge(s_xn_ready, c + 1)
                act(XROWH[:, t, 0, 0:512].rearrange("p t (k h d) -> p t k h d", k=DK, h=2)[:, :, :, 0, :],
                    X0[:, t, :].rearrange("p t (k d) -> p t k d", k=DK), ACT.Copy).then_inc(s_xhi_ready, 1)

            def rows_T(c):
                for t in range(c * XT, (c + 1) * XT):
                    b, tt = t // 2, t % 2
                    eng.wait_ge(s_pt0_ready, t + 1)
                    dst = (xT2[:, b - 1, :, :, :] if b else xT)[:, :, :, tt * P:tt * P + P]
                    act(dst, PSH[2 + t % 4][:, 0:512].rearrange("p (k h t) -> p k h t", k=DK, h=2), ACT.Copy).then_inc(s_xTev, 1)

            def wq_hi(g):
                cols = slice(g * WGC, (g + 1) * WGC)
                eng.wait_ge(s_wq_in[g], 16)
                act(wqh[:, :, cols], WQ[:, :, cols], ACT.Copy, scale=WS).then_inc(s_wqhi, 1)

            rows_hi(0)
            rows_hi(1)
            rows_T(0)
            rows_hi(2)
            rows_T(1)
            rows_hi(3)
            wq_hi(0)
            rows_T(2)
            rows_T(3)
            for g in range(1, NG):
                wq_hi(g)

            def project_hi(b, j, i):
                n = b * NH + j
                u, g, up = ahead(b, j)
                if not has_proj(n):
                    return
                if j % 2 == 1 and i == 1:
                    eng.wait_ge(s_v32_ready, u + 1)
                    if pos(n - 1):
                        eng.wait_ge(s_pv, n - 1)
                    act(vh[:, up, :, :].rearrange("p t n -> p (t n)"), v32, ACT.Copy).then_inc(s_vhi_ready, 1)
                    return
                eng.wait_ge(s_proj, n * 2 + (5 + i))
                if pos(n - j % 2):
                    eng.wait_ge(s_scores, n - j % 2)
                for m in range(2):
                    dst = qh[:, up, 2 * i + m, :] if j % 2 == 0 else kh[:, up, m, :]
                    col = (4 * g + 2 * i + m) if j % 2 == 0 else 16 + 2 * g + m
                    l = act(dst, bPJ[i][:, m * S:m * S + S], ACT.Identity, bias=qkb64[:, col:col + 1])
                l.then_inc(s_projhi, 1)

            def exponentials(b, j):
                n, par = b * NH + j, j % 2
                if not has(n, 0):
                    return
                eng.wait_ge(s_negm, n + 1)
                if pos(n - 1):
                    eng.wait_ge(s_pcomb, n - 1)
                for m in range(2):
                    for q in range(2):
                        c = slice(0, P) if q == 0 else slice(P, 3 * P)
                        l = act(ee[:, par, m, c], bS[:, m, c], ACT.Exp, bias=ngm[:, par, q, m:m + 1], scale=SCALE,
                                accum_out=rs[:, par, m, q:q + 1])
                l.then_inc(s_exped, 1)

            def o_hi(b, j):
                n, par = b * NH + j, j % 2
                if not has(n, 2):
                    return
                eng.wait_ge(s_oT, n - 1)
                if pos(n - 3):
                    eng.wait_ge(s_heads_out, n - 3)
                act(oth[:, par, :], bOT, ACT.Copy).then_inc(s_oThi, 1)

            def p_hi(b, j):
                n, par = b * NH + j, (j + 1) % 2
                if not has(n, 1):
                    return
                eng.wait_ge(s_pT, n)
                if pos(n - 2):
                    eng.wait_ge(s_pv, n - 2)
                act(pth[:, par, :], bPT[:, 0:384], ACT.Copy).then_inc(s_pThi, 1)

            def squares(b, j):
                n, par = b * NH + j, (j + 1) % 2
                if not has(n, 1):
                    return
                eng.wait_ge(s_oscale, n)
                eng.wait_ge(s_pv, n)
                if pos(n - 1):
                    eng.wait_ge(s_sumsq, n - 1)
                if pos(n - 2):
                    eng.wait_ge(s_meansq, n - 2)
                for q in range(2):
                    l = act(junk[:, q, :], bPV[:, q * VD:q * VD + VD], ACT.Square, scale=al[:, par, 0, q:q + 1],
                            accum_out=ss[:, par, q:q + 1])
                l.then_inc(s_sumsq, 1)

            def normalise(b, j, lag):
                n, par = b * NH + j, (j + lag) % 2
                if not has(n, lag):
                    return
                eng.wait_ge(s_ocoef, n - lag + 1)
                if pos(n - lag - 1):
                    eng.wait_ge(s_oT, n - lag - 1)
                for q in range(2):
                    l = act(on[:, par, q, :], bPV[:, q * VD:q * VD + VD], ACT.Copy, scale=rc[:, par, q:q + 1])
                l.then_inc(s_onorm, 1)

            def step(b, j):
                normalise(b, j, 2)
                p_hi(b, j)
                project_hi(b, j, 0)
                o_hi(b, j)
                exponentials(b, j)
                squares(b, j)
                project_hi(b, j, 1)

            eng.wait_ge(s_lam_ready, 4)
            project_hi(0, -2, 0)
            project_hi(0, -2, 1)
            eng.wait_ge(s_dd_ready, 1)
            act(ex, dd, ACT.Exp).then_inc(s_expw, 1)
            project_hi(0, -1, 0)
            project_hi(0, -1, 1)
            for c in range(4):
                eng.wait_ge(s_wo_scaled, c + 1)
                act(woh[:, 4 * c:4 * c + 4, :].rearrange("p a n -> p (a n)"), WOC[c], ACT.Copy).then_inc(s_wohi, 1)
            eng.wait_ge(s_xT_out, 16 * (B - 1))
            steps(eng, step)

            for e in range(NE):
                st = stage[:, e % 2, :].rearrange("p (b n) -> p b n", b=FB)
                eng.wait_ge(s_wd_in[e % 2], 16 * (e // 2 + 1))
                act(WD[:, e, 0, :, :], st, ACT.Copy, scale=ES).then_inc(s_wdhi, 1)

            def tile(t, j):
                i, par, last = t * 4 + j, j % 2, (j + 1) % 2
                if not isinstance(i, int) or i >= 1:
                    if pos(i):
                        eng.wait_ge(s_hTp, i)
                    if pos(i - 2):
                        eng.wait_ge(s_yp, i - 2)
                    act(hh[:, last, :], GUP[:, last, 0:768], ACT.Copy).then_inc(s_hhi, 1)
                if not isinstance(i, int) or i < NS:
                    eng.wait_ge(s_gup, i + 1)
                    if pos(i - 1):
                        eng.wait_ge(s_hmul, i - 1)
                    act(sg[:, par, 0:FF], GUP[:, par, 0:FF], ACT.Silu, scale=1.0 / ES).then_inc(s_silu, 1)
                if not isinstance(i, int) or i >= 1:
                    q = (j + 3) % 4
                    if pos(i):
                        eng.wait_ge(s_yp, i)
                    if pos((t + (j + 3) // 4 - 1) * 16):
                        eng.wait_ge(s_y_out[q], (t + (j + 3) // 4 - 1) * 16)
                    act(yy[:, q, :], PS[:, 6, 0:D], ACT.Copy, scale=xg[:, q, 257:258]).then_inc(s_yev, 1)

            tiles(eng, tile)
            for b in range(8):
                eng.wait_ge(s_fin_add, b + 1)
                act(FY[:, 1, 2 * b:2 * b + 2, :], FY[:, 0, 2 * b:2 * b + 2, :], ACT.Silu).then_inc(s_fin_silu, 1)

        @block.vector
        def _(eng):
            v = nc.vector
            def link(ins, chain):
                chain[1] += 1
                ins.then_inc(chain[0], 1)
                eng.wait_ge(chain[0], chain[1])

            coefs = [s_achain, 0]
            routing = [s_route, 0]
            fsum = [s_fin_sum, 0]
            fmul = [s_fin_mul, 0]
            a = lambda ins: link(ins, coefs)
            r = lambda ins: link(ins, routing)

            def lambdas():
                eng.wait_ge(s_lam_ready, 3)
                a(v.tensor_tensor(sm[:, 4:5], sm[:, 2:3], sm[:, 3:4], ALU.subtract))
                a(v.tensor_scalar(sm[:, 5:6], sm[:, 4:5], LAMBDA_INIT, None, ALU.add))
                a(v.tensor_scalar(sm[:, 6:7].bitcast(I32), sm[:, 5:6].bitcast(I32), 0x7F800000, None, ALU.bitwise_and))
                a(v.tensor_scalar(sm[:, 7:8], sm[:, 6:7], 1.0, None, ALU.max))
                a(v.tensor_scalar(sm[:, 8:9].bitcast(I32), sm[:, 7:8].bitcast(I32), 23, None, ALU.logical_shift_right))
                a(v.tensor_copy(sm[:, 12:13], sm[:, 8:9].bitcast(I32)))
                a(v.tensor_scalar(sm[:, 13:14], sm[:, 12:13], -127.0, -math.log(2.0), ALU.add, ALU.mult))
                a(v.memset(lc[:, :, :], 0.0))
                a(v.tensor_scalar(lc[:, :, 0], lc[:, :, 0], sm[:, 13:14], None, ALU.add))
                v.tensor_scalar(sm[:, 9:10], sm[:, 5:6], -1.0, None, ALU.mult).then_inc(s_lam_ready, 1)

            def normalise_rows(c):
                eng.wait_ge(s_rstd_ready, c // 2 + 1)
                for t in range(c * XT, (c + 1) * XT):
                    last = v.tensor_scalar(X0[:, t, :], X0[:, t, :], mv[:, t, 0:1], rstd[:, t:t + 1], ALU.subtract, ALU.mult)
                last.then_inc(s_xn_ready, 1)

            def rows_lo(c):
                eng.wait_ge(s_xhi_ready, c + 1)
                t = slice(c * XT, (c + 1) * XT)
                hl_ = XROWH[:, t, 0, 0:512].rearrange("p t (k h d) -> p t k h d", k=DK, h=2)
                v.tensor_tensor(hl_[:, :, :, 1, :], X0[:, t, :].rearrange("p t (k d) -> p t k d", k=DK), hl_[:, :, :, 0, :],
                                ALU.subtract).then_inc(s_xrow_ready, 1)

            def wq_lo(g):
                cols = slice(g * WGC, (g + 1) * WGC)
                eng.wait_ge(s_wqhi, g + 1)
                v.scalar_tensor_tensor(out=wql[:, :, cols], in0=WQ[:, :, cols], scalar=WS, in1=wqh[:, :, cols],
                                       op0=ALU.mult, op1=ALU.subtract).then_inc(s_wqlo, 1)

            for h in range(2):
                for t in range(h * NT // 2, (h + 1) * NT // 2):
                    if t % XT == 0:
                        eng.wait_ge(s_x_in[t // XT], 16)
                    v.bn_stats(bn[:, t, :], X0[:, t, :]).then_inc(s_stats, 1)
                for t in range(h * NT // 2, (h + 1) * NT // 2):
                    eng.wait_ge(s_stats, t + 1)
                    v.bn_aggr(mv[:, t, :], bn[:, t, :]).then_inc(s_moments, 1)
                eng.wait_ge(s_moments, (h + 1) * NT // 2)
                c = slice(h * NT // 2, (h + 1) * NT // 2)
                v.tensor_scalar(ve[:, c], mv[:, c, 1], EPS, None, ALU.add).then_inc(s_var_ready, 1)
            eng.wait_ge(s_small_in, 16 * 4)
            for i in range(2):
                v.tensor_tensor_reduce(out=lam_s[:, 2 * i, :], in0=lam_s[:, 2 * i, :], in1=lam_s[:, 2 * i + 1, :], scale=1.0, scalar=0.0,
                                       op0=ALU.mult, op1=ALU.add, accum_out=sm[:, i:i + 1]).then_inc(s_achain, 1)
            coefs[1] = 2
            v.tensor_scalar(sub_s[:, :], sub_s[:, :], (1.0 - LAMBDA_INIT) * WS, None, ALU.mult).then_inc(s_sub_ready, 1)
            eng.wait_ge(s_gw_ready, 1)
            v.scalar_tensor_tensor(out=gwl[:, :, :], in0=gw_s[:, :, :], scalar=WS, in1=gwh[:, :, :], op0=ALU.mult, op1=ALU.subtract).then_inc(s_gw_ready, 1)
            normalise_rows(0)
            normalise_rows(1)
            rows_lo(0)
            rows_lo(1)
            normalise_rows(2)
            normalise_rows(3)
            rows_lo(2)
            rows_lo(3)
            lambdas()
            wq_lo(0)

            def project_lo(b, j, i):
                u, g, up = ahead(b, j)
                if not has_proj(b * NH + j):
                    return
                if j % 2 == 1 and i == 1:
                    eng.wait_ge(s_proj, u * 4 + 4)
                    if pos(u):
                        eng.wait_ge(s_vlo_ready, u)
                    v.tensor_tensor(v32.rearrange("p (t n) -> p t n", t=2), bPJ[1].rearrange("p (t n) -> p t n", t=2),
                                    vb_s[:, g, :].unsqueeze(1).to_broadcast([P, 2, VD]), ALU.add).then_inc(s_v32_ready, 1)
                    return
                eng.wait_ge(s_projhi, u * 3 + (i + 1 if j % 2 == 0 else 3))
                for m in range(2):
                    dst = ql[:, up, 2 * i + m, :] if j % 2 == 0 else kl[:, up, m, :]
                    hi_ = qh[:, up, 2 * i + m, :] if j % 2 == 0 else kh[:, up, m, :]
                    col = (4 * g + 2 * i + m) if j % 2 == 0 else 16 + 2 * g + m
                    last = v.scalar_tensor_tensor(out=dst, in0=bPJ[i][:, m * S:m * S + S], scalar=qkb64[:, col:col + 1],
                                                  in1=hi_, op0=ALU.add, op1=ALU.subtract)
                last.then_inc(s_projlo, 1)

            eng.wait_ge(s_lg_ready, NT)
            eng.wait_ge(s_kf_ready, 2)
            r(v.tensor_scalar(L, PS[:, 6, 0:P].rearrange("p (t e) -> p t e", t=NT), 1.0 / WS, None, ALU.mult))

            def bc(a):
                return a.unsqueeze(2).to_broadcast([P, NT, NE])

            def be(a):
                return a.unsqueeze(1).to_broadcast([P, NT, NE])

            for src, mm, q, kk, kmx, oh in ((L, m1, eq, key, km, oh1), (L2, m2, eq2, key2, km2, oh2)):
                r(v.tensor_reduce(mm, src, AX, ALU.max))
                r(v.tensor_tensor(q, src, bc(mm), ALU.is_equal))
                r(v.tensor_tensor(kk, q, be(rev[:, :]), ALU.mult))
                r(v.tensor_reduce(kmx, kk, AX, ALU.max))
                r(v.tensor_tensor(oh, kk, bc(kmx), ALU.is_equal))
                if src is L:
                    r(v.scalar_tensor_tensor(out=L2, in0=oh1, scalar=-3e38, in1=L, op0=ALU.mult, op1=ALU.add))
            v.tensor_tensor(dd, m2, m1, ALU.subtract).then_inc(s_dd_ready, 1)
            v.tensor_tensor(M16.rearrange("p (t e) -> p t e", t=NT), oh1, oh2, ALU.add).then_inc(s_M_ready, 1)
            project_lo(0, -2, 0)
            project_lo(0, -2, 1)
            wq_lo(1)
            eng.wait_ge(s_bias_in, 16 * 3)
            a(v.tensor_scalar(vb_s[:, :, :], vb_s[:, :, :], WS, None, ALU.mult))
            project_lo(0, -1, 0)
            project_lo(0, -1, 1)
            eng.wait_ge(s_pre_ready, 1)
            r(v.tensor_copy(tc[:, 1, :], PS[:, 7, P:P + NE]))
            r(v.tensor_scalar(cnti, tc[:, 1, :], float(P - 1), None, ALU.add))
            r(v.tensor_scalar(cnts, cnti, 7, None, ALU.logical_shift_right))
            r(v.tensor_copy(tc[:, 0, :], cnts))
            srce = tc
            for n, sh in enumerate((1, 2, 4)):
                d_ = scE[n]
                r(v.tensor_copy(d_[:, :, 0:sh], srce[:, :, 0:sh]))
                r(v.tensor_tensor(d_[:, :, sh:NE], srce[:, :, sh:NE], srce[:, :, 0:NE - sh], ALU.add))
                srce = d_
            ends = srce[:, 0, :]
            r(v.tensor_tensor(tcx, srce, tc, ALU.subtract))
            r(v.tensor_scalar(base, tcx[:, 0, :], float(P), None, ALU.mult))
            r(v.tensor_tensor(slot, PS[:, 7, 0:P].rearrange("p (t e) -> p t e", t=NT), be(base), ALU.add))
            r(v.tensor_tensor(ps1, oh1, slot, ALU.mult))
            r(v.tensor_tensor(ps2, oh2, slot, ALU.mult))
            r(v.tensor_reduce(slf[:, 0, :], ps1, AX, ALU.add))
            r(v.tensor_reduce(slf[:, 1, :], ps2, AX, ALU.add))
            v.tensor_copy(sli[:, :, :], slf).then_inc(s_slots_ready, 1)
            eng.wait_ge(s_expw, 1)
            r(v.tensor_scalar(ex1, ex, 1.0, None, ALU.add))
            r(v.reciprocal(w1, ex1))
            r(v.tensor_tensor(w2, ex, w1, ALU.mult))
            v.tensor_scalar(XROW[:, :, 0, 257], w1, 1.0 / (HS * ES), None, ALU.mult).then_inc(s_fields, 1)
            v.tensor_scalar(XROW[:, :, 1, 257], w2, 1.0 / (HS * ES), None, ALU.mult).then_inc(s_fields, 1)

            def tile_experts():
                r(v.tensor_copy(tf[:, :], ti[:, :]))
                r(v.tensor_tensor(te, tf[:, :].unsqueeze(2).to_broadcast([P, NS, NE - 1]),
                                  ends[:, 0:NE - 1].unsqueeze(1).to_broadcast([P, NS, NE - 1]), ALU.is_ge))
                r(v.memset(tefs, 0.0))
                r(v.tensor_reduce(tefs[:, 1:NS + 1], te, AX, ALU.add))
                src = tef[:, 0:NQ, 0]
                for m in range(1, 5):
                    col = tef[:, 0:NQ, m] if m < 4 else tef[:, 1:NQ + 1, 0]
                    r(v.scalar_tensor_tensor(out=tep[m - 1], in0=col, scalar=float(1 << EB * m), in1=src, op0=ALU.mult, op1=ALU.add))
                    src = tep[m - 1]
                v.tensor_copy(texp[:, :], src).then_inc(s_texp_ready, 1)

            def pad_slots():
                r(v.tensor_tensor(free, base, tcx[:, 1, :], ALU.subtract))
                r(v.tensor_tensor(pg, kf[:, :].unsqueeze(2).to_broadcast([P, NPAD, NE]), free.unsqueeze(1).to_broadcast([P, NPAD, NE]), ALU.is_ge))
                r(v.tensor_tensor(pg2, pg, tc[:, 1, :].unsqueeze(1).to_broadcast([P, NPAD, NE]), ALU.mult))
                r(v.tensor_reduce(pr, pg2, AX, ALU.add))
                r(v.tensor_tensor(prs, pr, kf[:, :], ALU.add))
                v.tensor_copy(sp[:, :], prs).then_inc(s_pad_slots, 1)

            def maxima(b, j):
                n, par = b * NH + j, j % 2
                if not has(n, 0):
                    return
                eng.wait_ge(s_scores, n + 1)
                if pos(n - 1):
                    eng.wait_ge(s_exped, n - 1)
                for q in range(2):
                    c = slice(0, P) if q == 0 else slice(P, 3 * P)
                    last = v.tensor_reduce(mx[:, par, q, :], bS[:, :, c], AX, ALU.max)
                last.then_inc(s_maxed, 1)
                eng.wait_ge(s_maxed, n + 1)
                v.scalar_tensor_tensor(out=ngm[:, par, :, :], in0=mx[:, par, :, :], scalar=-SCALE, in1=lc[:, :, :],
                                       op0=ALU.mult, op1=ALU.add).then_inc(s_negm, 1)

            def o_lo(b, j):
                n, par = b * NH + j, j % 2
                if not has(n, 2):
                    return
                eng.wait_ge(s_oThi, n - 1)
                if pos(n - 3):
                    eng.wait_ge(s_heads_out, n - 3)
                v.tensor_tensor(otl[:, par, :], bOT, oth[:, par, :], ALU.subtract).then_inc(s_oTlo, 1)

            def p_lo(b, j):
                n, par = b * NH + j, (j + 1) % 2
                if not has(n, 1):
                    return
                eng.wait_ge(s_pThi, n)
                if pos(n - 2):
                    eng.wait_ge(s_pv, n - 2)
                v.tensor_tensor(ptl[:, par, :], bPT[:, 0:384], pth[:, par, :], ALU.subtract).then_inc(s_pTlo, 1)

            def combine(b, j):
                n, par = b * NH + j, j % 2
                if not has(n, 0):
                    return
                eng.wait_ge(s_exped, n + 1)
                if pos(n - 1):
                    eng.wait_ge(s_coef, n - 1)
                v.reciprocal(ri[:, par, :, :], rs[:, par, :, :]).then_inc(s_rsum_inv, 1)
                eng.wait_ge(s_rsum_inv, n + 1)
                v.scalar_tensor_tensor(out=al[:, par, 1, :], in0=rs[:, par, 0, :], scalar=sm[:, 9:10], in1=ri[:, par, 1, :],
                                       op0=ALU.mult, op1=ALU.mult).then_inc(s_coef, 1)
                eng.wait_ge(s_coef, n + 1)
                if pos(n - 1):
                    eng.wait_ge(s_pT, n - 1)
                for q in range(2):
                    c = slice(0, P) if q == 0 else slice(P, 3 * P)
                    last = v.scalar_tensor_tensor(out=pc[:, par, c], in0=ee[:, par, 1, c], scalar=al[:, par, 1, q:q + 1],
                                                  in1=ee[:, par, 0, c], op0=ALU.mult, op1=ALU.add)
                last.then_inc(s_pcomb, 1)
                if pos(n - 1):
                    eng.wait_ge(s_ocoef, n - 1)
                v.tensor_scalar(al[:, par, 0, :], ri[:, par, 0, :], 1.0 / WS, None, ALU.mult).then_inc(s_oscale, 1)

            def mean_square(b, j, lag):
                n, par = b * NH + j, (j + lag) % 2
                if not has(n, lag):
                    return
                eng.wait_ge(s_sumsq, n - lag + 1)
                if pos(n - lag - 1):
                    eng.wait_ge(s_rms, n - lag - 1)
                v.tensor_scalar(ms[:, par, :], ss[:, par, :], 1.0 / VD, EPS, ALU.mult, ALU.add).then_inc(s_meansq, 1)

            def out_coef(b, j, lag):
                n, par = b * NH + j, (j + lag) % 2
                if not has(n, lag):
                    return
                eng.wait_ge(s_rms, n - lag + 1)
                if pos(n - lag - 1):
                    eng.wait_ge(s_onorm, n - lag - 1)
                v.tensor_tensor(rc[:, par, :], rm[:, par, :], al[:, par, 0, :], ALU.mult).then_inc(s_ocoef, 1)

            def rows_out(b, j):
                if j % NH != 1 or (isinstance(b, int) and b * NH + j < NH):
                    return
                bb = b + j // NH
                eng.wait_ge(s_heads_out, bb * NH)
                if pos((bb - 1) * 16):
                    eng.wait_ge(s_s_out, (bb - 1) * 16)
                v.scalar_tensor_tensor(out=so.rearrange("p (q d) -> p q d", q=2), in0=bOUT.rearrange("p (q d) -> p q d", q=2),
                                       scalar=1.0 / WS, in1=ob_s[:, :].unsqueeze(1).to_broadcast([P, 2, D]),
                                       op0=ALU.mult, op1=ALU.add).then_inc(s_so_ready, 1)

            def step(b, j):
                out_coef(b, j, 2)
                maxima(b, j)
                p_lo(b, j)
                o_lo(b, j)
                project_lo(b, j, 0)
                combine(b, j)
                mean_square(b, j, 1)
                project_lo(b, j, 1)
                rows_out(b, j)
                if isinstance(b, int) and b == 0 and j == 0:
                    eng.wait_ge(s_xrow_ready, XG)
                    v.tensor_copy(XROWH[:, :, 1, 0:512], XROWH[:, :, 0, 0:512]).then_inc(s_copied, 1)
                    wq_lo(2)
                    wq_lo(3)
                if isinstance(b, int) and b == 0 and j == 1:
                    pad_slots()
                if isinstance(b, int) and b == 0 and j == 3:
                    tile_experts()

            eng.wait_ge(s_xT_out, 16 * (B - 1))
            steps(eng, step)

            for e in range(NE):
                st = stage[:, e % 2, :].rearrange("p (b n) -> p b n", b=FB)
                eng.wait_ge(s_wdhi, e + 1)
                v.scalar_tensor_tensor(out=WD[:, e, 1, :, :], in0=st, scalar=ES, in1=WD[:, e, 0, :, :], op0=ALU.mult, op1=ALU.subtract).then_inc(s_wdlo, 1)

            def xev(i, j):
                eng.wait_ge(s_xgTp, i + 1)
                if pos(i - 1):
                    eng.wait_ge(s_gup, i - 1)
                v.tensor_copy(xgT[:, j % 2, :], PSH[7][:, 0:512]).then_inc(s_xgT_ready, 1)

            xev(0, 0)

            def tile(t, j):
                i, par, last = t * 4 + j, j % 2, (j + 1) % 2
                if not isinstance(i, int) or i >= 1:
                    if pos(i):
                        eng.wait_ge(s_hhi, i)
                    if pos(i - 2):
                        eng.wait_ge(s_yp, i - 2)
                    v.tensor_tensor(hl[:, last, :], GUP[:, last, 0:768], hh[:, last, :], ALU.subtract).then_inc(s_hlo, 1)
                if not isinstance(i, int) or i + 1 < NS:
                    xev(i + 1, j + 1)
                if not isinstance(i, int) or i < NS:
                    eng.wait_ge(s_silu, i + 1)
                    if pos(i - 1):
                        eng.wait_ge(s_hTp, i - 1)
                    v.scalar_tensor_tensor(out=h32[:, par, 0:FF], in0=GUP[:, par, FF:GUW], scalar=HS / ES, in1=sg[:, par, 0:FF],
                                           op0=ALU.mult, op1=ALU.mult).then_inc(s_hmul, 1)

            tiles(eng, tile)
            eng.wait_ge(s_fin_in, 64)
            bias = fb_s[:, :].unsqueeze(1).to_broadcast([P, 2, D])
            for b in range(8):
                t = slice(2 * b, 2 * b + 2)
                link(v.tensor_tensor(FY[:, 0, t, :], FY[:, 0, t, :], FY[:, 1, t, :], ALU.add), fsum)
                v.tensor_tensor(FY[:, 0, t, :], FY[:, 0, t, :], bias, ALU.add).then_inc(s_fin_add, 1)
            for b in range(8):
                t = slice(2 * b, 2 * b + 2)
                eng.wait_ge(s_fin_silu, b + 1)
                link(v.tensor_tensor(FSA[:, t, :], FSA[:, t, :], FY[:, 1, t, :], ALU.mult), fmul)
                v.tensor_tensor(FX[:, t, :], FX[:, t, :], FSA[:, t, :], ALU.add).then_inc(s_fin_done, 1)


def kernel(**inputs):
    import numpy as np
    import concourse.bacc as bacc
    from concourse.bass_utils import run_bass_kernel_spmd

    g = {k[3:]: np.asarray(a) for k, a in inputs.items()}
    c = np.ascontiguousarray
    wg = g["ffn_w_in_gate"].transpose(0, 2, 1).reshape(NE, DK, P, FF).transpose(0, 2, 1, 3)
    wu = g["ffn_w_in_up"].transpose(0, 2, 1).reshape(NE, DK, P, FF).transpose(0, 2, 1, 3)
    wd = np.zeros((NE, P, FB, D), np.float32)
    for b in range(FB):
        r = P if b < FB - 1 else FF - b * P
        wd[:, P - r:, b] = g["ffn_w_out"].transpose(0, 2, 1)[:, b * P:b * P + r]
    cols = np.concatenate([np.r_[q * 512:q * 512 + 512, 2048 + q * 256:2304 + q * 256, 3072 + q * 256:3328 + q * 256] for q in range(NG)])
    arrays = {
        "x": c(g["attn_hidden_states"].reshape(T, D)),
        "wqkv": c(g["attn_Wqkv_w"][cols].T.reshape(DK, P, 4096).transpose(1, 0, 2)),
        "qkb": c(g["attn_Wqkv_b"][:3072].reshape(24, P).T),
        "vb": c(g["attn_Wqkv_b"][3072:]),
        "lam_in": np.concatenate([g["attn_lambda_q1"], g["attn_lambda_k1"], g["attn_lambda_q2"], g["attn_lambda_k2"]]),
        "sub": c(g["attn_subln_w"].reshape(2, P).T),
        "wo": c(g["attn_out_w"].T.reshape(16, P, D).transpose(1, 0, 2).reshape(P, 16 * D)),
        "outb": c(g["attn_out_b"]),
        "gw": c(g["ffn_gate_w"].T.reshape(DK, P, NE).transpose(1, 0, 2)),
        "wgu": np.concatenate([wg, wu], axis=-1),
        "wd": wd,
        "fbias": c(g["ffn_bias"]),
    }
    nc = bacc.Bacc("TRN2", target_bir_lowering=False, num_devices=1)
    aps = {k: nc.dram_tensor(f"in_{k}", a.shape, mybir.dt.from_np(a.dtype), kind="ExternalInput").ap() for k, a in arrays.items()}
    out = nc.dram_tensor("out_0", (T, D), F32, kind="ExternalOutput").ap()
    build(nc, out=out, **aps)
    r = run_bass_kernel_spmd(nc, [{f"in_{k}": a for k, a in arrays.items()}], core_ids=[0])
    return r.results[0]["out_0"].reshape(B, S, D)
```

```python
import math
from contextlib import ExitStack

import concourse.bass as bass
from concourse import mybir

F32 = mybir.dt.float32
F16 = mybir.dt.float16
I32 = mybir.dt.int32
U32 = mybir.dt.uint32
ALU = mybir.AluOpType
ACT = mybir.ActivationFunctionType
AX = mybir.AxisListType.X
ds = bass.ds

P = 128
B, S, D = 8, 256, 256
T = B * S
NT = T // P
DK = D // P
NH = 8
HD = 128
VD = 256
NG = 4
NN = B * NH
NE = 8
FF = 704
FB = -(-FF // P)
H0 = [min(c * P, FF - P) for c in range(FB)]
GUW = 2 * FF
EB = 3
NS = 2 * T // P + NE - 1
NQ = NS // 4 + 1
N8 = (NQ - 2) // 2
SLOTS = NS * P
NPAD = (SLOTS - 2 * T) // P
XG = 4
XT = NT // XG
WGC = 4096 // NG
ROW = 516
LAMBDA_INIT = 0.8 - 0.6 * math.exp(-0.3)
EPS = 1e-5
WS = 64.0
ES = 32.0
HS = 16.0
SCALE = HD ** -0.5 / (WS * WS)
MASK = 65504.0
FMAX = 3.4028234e38


def build(nc, x, wqkv, qkb, vb, lam_in, sub, wo, outb, gw, wgu, wd, fbias, out):
    xrow_dram = nc.dram_tensor("xrow_dram", (SLOTS, ROW // 2), F32, kind="Internal").ap()
    y_dram = nc.dram_tensor("y_dram", (2 * T + NPAD * P, D), F32, kind="Internal").ap()
    xT_dram = nc.dram_tensor("xT_dram", (B * P, 4 * S), F16, kind="Internal").ap()
    s_dram = nc.dram_tensor("s_dram", (T, D), F32, kind="Internal").ap()

    with ExitStack() as ctx:
        def sb(name, shape, dt):
            return ctx.enter_context(nc.sbuf_tensor(name, shape, dt))

        def sem(name):
            return ctx.enter_context(nc.semaphore(name))

        GU = sb("GU", [P, NE, DK, 2, GUW], F16)
        gu32 = GU[:, :, :, :, :].rearrange("p e k h n -> p (e k h n)").bitcast(F32)
        EXP32 = DK * GUW
        WQ = gu32[:, 0:8192].rearrange("p (k n) -> p k n", k=DK)
        X0 = gu32[:, 3 * EXP32:3 * EXP32 + NT * D].rearrange("p (t d) -> p t d", t=NT)
        XR0 = 3 * EXP32 + NT * D
        XROW = gu32[:, XR0:XR0 + NT * 2 * ROW // 2].rearrange("p (t k w) -> p t k w", t=NT, k=2)
        XROWH = XROW.bitcast(F16)
        WO3 = gu32[:, XR0 + NT * ROW:XR0 + NT * ROW + 1024]
        PADR = gu32[:, 5632:5632 + NPAD * ROW // 2].rearrange("p (k w) -> p k w", k=NPAD)
        FX = gu32[:, 0:4096].rearrange("p (t d) -> p t d", t=NT)
        FY = gu32[:, 4096:12288].rearrange("p (k t d) -> p k t d", k=2, t=NT)
        stage = sb("stage", [P, 2, 1536], F32)
        W2 = sb("W2", [P, 24576], F16)
        wqh = W2[:, 0:8192].rearrange("p (k n) -> p k n", k=DK)
        wql = W2[:, 8192:16384].rearrange("p (k n) -> p k n", k=DK)
        woh = W2[:, 16384:20480].rearrange("p (t n) -> p t n", t=16)
        wol = W2[:, 20480:24576].rearrange("p (t n) -> p t n", t=16)
        slots = W2[:, :].bitcast(F32).rearrange("p (e n) -> p e n", e=NE)
        WDRAW = [stage[:, 0, :], slots[:, 2, :], slots[:, 3, :], slots[:, 4, :], stage[:, 1, :], slots[:, 7, :], stage[:, 0, :], stage[:, 1, :]]
        WD = W2[:, :].rearrange("p (e h b n) -> p e h b n", e=NE, h=2, b=FB)
        stg = stage[:, :, :].rearrange("p a n -> p (a n)")
        WOC = [stg[:, 0:1024], stg[:, 1024:2048], stg[:, 2048:3072], WO3]
        WK = sb("WK", [P, 11272], F32)
        at = [0]

        def view(words, dt=F32):
            v = WK[:, at[0]:at[0] + words]
            at[0] += words
            assert at[0] <= 11272
            return v if dt == F32 else v.bitcast(dt)

        xT2 = WK[:, 11264 - 7 * 512:11264].bitcast(F16).rearrange("p (b k h t) -> p b k h t", b=B - 1, k=DK, h=2)
        rt = X0.rearrange("p t d -> p (t d)")
        at[0] = 0
        xT = view(512, F16).rearrange("p (k h t) -> p k h t", k=DK, h=2)
        qh = view(1024, F16).rearrange("p (u m t) -> p u m t", u=2, m=4)
        ql = view(1024, F16).rearrange("p (u m t) -> p u m t", u=2, m=4)
        kh = view(512, F16).rearrange("p (u m t) -> p u m t", u=2, m=2)
        kl = view(512, F16).rearrange("p (u m t) -> p u m t", u=2, m=2)
        vh = view(512, F16).rearrange("p (u t n) -> p u t n", u=2, t=2)
        vl = view(512, F16).rearrange("p (u t n) -> p u t n", u=2, t=2)
        v32 = view(512)
        ee = view(2 * 2 * 384).rearrange("p (b m n) -> p b m n", b=2, m=2)
        pc = view(2 * 384).rearrange("p (b n) -> p b n", b=2)
        pth = view(384, F16).rearrange("p (b n) -> p b n", b=2)
        ptl = view(384, F16).rearrange("p (b n) -> p b n", b=2)
        on = view(1024).rearrange("p (b q n) -> p b q n", b=2, q=2)
        oth = view(512, F16).rearrange("p (b n) -> p b n", b=2)
        otl = view(512, F16).rearrange("p (b n) -> p b n", b=2)
        junk = view(512).rearrange("p (q n) -> p q n", q=2)
        so = view(512)
        at[0] = 0
        xg = view(4 * ROW // 2).rearrange("p (b w) -> p b w", b=4)
        xgh = xg.bitcast(F16)
        xgT = view(512, F16).rearrange("p (b n) -> p b n", b=2)
        sg = view(2 * 768).rearrange("p (b n) -> p b n", b=2)
        h32 = view(2 * 768).rearrange("p (b n) -> p b n", b=2)
        hh = view(768, F16).rearrange("p (b n) -> p b n", b=2)
        hl = view(768, F16).rearrange("p (b n) -> p b n", b=2)
        yy = view(1024).rearrange("p (b n) -> p b n", b=4)
        FS = view(4096).rearrange("p (t d) -> p t d", t=NT)

        ident16 = sb("ident16", [P, P], F16)
        ident32 = sb("ident32", [P, P], F32)
        maskl = sb("maskl", [P, P], F16)
        maskr = sb("maskr", [P, P], F16)
        sut = sb("sut", [P, P], F16)
        ones16 = sb("ones16", [P, P], F16)
        es_c = sb("es_c", [P, 1], F32)
        ws_c = sb("ws_c", [P, 1], F32)
        half_c = sb("half_c", [P, NT // 2], F32)
        ki = sb("ki", [P, NPAD], I32)
        kf = sb("kf", [P, NPAD], F32)
        sp = sb("sp", [P, NPAD], I32)
        rev = sb("rev", [P, NE], F32)
        revi = sb("revi", [P, NE], I32)
        ti = sb("ti", [P, NS], I32)
        tf = sb("tf", [P, NS], F32)
        qkb_s = sb("qkb_s", [P, 24], F32)
        qkb64 = sb("qkb64", [P, 24], F32)
        vb_s = sb("vb_s", [P, NG, VD], F32)
        ob_s = sb("ob_s", [P, D], F32)
        fb_s = sb("fb_s", [P, D], F32)
        lam_s = sb("lam_s", [P, 4, HD], F32)
        sub_s = sb("sub_s", [P, 2], F32)
        gw_s = sb("gw_s", [P, DK, NE], F32)
        gwh = sb("gwh", [P, DK, NE], F16)
        gwl = sb("gwl", [P, DK, NE], F16)
        sm = sb("sm", [P, 64], F32)
        rcp_c, eps_c, max_c = sm[:, 14:15], sm[:, 15:16], sm[:, 16:17]
        lc = sb("lc", [P, 2, 2], F32)
        bn = sb("bn", [P, NT, 6], F32)
        mv = sb("mv", [P, NT, 2], F32)
        ve = sb("ve", [P, NT], F32)
        rstd = sb("rstd", [P, NT], F32)
        mx = sb("mx", [P, 2, 2, 2], F32)
        ngm = sb("ngm", [P, 2, 2, 2], F32)
        rs = sb("rs", [P, 2, 2, 2], F32)
        ri = sb("ri", [P, 2, 2, 2], F32)
        al = sb("al", [P, 2, 2, 2], F32)
        am = sb("am", [P, 2, 2], F32)
        ss = sb("ss", [P, 2, 2], F32)
        ms = sb("ms", [P, 2, 2], F32)
        rm = sb("rm", [P, 2, 2], F32)
        rc = sb("rc", [P, 2, 2], F32)

        ra = [0]

        def rview(*shape):
            n = int(math.prod(shape))
            v = rt[:, ra[0]:ra[0] + n]
            ra[0] += n
            if len(shape) == 2:
                v = v.rearrange("p (a b) -> p a b", a=shape[0])
            return v

        L = rview(NT, NE)
        L2 = rview(NT, NE)
        m1 = rview(NT)
        m2 = rview(NT)
        km = rview(NT)
        km2 = rview(NT)
        eq = rview(NT, NE)
        eq2 = rview(NT, NE)
        key = rview(NT, NE)
        key2 = rview(NT, NE)
        oh1 = rview(NT, NE)
        oh2 = rview(NT, NE)
        M16 = rview(64).bitcast(F16)
        cnti = rview(NE).bitcast(I32)
        cnts = rview(NE).bitcast(I32)
        tc = rview(2, NE)
        scE = [rview(2, NE) for _ in range(3)]
        tcx = rview(2, NE)
        base = rview(NE)
        free = rview(NE)
        pg = rview(NPAD, NE)
        pg2 = rview(NPAD, NE)
        pr = rview(NPAD)
        prs = rview(NPAD)
        slot = rview(NT, NE)
        ps1 = rview(NT, NE)
        ps2 = rview(NT, NE)
        slf = rview(2, NT)
        dd = rview(NT)
        ex = rview(NT)
        ex1 = rview(NT)
        w1 = rview(NT)
        w2 = rview(NT)
        te = rview(NS, NE - 1)
        tef = rview(NQ + 1, 4)
        tefs = tef.rearrange("p a b -> p (a b)")
        tep = [rview(NQ) for _ in range(4)]
        texp = sb("texp", [P, NQ + N8], I32)
        texh = sb("texh", [P, N8], I32)
        sli = sb("sli", [P, 2, NT], I32)

        PS = ctx.enter_context(nc.psum_tensor("PS", [P, 8, 512], F32))
        PSH = [PS[:, i, :].bitcast(F16) for i in range(8)]
        bPJ = [PS[:, 0, :], PS[:, 1, :]]
        bS = PS[:, 2:4, :]
        GUP = PS[:, 0:6, :].rearrange("p (a b) n -> p a (b n)", a=2)
        bPT, bPV, bOT, bOUT = (PS[:, i, :] for i in (4, 5, 6, 7))

        s_x_in = [sem(f"s_x_in{i}") for i in range(XG)]
        s_wq_in = [sem(f"s_wq_in{i}") for i in range(NG)]
        s_small_in = sem("s_small_in")
        s_bias_in = sem("s_bias_in")
        s_wo_in = [sem(f"s_wo_in{i}") for i in range(4)]
        s_consts = sem("s_consts")
        s_stats = sem("s_stats")
        s_moments = sem("s_moments")
        s_var_ready = sem("s_var_ready")
        s_rstd_ready = sem("s_rstd_ready")
        s_xhi_ready = sem("s_xhi_ready")
        s_xn_ready = sem("s_xn_ready")
        s_xrow_ready = sem("s_xrow_ready")
        s_pt0_ready = sem("s_pt0_ready")
        s_xTev = sem("s_xTev")
        s_xT_out = sem("s_xT_out")
        s_gw_ready = sem("s_gw_ready")
        s_lg_ready = sem("s_lg_ready")
        s_route = sem("s_route")
        s_dd_ready = sem("s_dd_ready")
        s_M_ready = sem("s_M_ready")
        s_pre_ready = sem("s_pre_ready")
        s_slots_ready = sem("s_slots_ready")
        s_texp_ready = sem("s_texp_ready")
        s_fields = sem("s_fields")
        s_kf_ready = sem("s_kf_ready")
        s_pad_zero = sem("s_pad_zero")
        s_pad_rows = sem("s_pad_rows")
        s_pad_slots = sem("s_pad_slots")
        s_copied = sem("s_copied")
        s_sub_ready = sem("s_sub_ready")
        s_scat_out = sem("s_scat_out")
        s_wqhi = sem("s_wqhi")
        s_wqlo = sem("s_wqlo")
        s_wq3_scaled = sem("s_wq3_scaled")
        s_wq3lo = sem("s_wq3lo")
        s_wo_scaled = sem("s_wo_scaled")
        s_wohi = sem("s_wohi")
        s_wolo = sem("s_wolo")
        s_achain = sem("s_achain")
        s_lam_ready = sem("s_lam_ready")
        s_expw = sem("s_expw")
        s_xT_in = sem("s_xT_in")
        s_proj = sem("s_proj")
        s_projhi = sem("s_projhi")
        s_projlo = sem("s_projlo")
        s_v32_ready = sem("s_v32_ready")
        s_vhi_ready = sem("s_vhi_ready")
        s_vlo_ready = sem("s_vlo_ready")
        s_scores = sem("s_scores")
        s_maxed = sem("s_maxed")
        s_negm = sem("s_negm")
        s_exped = sem("s_exped")
        s_rsum_inv = sem("s_rsum_inv")
        s_coef = sem("s_coef")
        s_oscale = sem("s_oscale")
        s_omask = sem("s_omask")
        s_pcomb = sem("s_pcomb")
        s_pT = sem("s_pT")
        s_pThi = sem("s_pThi")
        s_pTlo = sem("s_pTlo")
        s_pv = sem("s_pv")
        s_sumsq = sem("s_sumsq")
        s_meansq = sem("s_meansq")
        s_rms = sem("s_rms")
        s_ocoef = sem("s_ocoef")
        s_onorm = sem("s_onorm")
        s_oT = sem("s_oT")
        s_oThi = sem("s_oThi")
        s_oTlo = sem("s_oTlo")
        s_heads_out = sem("s_heads_out")
        s_so_ready = sem("s_so_ready")
        s_s_out = sem("s_s_out")
        s_gu_in = [sem(f"s_gu_in{i}") for i in range(2)]
        s_gu_mul = sem("s_gu_mul")
        s_gu_split = sem("s_gu_split")
        s_wd_in = [sem(f"s_wd_in{i}") for i in range(NE)]
        s_wd_mul = sem("s_wd_mul")
        s_wd_pool = sem("s_wd_pool")
        s_wdhi = sem("s_wdhi")
        s_wdlo = sem("s_wdlo")
        s_xg_in = [sem(f"s_xg_in{i}") for i in range(4)]
        s_xgTp = sem("s_xgTp")
        s_xgT_ready = sem("s_xgT_ready")
        s_gup = sem("s_gup")
        s_silu = sem("s_silu")
        s_hmul = sem("s_hmul")
        s_hTp = sem("s_hTp")
        s_hhi = sem("s_hhi")
        s_hlo = sem("s_hlo")
        s_yp = sem("s_yp")
        s_yev = sem("s_yev")
        s_y_out = [sem(f"s_y_out{i}") for i in range(4)]
        s_scatter_turn = sem("s_scatter_turn")
        s_fin_x_in = sem("s_fin_x_in")
        s_fin_s_in = sem("s_fin_s_in")
        s_fin_y_in = [sem(f"s_fin_y_in{i}") for i in range(NT // 2)]
        s_fin_add = sem("s_fin_add")
        s_fin_mul = sem("s_fin_mul")
        s_fin_silu = sem("s_fin_silu")
        s_fin_done = sem("s_fin_done")
        s_fin_out = sem("s_fin_out")

        def pos(value):
            return not isinstance(value, int) or value > 0

        block = ctx.enter_context(nc.Block())

        def steps(eng, step):
            for j in range(NH):
                step(0, j)
            with eng.Fori(1, B - 1) as b:
                for j in range(NH):
                    step(b, j)
            for j in range(NH + 2):
                step(B - 1, j)

        def has(n, lag):
            return not isinstance(n, int) or 0 <= n - lag < NN

        def has_proj(n):
            return not isinstance(n, int) or n < NN - 2

        def ahead(b, j):
            u = b * NG + (j + 2) // 2
            return u, (j + 2) // 2 % NG, (j + 2) // 2 % 2

        def tiles(eng, step):
            for j in range(4):
                step(0, j)
            with eng.Fori(1, NS // 4) as t:
                for j in range(4):
                    step(t, j)
            for j in range(NS % 4 + 1):
                step(NS // 4, j)

        @block.sync
        def _(eng):
            eng.sem_inc(s_s_out, 16)
            for c in range(XG):
                rows = slice(c * XT * P, (c + 1) * XT * P)
                eng.dma_start(X0[:, c * XT:(c + 1) * XT, :], x[rows, :].rearrange("(t p) d -> p t d", p=P)).then_inc(s_x_in[c], 16)
            for g in range(NG):
                cols = slice(g * WGC, (g + 1) * WGC)
                eng.dma_start(WQ[:, :, cols], wqkv[:, :, cols]).then_inc(s_wq_in[g], 16)
            for c in range(4):
                eng.dma_start(WOC[c], wo[:, 1024 * c:1024 * c + 1024]).then_inc(s_wo_in[c], 16)
            for b in range(1, B):
                eng.wait_ge(s_xTev, 2 * b + 2)
                eng.dma_start(xT_dram[b * P:b * P + P, :],
                              xT2[:, b - 1, :, :, :].rearrange("p k h t -> p (k h t)")).then_inc(s_xT_out, 16)

            def load_xT(b):
                eng.dma_start(xT.rearrange("p k h t -> p (k h t)"), xT_dram[ds(b * P, P), :]).then_inc(s_xT_in, 16)

            def load_gu(e, k, before):
                if pos(before):
                    eng.wait_ge(s_gu_split, before)
                src = wgu[ds(e, 1), :, k, :].rearrange("a p n -> (a p) n")
                eng.dma_start(stage[:, k, 0:GUW], src).then_inc(s_gu_in[k], 16)

            def store_s(b):
                eng.wait_ge(s_so_ready, b + 1)
                eng.dma_start(s_dram[ds(b * S, S), :].rearrange("(q p) d -> p q d", p=P),
                              so.rearrange("p (q d) -> p q d", q=2)).then_inc(s_s_out, 16)

            eng.wait_ge(s_wohi, 4)
            eng.wait_ge(s_wolo, 4)
            load_gu(1, 0, 0)
            eng.wait_ge(s_xT_out, 16 * (B - 1))

            def batch(b):
                eng.wait_ge(s_proj, b * 16)
                load_xT(b)
                load_gu(b, 1, b * 8 - 8)
                store_s(b - 1)
                if not isinstance(b, int) or b + 1 < B:
                    load_gu(b + 1, 0, b * 8 - 4)

            batch(1)
            with eng.Fori(2, B - 1) as b:
                batch(b)
            batch(B - 1)
            load_gu(0, 0, 8 * (B - 2) + 4)
            load_gu(0, 1, 8 * (B - 2) + 8)
            def load_wd(e):
                eng.dma_start(WDRAW[e], wd[e]).then_inc(s_wd_in[e], 16)

            eng.wait_ge(s_gu_split, 8 * NE - 4)
            load_wd(0)
            eng.wait_ge(s_proj, 2 * NN)
            load_wd(1)
            load_wd(2)
            load_wd(3)
            eng.wait_ge(s_gu_split, 8 * NE)
            load_wd(4)

            def load(t, j):
                if isinstance(t, int) and 4 * t + j >= NS:
                    return
                if pos(t * 16):
                    eng.wait_ge(s_y_out[j], t * 16)
                eng.dma_start(xg[:, j, :], xrow_dram[ds(t * (4 * P) + j * P, P), :]).then_inc(s_xg_in[j], 16)

            eng.wait_ge(s_scat_out, 16 * (2 * NT + NPAD))
            eng.wait_ge(s_scores, NN)
            for j in range(4):
                load(0, j)
            store_s(B - 1)
            load_wd(5)
            eng.wait_ge(s_wd_pool, 1)
            load_wd(6)
            eng.wait_ge(s_wdlo, 5)
            load_wd(7)
            eng.wait_ge(s_s_out, 16 * B + 16)
            eng.dma_start(FS, s_dram.rearrange("(p t) d -> p t d", p=P)).then_inc(s_fin_s_in, 16)
            with eng.Fori(1, NS // 4) as t:
                for j in range(4):
                    load(t, j)
            for j in range(NS % 4):
                load(NS // 4, j)
            eng.wait_ge(s_gup, NS)
            eng.dma_start(FX, x.rearrange("(p t) d -> p t d", p=P)).then_inc(s_fin_x_in, 16)
            for j in range(4):
                eng.wait_ge(s_y_out[j], 16 * ((NS + 3 - j) // 4))
            y2 = y_dram[0:2 * T, :].rearrange("(k p t) d -> p k t d", k=2, p=P)
            for b in range(NT // 2):
                eng.dma_start(FY[:, :, 2 * b:2 * b + 2, :], y2[:, :, 2 * b:2 * b + 2, :]).then_inc(s_fin_y_in[b], 16)
            for b in range(NT // 2):
                eng.wait_ge(s_fin_done, b + 1)
                eng.dma_start(out.rearrange("(p t) d -> p t d", p=P)[:, 2 * b:2 * b + 2, :], FX[:, 2 * b:2 * b + 2, :]).then_inc(s_fin_out, 16)
            eng.wait_ge(s_fin_out, 16 * (NT // 2))

        @block.gpsimd
        def _(eng):
            eng.memset(ident16[:, :], 0.0).then_inc(s_consts, 1)
            eng.memset(ident32[:, :], 0.0).then_inc(s_consts, 1)
            eng.memset(maskl[:, :], 0.0).then_inc(s_consts, 1)
            eng.memset(maskr[:, :], 0.0).then_inc(s_consts, 1)
            eng.memset(sut[:, :], 1.0).then_inc(s_consts, 1)
            eng.wait_ge(s_consts, 5)
            for m, v in ((ident16, 1.0), (ident32, 1.0), (maskl, MASK)):
                eng.affine_select(out=m[:, :], in_=m[:, :], compare_op=ALU.not_equal, fill=v, base=0,
                                  pattern=[[-1, P]], channel_multiplier=1).then_inc(s_consts, 1)
            eng.affine_select(out=maskr[:, :], in_=maskr[:, :], compare_op=ALU.is_ge, fill=-MASK, base=0,
                              pattern=[[-1, P]], channel_multiplier=1).then_inc(s_consts, 1)
            eng.affine_select(out=sut[:, :], in_=sut[:, :], compare_op=ALU.is_ge, fill=0.0, base=-1,
                              pattern=[[1, P]], channel_multiplier=-1).then_inc(s_consts, 1)
            eng.memset(ones16[:, :], 1.0).then_inc(s_consts, 1)
            eng.memset(es_c[:, :], ES).then_inc(s_consts, 1)
            eng.memset(ws_c[:, :], WS).then_inc(s_consts, 1)
            eng.memset(half_c[:, :], -0.5).then_inc(s_consts, 1)
            eng.iota(ki[:, :], pattern=[[P, NPAD]], base=0, channel_multiplier=1).then_inc(s_consts, 1)
            eng.iota(revi[:, :], pattern=[[-1, NE]], base=NE, channel_multiplier=0).then_inc(s_consts, 1)
            eng.iota(ti[:, :], pattern=[[1, NS]], base=0, channel_multiplier=0).then_inc(s_consts, 1)
            eng.wait_ge(s_consts, 17)
            eng.tensor_copy(rev[:, :], revi[:, :]).then_inc(s_kf_ready, 1)
            eng.tensor_copy(kf[:, :], ki[:, :]).then_inc(s_kf_ready, 1)
            for h in range(2):
                c = slice(h * NT // 2, (h + 1) * NT // 2)
                eng.wait_ge(s_var_ready, h + 1)
                eng.tensor_tensor(rstd[:, c], ve[:, c], half_c[:, :], ALU.pow).then_inc(s_rstd_ready, 1)
            eng.iota(XROW[:, :, :, 256].bitcast(I32), pattern=[[P, NT], [T, 2]], base=0, channel_multiplier=1).then_inc(s_fields, 1)
            eng.wait_ge(s_sub_ready, 1)
            for c in range(4):
                w4 = WOC[c].rearrange("p (a e n) -> p a e n", a=2, e=2)
                eng.wait_ge(s_wo_in[c], 16)
                for eb in range(2):
                    last = eng.tensor_tensor(w4[:, :, eb, :], w4[:, :, eb, :], sub_s[:, eb:eb + 1].unsqueeze(2).to_broadcast([P, 2, D]), ALU.mult)
                last.then_inc(s_wo_scaled, 1)

            def wo_lo(c):
                t = slice(4 * c, 4 * c + 4)
                eng.wait_ge(s_wohi, c + 1)
                eng.tensor_tensor(wol[:, t, :].rearrange("p a n -> p (a n)"), WOC[c],
                                  woh[:, t, :].rearrange("p a n -> p (a n)"), ALU.subtract).then_inc(s_wolo, 1)

            def dispatch(t):
                eng.wait_ge(s_copied, t // XT + 1)
                for k in range(2):
                    eng.indirect_dma_start(xrow_dram, bass.IndirectOffsetOnAxis(ap=sli[:, k, t:t + 1].bitcast(U32), axis=0),
                                           XROW[:, t, k, :], None).then_inc(s_scat_out, 16)

            def pad_rows():
                eng.wait_ge(s_wqlo, NG - 1)
                eng.memset(PADR, 0.0).then_inc(s_pad_zero, 1)
                eng.wait_ge(s_pad_zero, 1)
                eng.iota(PADR[:, :, 256].bitcast(I32), pattern=[[P, NPAD]], base=2 * T, channel_multiplier=1).then_inc(s_pad_rows, 1)

            def dispatch_pads(k):
                eng.wait_ge(s_pad_slots, 1)
                eng.wait_ge(s_pad_rows, 1)
                eng.indirect_dma_start(xrow_dram, bass.IndirectOffsetOnAxis(ap=sp[:, k:k + 1].bitcast(U32), axis=0),
                                       PADR[:, k, :], None).then_inc(s_scat_out, 16)

            def value_lo(b, j):
                u, _, up = ahead(b, j)
                if not has_proj(b * NH + j) or j % 2 == 0:
                    return
                eng.wait_ge(s_vhi_ready, u + 1)
                eng.tensor_tensor(vl[:, up, :, :].rearrange("p t n -> p (t n)"), v32,
                                  vh[:, up, :, :].rearrange("p t n -> p (t n)"), ALU.subtract).then_inc(s_vlo_ready, 1)

            def split(b, j):
                if j >= NH or (isinstance(b, int) and b == 0):
                    return
                last = isinstance(b, int) and b == B - 1
                for n in (2 * j, 2 * j + 1) if last else (j,):
                    k, q = n // 4 % 2, n % 4
                    e = 0 if n >= 8 else b
                    c = slice(q * GUW // 4, (q + 1) * GUW // 4)
                    w = stage[:, k, c]
                    hi = GU[:, ds(e, 1), k, 0, c].rearrange("p a n -> p (a n)")
                    lo = GU[:, ds(e, 1), k, 1, c].rearrange("p a n -> p (a n)")
                    sc = es_c[:, 0:1].to_broadcast([P, GUW // 4])
                    eng.wait_ge(s_gu_in[k], (b + n // 8) * 16)
                    eng.tensor_tensor(hi, w, sc, ALU.mult).then_inc(s_gu_mul, 1)
                    eng.tensor_tensor(w, w, sc, ALU.mult).then_inc(s_gu_mul, 1)
                    eng.wait_ge(s_gu_mul, b * 16 + (2 * n - 14))
                    eng.tensor_tensor(lo, w, hi, ALU.subtract).then_inc(s_gu_split, 1)

            def wd_pool():
                w = WDRAW[0]
                hi, lo = (WD[:, 0, h, :, :].rearrange("p b n -> p (b n)") for h in range(2))
                sc = es_c[:, 0:1].to_broadcast([P, FB * D])
                eng.wait_ge(s_wd_in[0], 16)
                eng.wait_ge(s_proj, 2 * NN)
                eng.tensor_tensor(hi, w, sc, ALU.mult).then_inc(s_wd_mul, 1)
                eng.tensor_tensor(w, w, sc, ALU.mult).then_inc(s_wd_mul, 1)
                eng.wait_ge(s_wd_mul, 2)
                eng.tensor_tensor(lo, w, hi, ALU.subtract).then_inc(s_wd_pool, 1)

            def root(b, j, lag):
                n, par = b * NH + j, (j + lag) % 2
                if not has(n, lag):
                    return
                eng.wait_ge(s_meansq, n - lag + 1)
                eng.tensor_tensor(rm[:, par, :], ms[:, par, :], half_c[:, 0:2], ALU.pow).then_inc(s_rms, 1)

            def step(b, j):
                root(b, j, 1)
                split(b, j)
                value_lo(b, j)
                if isinstance(b, int) and b == 0:
                    dispatch(2 * j)
                    dispatch(2 * j + 1)
                    if j == 1:
                        pad_rows()
                    if 1 <= j:
                        dispatch_pads(j - 1)
                elif j == NH // 2 and not isinstance(b, int):
                    eng.wait_ge(s_scat_out, 16 * (2 * NT + NPAD))
                if isinstance(b, int) and b == B - 1 and j == NH:
                    wd_pool()

            cols = slice((NG - 1) * WGC, NG * WGC)
            eng.wait_ge(s_wqhi, NG)
            for k in range(DK):
                eng.tensor_tensor(WQ[:, k, cols], WQ[:, k, cols], ws_c[:, 0:1].to_broadcast([P, WGC]), ALU.mult).then_inc(s_wq3_scaled, 1)
            for k in range(DK):
                eng.wait_ge(s_wq3_scaled, k + 1)
                eng.tensor_tensor(wql[:, k, cols], WQ[:, k, cols], wqh[:, k, cols], ALU.subtract).then_inc(s_wq3lo, 1)
            value_lo(0, -1)
            for c in range(4):
                wo_lo(c)
            eng.wait_ge(s_slots_ready, 1)
            eng.wait_ge(s_fields, 3)
            steps(eng, step)

            def scatter(t, j):
                i = t * 4 + j
                if isinstance(i, int) and i == 0:
                    return
                if pos(i):
                    eng.wait_ge(s_yev, i)
                eng.sem_inc(s_scatter_turn, 1)
                q = (j + 3) % 4
                eng.indirect_dma_start(y_dram, bass.IndirectOffsetOnAxis(ap=xg[:, q, 256:257].bitcast(U32), axis=0),
                                       yy[:, q, :], None).then_inc(s_y_out[q], 16)

            tiles(eng, scatter)
            for j in range(4):
                eng.wait_ge(s_y_out[j], 16 * ((NS + 3 - j) // 4))
            eng.wait_ge(s_fin_x_in, 16)
            for b in range(NT // 2 - 1):
                t = slice(2 * b, 2 * b + 2)
                eng.wait_ge(s_fin_mul, b + 1)
                eng.tensor_tensor(FX[:, t, :], FX[:, t, :], FY[:, 1, t, :], ALU.add).then_inc(s_fin_done, 1)

        def three(o, ah, al_, bh, bl, first, last, **kw):
            nc.tensor.matmul(o, ah, bh, start=first, stop=False, **kw)
            nc.tensor.matmul(o, al_, bh, start=False, stop=False, **kw)
            return nc.tensor.matmul(o, ah, bl, start=False, stop=last, **kw)

        @block.tensor
        def _(eng):
            eng.wait_ge(s_consts, 17)
            eng.wait_ge(s_gw_ready, 2)

            def logits(t):
                b, tt = t // 2, t % 2
                eng.wait_ge(s_xTev, t + 1)
                for k in range(DK):
                    xs = [(xT2[:, b - 1, k, h, :] if b else xT[:, k, h, :])[:, tt * P:tt * P + P] for h in range(2)]
                    l = three(PS[:, 6, t * NE:t * NE + NE], xs[0], xs[1], gwh[:, k, :], gwl[:, k, :], k == 0, k == DK - 1)
                l.then_inc(s_lg_ready, 1)

            for t in range(NT):
                eng.wait_ge(s_xrow_ready, t // XT + 1)
                if t >= 4:
                    eng.wait_ge(s_xTev, t - 3)
                for q in range(4):
                    l = nc.tensor.transpose(PSH[2 + t % 4][:, q * P:q * P + P], XROWH[:, t, 0, q * P:q * P + P], ident16[:, :])
                l.then_inc(s_pt0_ready, 1)
                if t >= 2:
                    logits(t - 2)
            logits(NT - 2)
            logits(NT - 1)

            def proj(b, j, i):
                u, g, _ = ahead(b, j)
                if not has_proj(b * NH + j):
                    return
                if g == 0 and j == NH - 2 and i == 0:
                    eng.wait_ge(s_xT_in, b * 16 + 16)
                if isinstance(b, int) and u < NG and j % 2 == 0 and i == 0:
                    eng.wait_ge(s_wqhi, g + 1)
                    if g < NG - 1:
                        eng.wait_ge(s_wqlo, g + 1)
                    else:
                        eng.wait_ge(s_wq3lo, DK)
                bank = bPJ[i]
                if j % 2 == 0 and i == 1:
                    if pos(u):
                        eng.wait_ge(s_v32_ready, u)
                elif pos(u * 3 + (i + 1 if j % 2 else 0)):
                    eng.wait_ge(s_projhi, u * 3 + (i + 1 if j % 2 else 0))
                    eng.wait_ge(s_projlo, u * 3 + (i + 1 if j % 2 else 0))
                if j % 2 == 1 and i == 1:
                    vc = slice(g * WGC + 768, g * WGC + 768 + VD)
                    for tt in range(2):
                        tk = slice(tt * P, tt * P + P)
                        for k in range(DK):
                            l = three(bank[:, tt * VD:tt * VD + VD], xT[:, k, 0, tk], xT[:, k, 1, tk],
                                      wqh[:, k, vc], wql[:, k, vc], k == 0, k == DK - 1)
                else:
                    c0 = g * WGC + (i * 256 if j % 2 == 0 else 512)
                    for m in range(2):
                        c = c0 + m * P
                        for k in range(DK):
                            l = three(bank[:, m * S:m * S + S], wqh[:, k, c:c + P], wql[:, k, c:c + P],
                                      xT[:, k, 0, :], xT[:, k, 1, :], k == 0, k == DK - 1)
                l.then_inc(s_proj, 1)

            def xt(t, j):
                t, j = t + j // 4, j % 4
                eng.wait_ge(s_xg_in[j], t * 16 + 16)
                if pos(t * 4 + j):
                    eng.wait_ge(s_xgT_ready, t * 4 + j)
                if isinstance(t, int) and t * 4 + j == 0:
                    eng.wait_ge(s_oThi, NN)
                    eng.wait_ge(s_oTlo, NN)
                for q in range(4):
                    l = nc.tensor.transpose(PSH[6][:, q * P:q * P + P], xgh[:, j, q * P:q * P + P], ident16[:, :])
                l.then_inc(s_xgTp, 1)

            def score(b, j):
                n = b * NH + j
                if not has(n, 0):
                    return
                up, h = (j // 2) % 2, j % 2
                eng.wait_ge(s_projhi, (b * NG + j // 2) * 3 + 3)
                eng.wait_ge(s_projlo, (b * NG + j // 2) * 3 + 3)
                if pos(n):
                    eng.wait_ge(s_exped, n)
                for m in range(2):
                    q0, q1 = slice(0, P), slice(P, 2 * P)
                    hm = 2 * h + m
                    three(bS[:, m, 0:P], qh[:, up, hm, q0], ql[:, up, hm, q0], kh[:, up, m, q0], kl[:, up, m, q0], True, False)
                    nc.tensor.matmul(bS[:, m, 0:P], maskl[:, :], maskr[:, :], start=False, stop=True)
                    three(bS[:, m, P:3 * P], qh[:, up, hm, q1], ql[:, up, hm, q1], kh[:, up, m, :], kl[:, up, m, :], True, False)
                    l = nc.tensor.matmul(bS[:, m, 2 * P:3 * P], maskl[:, :], maskr[:, :], start=False, stop=True)
                l.then_inc(s_scores, 1)

            def transpose_p(b, j):
                n, par = b * NH + j, (j + 1) % 2
                if not has(n, 1):
                    return
                eng.wait_ge(s_pcomb, n)
                if pos(n - 1):
                    eng.wait_ge(s_pThi, n - 1)
                    eng.wait_ge(s_pTlo, n - 1)
                for q in range(3):
                    l = nc.tensor.transpose(bPT[:, q * P:q * P + P], pc[:, par, q * P:q * P + P], ident32[:, :])
                l.then_inc(s_pT, 1)

            def weigh_values(b, j):
                n, par, up = b * NH + j, (j + 1) % 2, (j - 1) // 2 % 2
                if not has(n, 1):
                    return
                eng.wait_ge(s_pThi, n)
                eng.wait_ge(s_pTlo, n)
                eng.wait_ge(s_vlo_ready, b * NG + (j - 1) // 2 + 1)
                if pos(n - 1):
                    eng.wait_ge(s_onorm, n - 1)
                v = [(vh[:, up, t, :], vl[:, up, t, :]) for t in range(2)]
                three(bPV[:, 0:VD], pth[:, par, 0:P], ptl[:, par, 0:P], *v[0], True, True)
                three(bPV[:, VD:2 * VD], pth[:, par, P:2 * P], ptl[:, par, P:2 * P], *v[0], True, False)
                l = three(bPV[:, VD:2 * VD], pth[:, par, 2 * P:3 * P], ptl[:, par, 2 * P:3 * P], *v[1], False, True)
                l.then_inc(s_pv, 1)

            def transpose_o(b, j):
                n, par = b * NH + j, j % 2
                if not has(n, 2):
                    return
                eng.wait_ge(s_onorm, n - 1)
                if pos(n - 2):
                    eng.wait_ge(s_oThi, n - 2)
                    eng.wait_ge(s_oTlo, n - 2)
                for q in range(2):
                    for eb in range(2):
                        l = nc.tensor.transpose(bOT[:, (q * 2 + eb) * P:(q * 2 + eb + 1) * P], on[:, par, q, eb * P:eb * P + P], ident32[:, :])
                l.then_inc(s_oT, 1)

            def project_out(b, j):
                n, par, hd = b * NH + j, j % 2, (j + NH - 2) % NH
                if not has(n, 2):
                    return
                eng.wait_ge(s_oThi, n - 1)
                eng.wait_ge(s_oTlo, n - 1)
                if isinstance(n, int) and n == 2:
                    eng.wait_ge(s_wolo, 4)
                if hd == 0 and pos(b):
                    eng.wait_ge(s_so_ready, b)
                for q in range(2):
                    for eb in range(2):
                        c = (q * 2 + eb) * P
                        l = three(bOUT[:, q * D:q * D + D], oth[:, par, c:c + P], otl[:, par, c:c + P],
                                  woh[:, 2 * hd + eb, :], wol[:, 2 * hd + eb, :],
                                  hd == 0 and q == 0 and eb == 0, hd == NH - 1 and q == 1 and eb == 1, skip_group_check=True)
                l.then_inc(s_heads_out, 1)

            def step(b, j):
                score(b, j)
                transpose_p(b, j)
                proj(b, j, 0)
                transpose_o(b, j)
                weigh_values(b, j)
                proj(b, j, 1)
                if isinstance(b, int) and b * NH + j == NN + 1:
                    xt(0, 0)
                project_out(b, j)

            proj(0, -2, 0)
            proj(0, -2, 1)
            eng.wait_ge(s_M_ready, 1)
            for sh in range(1, NT):
                nc.tensor.matmul(PS[:, 7, sh * NE:P], ones16[:, :], M16[:, 0:P - sh * NE], start=sh == 1, stop=False, skip_group_check=True)
            nc.tensor.matmul(PS[:, 7, 0:P], sut[:, :], M16, start=False, stop=True, skip_group_check=True)
            for t in range(NT):
                l = nc.tensor.matmul(PS[:, 7, P:P + NE], ones16[:, :], M16[:, t * NE:t * NE + NE], start=t == 0, stop=t == NT - 1)
            l.then_inc(s_pre_ready, 1)
            proj(0, -1, 0)
            proj(0, -1, 1)
            steps(eng, step)

            packed = [None]

            def tile(t, j):
                i = t * 4 + j
                par, last = j % 2, (j + 1) % 2
                e = (packed[0] >> (EB * (j + 1))) & (NE - 1)
                e1 = (packed[0] >> (EB * j)) & (NE - 1)

                def gate_up(c):
                    cols = slice(c * 512, min(c * 512 + 512, GUW))
                    for k in range(DK):
                        w = [GU[:, ds(e, 1), k, h, cols].rearrange("p a n -> p (a n)") for h in range(2)]
                        xs = [xgT[:, par, (k * 2 + h) * P:(k * 2 + h + 1) * P] for h in range(2)]
                        l = three(GUP[:, par, cols], xs[0], xs[1], w[0], w[1], k == 0, k == DK - 1)
                    return l

                if not isinstance(i, int) or i < NS:
                    eng.wait_ge(s_xgT_ready, i + 1)
                    if pos(i - 1):
                        eng.wait_ge(s_hhi, i - 1)
                        eng.wait_ge(s_hlo, i - 1)
                    gate_up(0)
                if not isinstance(i, int) or i >= 1:
                    if pos(i):
                        eng.wait_ge(s_hmul, i)
                    for c in range(FB):
                        l = nc.tensor.transpose(GUP[:, last, c * P:c * P + P], h32[:, last, H0[c]:H0[c] + P], ident32[:, :])
                    l.then_inc(s_hTp, 1)
                if not isinstance(i, int) or i < NS:
                    gate_up(1)
                    gate_up(2).then_inc(s_gup, 1)
                    if not isinstance(i, int) or i + 1 < NS:
                        xt(t, j + 1)
                if not isinstance(i, int) or i >= 1:
                    if pos(i):
                        eng.wait_ge(s_hhi, i)
                        eng.wait_ge(s_hlo, i)
                    if pos(i - 1):
                        eng.wait_ge(s_yev, i - 1)
                    if isinstance(i, int) and i == 1:
                        eng.wait_ge(s_so_ready, B)
                        eng.wait_ge(s_wd_pool, 1)
                    eng.wait_ge(s_wdlo, e1 + 1)
                    for c in range(FB):
                        w = [WD[:, ds(e1, 1), h, c, :].rearrange("p a n -> p (a n)") for h in range(2)]
                        l = three(PS[:, 7, 0:D], hh[:, last, c * P:c * P + P], hl[:, last, c * P:c * P + P], w[0], w[1], c == 0, c == FB - 1)
                    l.then_inc(s_yp, 1)

            eng.wait_ge(s_gu_split, 8 * NE)
            eng.wait_ge(s_texp_ready, 1)
            def load_experts(word, n):
                packed[0] = eng.value_load(texp[0:1, ds(word, 1)], min_val=0, max_val=(1 << (n + 1) * EB) - 1)

            load_experts(0, 4)
            for j in range(4):
                tile(0, j)
            with eng.Fori(0, N8) as u:
                load_experts(u + NQ, 8)
                for j in range(8):
                    tile(u * 2 + 1, j)
            load_experts(NQ - 1, 4)
            for j in range(NS % 4 + 1):
                tile(NQ - 1, j)

        @block.scalar
        def _(eng):
            act = eng.activation
            eng.dma_start(lam_s[:, :, :].rearrange("p a b -> p (a b)"), lam_in.partition_broadcast(P)).then_inc(s_small_in, 16)
            eng.dma_start(gw_s[:, :, :], gw).then_inc(s_small_in, 16)
            eng.dma_start(qkb_s[:, :], qkb).then_inc(s_small_in, 16)
            eng.dma_start(sub_s[:, :], sub).then_inc(s_small_in, 16)
            eng.wait_ge(s_small_in, 16 * 4)
            act(gwh[:, :, :], gw_s[:, :, :], ACT.Copy, scale=WS).then_inc(s_gw_ready, 1)
            act(qkb64[:, :], qkb_s[:, :], ACT.Copy, scale=WS).then_inc(s_lam_ready, 1)
            eng.dma_start(vb_s[:, :, :].rearrange("p a b -> p (a b)"), vb.partition_broadcast(P)).then_inc(s_bias_in, 16)
            eng.dma_start(ob_s[:, :], outb.partition_broadcast(P)).then_inc(s_bias_in, 16)
            eng.dma_start(fb_s[:, :], fbias.partition_broadcast(P)).then_inc(s_bias_in, 16)
            eng.wait_ge(s_achain, 2)
            act(sm[:, 2:3], sm[:, 0:1], ACT.Exp).then_inc(s_lam_ready, 1)
            act(sm[:, 3:4], sm[:, 1:2], ACT.Exp).then_inc(s_lam_ready, 1)

            def rows_hi(c):
                t = slice(c * XT, (c + 1) * XT)
                eng.wait_ge(s_xn_ready, c + 1)
                act(XROWH[:, t, 0, 0:512].rearrange("p t (k h d) -> p t k h d", k=DK, h=2)[:, :, :, 0, :],
                    X0[:, t, :].rearrange("p t (k d) -> p t k d", k=DK), ACT.Copy).then_inc(s_xhi_ready, 1)

            def rows_T(c):
                for t in range(c * XT, (c + 1) * XT):
                    b, tt = t // 2, t % 2
                    eng.wait_ge(s_pt0_ready, t + 1)
                    dst = (xT2[:, b - 1, :, :, :] if b else xT)[:, :, :, tt * P:tt * P + P]
                    act(dst, PSH[2 + t % 4][:, 0:512].rearrange("p (k h t) -> p k h t", k=DK, h=2), ACT.Copy).then_inc(s_xTev, 1)

            def wq_hi(g):
                cols = slice(g * WGC, (g + 1) * WGC)
                eng.wait_ge(s_wq_in[g], 16)
                act(wqh[:, :, cols], WQ[:, :, cols], ACT.Copy, scale=WS).then_inc(s_wqhi, 1)

            rows_hi(0)
            rows_hi(1)
            rows_T(0)
            rows_hi(2)
            rows_hi(3)
            rows_T(1)
            rows_T(2)
            wq_hi(0)
            rows_T(3)
            for g in range(1, NG):
                wq_hi(g)

            def wd_hi(e):
                eng.wait_ge(s_wd_in[e], 16)
                if e in (2, 3, 4):
                    eng.wait_ge(s_wdlo, e)
                if e == 7:
                    eng.wait_ge(s_wdlo, 6)
                act(WD[:, e, 0, :, :].rearrange("p b n -> p (b n)"), WDRAW[e], ACT.Copy, scale=ES).then_inc(s_wdhi, 1)

            def project_hi(b, j, i):
                n = b * NH + j
                u, g, up = ahead(b, j)
                if not has_proj(n):
                    return
                if j % 2 == 1 and i == 1:
                    eng.wait_ge(s_v32_ready, u + 1)
                    if pos(n - 1):
                        eng.wait_ge(s_pv, n - 1)
                    act(vh[:, up, :, :].rearrange("p t n -> p (t n)"), v32, ACT.Copy).then_inc(s_vhi_ready, 1)
                    return
                eng.wait_ge(s_proj, n * 2 + (5 + i))
                if pos(n - j % 2):
                    eng.wait_ge(s_scores, n - j % 2)
                for m in range(2):
                    dst = qh[:, up, 2 * i + m, :] if j % 2 == 0 else kh[:, up, m, :]
                    col = (4 * g + 2 * i + m) if j % 2 == 0 else 16 + 2 * g + m
                    l = act(dst, bPJ[i][:, m * S:m * S + S], ACT.Identity, bias=qkb64[:, col:col + 1])
                l.then_inc(s_projhi, 1)

            def exponentials(b, j):
                n, par = b * NH + j, j % 2
                if not has(n, 0):
                    return
                eng.wait_ge(s_negm, n + 1)
                if pos(n - 1):
                    eng.wait_ge(s_pcomb, n - 1)
                for m in range(2):
                    for q in range(2):
                        c = slice(0, P) if q == 0 else slice(P, 3 * P)
                        l = act(ee[:, par, m, c], bS[:, m, c], ACT.Exp, bias=ngm[:, par, q, m:m + 1], scale=SCALE,
                                accum_out=rs[:, par, m, q:q + 1])
                l.then_inc(s_exped, 1)

            def o_hi(b, j):
                n, par = b * NH + j, j % 2
                if not has(n, 2):
                    return
                eng.wait_ge(s_oT, n - 1)
                if pos(n - 3):
                    eng.wait_ge(s_heads_out, n - 3)
                act(oth[:, par, :], bOT, ACT.Copy).then_inc(s_oThi, 1)

            def p_hi(b, j):
                n, par = b * NH + j, (j + 1) % 2
                if not has(n, 1):
                    return
                eng.wait_ge(s_pT, n)
                if pos(n - 2):
                    eng.wait_ge(s_pv, n - 2)
                act(pth[:, par, :], bPT[:, 0:384], ACT.Copy).then_inc(s_pThi, 1)

            def squares(b, j):
                n, par = b * NH + j, (j + 1) % 2
                if not has(n, 1):
                    return
                eng.wait_ge(s_oscale, n)
                eng.wait_ge(s_pv, n)
                if pos(n - 1):
                    eng.wait_ge(s_sumsq, n - 1)
                if pos(n - 2):
                    eng.wait_ge(s_meansq, n - 2)
                for q in range(2):
                    l = act(junk[:, q, :], bPV[:, q * VD:q * VD + VD], ACT.Square, scale=al[:, par, 0, q:q + 1],
                            accum_out=ss[:, par, q:q + 1])
                l.then_inc(s_sumsq, 1)

            def normalise(b, j, lag):
                n, par = b * NH + j, (j + lag) % 2
                if not has(n, lag):
                    return
                eng.wait_ge(s_ocoef, n - lag + 1)
                if pos(n - lag - 1):
                    eng.wait_ge(s_oT, n - lag - 1)
                for q in range(2):
                    l = act(on[:, par, q, :], bPV[:, q * VD:q * VD + VD], ACT.Copy, scale=rc[:, par, q:q + 1])
                l.then_inc(s_onorm, 1)

            def step(b, j):
                normalise(b, j, 2)
                p_hi(b, j)
                project_hi(b, j, 0)
                o_hi(b, j)
                exponentials(b, j)
                squares(b, j)
                project_hi(b, j, 1)
                if isinstance(b, int) and b == B - 1 and j == NH + 1:
                    wd_hi(1)

            eng.wait_ge(s_lam_ready, 4)
            project_hi(0, -2, 0)
            project_hi(0, -2, 1)
            eng.wait_ge(s_dd_ready, 1)
            act(ex, dd, ACT.Exp).then_inc(s_expw, 1)
            project_hi(0, -1, 0)
            project_hi(0, -1, 1)
            for c in range(4):
                eng.wait_ge(s_wo_scaled, c + 1)
                act(woh[:, 4 * c:4 * c + 4, :].rearrange("p a n -> p (a n)"), WOC[c], ACT.Copy).then_inc(s_wohi, 1)
            eng.wait_ge(s_xT_out, 16 * (B - 1))
            steps(eng, step)

            wd_hi(2)
            wd_hi(3)

            def tile(t, j):
                i, par, last = t * 4 + j, j % 2, (j + 1) % 2
                if not isinstance(i, int) or i >= 1:
                    if pos(i):
                        eng.wait_ge(s_hTp, i)
                    if pos(i - 2):
                        eng.wait_ge(s_yp, i - 2)
                    act(hh[:, last, :], GUP[:, last, 0:768], ACT.Copy).then_inc(s_hhi, 1)
                if not isinstance(i, int) or i < NS:
                    eng.wait_ge(s_gup, i + 1)
                    if pos(i - 1):
                        eng.wait_ge(s_hmul, i - 1)
                    act(sg[:, par, 0:FF], GUP[:, par, 0:FF], ACT.Silu, scale=1.0 / ES).then_inc(s_silu, 1)
                if isinstance(i, int) and i == 0:
                    wd_hi(4)
                    wd_hi(5)
                if isinstance(i, int) and i == 1:
                    wd_hi(6)
                    wd_hi(7)

            tiles(eng, tile)
            for b in range(NT // 2):
                eng.wait_ge(s_fin_add, b + 1)
                act(FY[:, 1, 2 * b:2 * b + 2, :], FY[:, 0, 2 * b:2 * b + 2, :], ACT.Silu).then_inc(s_fin_silu, 1)

        @block.vector
        def _(eng):
            v = nc.vector
            def link(ins, chain):
                chain[1] += 1
                ins.then_inc(chain[0], 1)
                eng.wait_ge(chain[0], chain[1])

            coefs = [s_achain, 0]
            routing = [s_route, 0]
            a = lambda ins: link(ins, coefs)
            r = lambda ins: link(ins, routing)

            def lambdas():
                eng.wait_ge(s_lam_ready, 3)
                a(v.tensor_tensor(sm[:, 4:5], sm[:, 2:3], sm[:, 3:4], ALU.subtract))
                a(v.tensor_scalar(sm[:, 5:6], sm[:, 4:5], LAMBDA_INIT, None, ALU.add))
                a(v.tensor_scalar(sm[:, 6:7].bitcast(I32), sm[:, 5:6].bitcast(I32), 0x7F800000, None, ALU.bitwise_and))
                a(v.tensor_scalar(sm[:, 7:8], sm[:, 6:7], 1.0, None, ALU.max))
                a(v.tensor_scalar(sm[:, 8:9].bitcast(I32), sm[:, 7:8].bitcast(I32), 23, None, ALU.logical_shift_right))
                a(v.tensor_copy(sm[:, 12:13], sm[:, 8:9].bitcast(I32)))
                a(v.tensor_scalar(sm[:, 13:14], sm[:, 12:13], -127.0, -math.log(2.0), ALU.add, ALU.mult))
                a(v.reciprocal(rcp_c, sm[:, 7:8]))
                a(v.tensor_scalar(eps_c, rcp_c, rcp_c, EPS, ALU.mult, ALU.mult))
                a(v.tensor_scalar(eps_c, eps_c, 1e-36, None, ALU.max))
                a(v.tensor_scalar(max_c, rcp_c, FMAX, rcp_c, ALU.mult, ALU.mult))
                a(v.memset(lc[:, :, :], 0.0))
                a(v.tensor_scalar(lc[:, :, 0], lc[:, :, 0], sm[:, 13:14], None, ALU.add))
                v.tensor_scalar(sm[:, 9:10], sm[:, 5:6], -1.0, None, ALU.mult).then_inc(s_lam_ready, 1)

            def normalise_rows(c):
                eng.wait_ge(s_rstd_ready, c // 2 + 1)
                for t in range(c * XT, (c + 1) * XT):
                    last = v.tensor_scalar(X0[:, t, :], X0[:, t, :], mv[:, t, 0:1], rstd[:, t:t + 1], ALU.subtract, ALU.mult)
                last.then_inc(s_xn_ready, 1)

            def rows_lo(c):
                eng.wait_ge(s_xhi_ready, c + 1)
                t = slice(c * XT, (c + 1) * XT)
                hl_ = XROWH[:, t, 0, 0:512].rearrange("p t (k h d) -> p t k h d", k=DK, h=2)
                v.tensor_tensor(hl_[:, :, :, 1, :], X0[:, t, :].rearrange("p t (k d) -> p t k d", k=DK), hl_[:, :, :, 0, :],
                                ALU.subtract).then_inc(s_xrow_ready, 1)

            def wq_lo(g):
                cols = slice(g * WGC, (g + 1) * WGC)
                eng.wait_ge(s_wqhi, g + 1)
                v.scalar_tensor_tensor(out=wql[:, :, cols], in0=WQ[:, :, cols], scalar=WS, in1=wqh[:, :, cols],
                                       op0=ALU.mult, op1=ALU.subtract).then_inc(s_wqlo, 1)

            for h in range(2):
                for t in range(h * NT // 2, (h + 1) * NT // 2):
                    if t % XT == 0:
                        eng.wait_ge(s_x_in[t // XT], 16)
                    v.bn_stats(bn[:, t, :], X0[:, t, :]).then_inc(s_stats, 1)
                for t in range(h * NT // 2, (h + 1) * NT // 2):
                    eng.wait_ge(s_stats, t + 1)
                    v.bn_aggr(mv[:, t, :], bn[:, t, :]).then_inc(s_moments, 1)
                eng.wait_ge(s_moments, (h + 1) * NT // 2)
                c = slice(h * NT // 2, (h + 1) * NT // 2)
                v.tensor_scalar(ve[:, c], mv[:, c, 1], EPS, None, ALU.add).then_inc(s_var_ready, 1)
            eng.wait_ge(s_small_in, 16 * 4)
            for i in range(2):
                v.tensor_tensor_reduce(out=lam_s[:, 2 * i, :], in0=lam_s[:, 2 * i, :], in1=lam_s[:, 2 * i + 1, :], scale=1.0, scalar=0.0,
                                       op0=ALU.mult, op1=ALU.add, accum_out=sm[:, i:i + 1]).then_inc(s_achain, 1)
            coefs[1] = 2
            v.tensor_scalar(sub_s[:, :], sub_s[:, :], (1.0 - LAMBDA_INIT) * WS, None, ALU.mult).then_inc(s_sub_ready, 1)
            eng.wait_ge(s_gw_ready, 1)
            v.scalar_tensor_tensor(out=gwl[:, :, :], in0=gw_s[:, :, :], scalar=WS, in1=gwh[:, :, :], op0=ALU.mult, op1=ALU.subtract).then_inc(s_gw_ready, 1)
            normalise_rows(0)
            normalise_rows(1)
            rows_lo(0)
            rows_lo(1)
            normalise_rows(2)
            normalise_rows(3)
            rows_lo(2)
            rows_lo(3)
            lambdas()
            wq_lo(0)

            def project_lo(b, j, i):
                u, g, up = ahead(b, j)
                if not has_proj(b * NH + j):
                    return
                if j % 2 == 1 and i == 1:
                    eng.wait_ge(s_proj, u * 4 + 4)
                    if pos(u):
                        eng.wait_ge(s_vlo_ready, u)
                    v.tensor_tensor(v32.rearrange("p (t n) -> p t n", t=2), bPJ[1].rearrange("p (t n) -> p t n", t=2),
                                    vb_s[:, g, :].unsqueeze(1).to_broadcast([P, 2, VD]), ALU.add).then_inc(s_v32_ready, 1)
                    return
                eng.wait_ge(s_projhi, u * 3 + (i + 1 if j % 2 == 0 else 3))
                for m in range(2):
                    dst = ql[:, up, 2 * i + m, :] if j % 2 == 0 else kl[:, up, m, :]
                    hi_ = qh[:, up, 2 * i + m, :] if j % 2 == 0 else kh[:, up, m, :]
                    col = (4 * g + 2 * i + m) if j % 2 == 0 else 16 + 2 * g + m
                    last = v.scalar_tensor_tensor(out=dst, in0=bPJ[i][:, m * S:m * S + S], scalar=qkb64[:, col:col + 1],
                                                  in1=hi_, op0=ALU.add, op1=ALU.subtract)
                last.then_inc(s_projlo, 1)

            eng.wait_ge(s_lg_ready, NT)
            eng.wait_ge(s_kf_ready, 2)
            r(v.tensor_scalar(L, PS[:, 6, 0:P].rearrange("p (t e) -> p t e", t=NT), 1.0 / WS, None, ALU.mult))

            def bc(a):
                return a.unsqueeze(2).to_broadcast([P, NT, NE])

            def be(a):
                return a.unsqueeze(1).to_broadcast([P, NT, NE])

            for src, mm, q, kk, kmx, oh in ((L, m1, eq, key, km, oh1), (L2, m2, eq2, key2, km2, oh2)):
                r(v.tensor_reduce(mm, src, AX, ALU.max))
                r(v.tensor_tensor(q, src, bc(mm), ALU.is_equal))
                r(v.tensor_tensor(kk, q, be(rev[:, :]), ALU.mult))
                r(v.tensor_reduce(kmx, kk, AX, ALU.max))
                r(v.tensor_tensor(oh, kk, bc(kmx), ALU.is_equal))
                if src is L:
                    r(v.scalar_tensor_tensor(out=L2, in0=oh1, scalar=-3e38, in1=L, op0=ALU.mult, op1=ALU.add))
            v.tensor_tensor(dd, m2, m1, ALU.subtract).then_inc(s_dd_ready, 1)
            v.tensor_tensor(M16.rearrange("p (t e) -> p t e", t=NT), oh1, oh2, ALU.add).then_inc(s_M_ready, 1)
            project_lo(0, -2, 0)
            project_lo(0, -2, 1)
            wq_lo(1)
            eng.wait_ge(s_bias_in, 16 * 3)
            a(v.tensor_scalar(vb_s[:, :, :], vb_s[:, :, :], WS, None, ALU.mult))
            a(v.tensor_scalar(fb_s[:, :], fb_s[:, :], 0.5, None, ALU.mult))
            project_lo(0, -1, 0)
            project_lo(0, -1, 1)
            eng.wait_ge(s_pre_ready, 1)
            r(v.tensor_copy(tc[:, 1, :], PS[:, 7, P:P + NE]))
            r(v.tensor_scalar(cnti, tc[:, 1, :], float(P - 1), None, ALU.add))
            r(v.tensor_scalar(cnts, cnti, 7, None, ALU.logical_shift_right))
            r(v.tensor_copy(tc[:, 0, :], cnts))
            srce = tc
            for n, sh in enumerate((1, 2, 4)):
                d_ = scE[n]
                r(v.tensor_copy(d_[:, :, 0:sh], srce[:, :, 0:sh]))
                r(v.tensor_tensor(d_[:, :, sh:NE], srce[:, :, sh:NE], srce[:, :, 0:NE - sh], ALU.add))
                srce = d_
            ends = srce[:, 0, :]
            r(v.tensor_tensor(tcx, srce, tc, ALU.subtract))
            r(v.tensor_scalar(base, tcx[:, 0, :], float(P), None, ALU.mult))
            r(v.tensor_tensor(slot, PS[:, 7, 0:P].rearrange("p (t e) -> p t e", t=NT), be(base), ALU.add))
            r(v.tensor_tensor(ps1, oh1, slot, ALU.mult))
            r(v.tensor_tensor(ps2, oh2, slot, ALU.mult))
            r(v.tensor_reduce(slf[:, 0, :], ps1, AX, ALU.add))
            r(v.tensor_reduce(slf[:, 1, :], ps2, AX, ALU.add))
            v.tensor_copy(sli[:, :, :], slf).then_inc(s_slots_ready, 1)
            eng.wait_ge(s_expw, 1)
            r(v.tensor_scalar(ex1, ex, 1.0, None, ALU.add))
            r(v.reciprocal(w1, ex1))
            r(v.tensor_tensor(w2, ex, w1, ALU.mult))
            v.tensor_scalar(XROW[:, :, 0, 257], w1, 1.0 / (HS * ES), None, ALU.mult).then_inc(s_fields, 1)
            v.tensor_scalar(XROW[:, :, 1, 257], w2, 1.0 / (HS * ES), None, ALU.mult).then_inc(s_fields, 1)

            def tile_experts():
                r(v.tensor_copy(tf[:, :], ti[:, :]))
                r(v.tensor_tensor(te, tf[:, :].unsqueeze(2).to_broadcast([P, NS, NE - 1]),
                                  ends[:, 0:NE - 1].unsqueeze(1).to_broadcast([P, NS, NE - 1]), ALU.is_ge))
                r(v.memset(tefs, 0.0))
                r(v.tensor_reduce(tefs[:, 1:NS + 1], te, AX, ALU.add))
                src = tef[:, 0:NQ, 0]
                for m in range(1, 5):
                    col = tef[:, 0:NQ, m] if m < 4 else tef[:, 1:NQ + 1, 0]
                    r(v.scalar_tensor_tensor(out=tep[m - 1], in0=col, scalar=float(1 << EB * m), in1=src, op0=ALU.mult, op1=ALU.add))
                    src = tep[m - 1]
                r(v.tensor_copy(texp[:, 0:NQ], src))
                five = [texp[:, m:m + 2 * N8].rearrange("p (u m) -> p u m", m=2)[:, :, 0] for m in (1, 2)]
                r(v.tensor_scalar(texh[:, :], five[1], 4 * EB, None, ALU.logical_shift_left))
                v.tensor_tensor(texp[:, NQ:NQ + N8], five[0], texh[:, :], ALU.bitwise_or).then_inc(s_texp_ready, 1)

            def pad_slots():
                r(v.tensor_tensor(free, base, tcx[:, 1, :], ALU.subtract))
                r(v.tensor_tensor(pg, kf[:, :].unsqueeze(2).to_broadcast([P, NPAD, NE]), free.unsqueeze(1).to_broadcast([P, NPAD, NE]), ALU.is_ge))
                r(v.tensor_tensor(pg2, pg, tc[:, 1, :].unsqueeze(1).to_broadcast([P, NPAD, NE]), ALU.mult))
                r(v.tensor_reduce(pr, pg2, AX, ALU.add))
                r(v.tensor_tensor(prs, pr, kf[:, :], ALU.add))
                v.tensor_copy(sp[:, :], prs).then_inc(s_pad_slots, 1)

            def wd_lo(e):
                eng.wait_ge(s_wdhi, e)
                hi, lo = (WD[:, e, h, :, :].rearrange("p b n -> p (b n)") for h in range(2))
                v.scalar_tensor_tensor(out=lo, in0=WDRAW[e], scalar=ES, in1=hi, op0=ALU.mult, op1=ALU.subtract).then_inc(s_wdlo, 1)

            def xev(i, j):
                eng.wait_ge(s_xgTp, i + 1)
                if pos(i - 1):
                    eng.wait_ge(s_gup, i - 1)
                v.tensor_copy(xgT[:, j % 2, :], PSH[6][:, 0:512]).then_inc(s_xgT_ready, 1)

            def maxima(b, j):
                n, par = b * NH + j, j % 2
                if not has(n, 0):
                    return
                eng.wait_ge(s_scores, n + 1)
                if pos(n - 1):
                    eng.wait_ge(s_exped, n - 1)
                for q in range(2):
                    c = slice(0, P) if q == 0 else slice(P, 3 * P)
                    last = v.tensor_reduce(mx[:, par, q, :], bS[:, :, c], AX, ALU.max)
                last.then_inc(s_maxed, 1)
                eng.wait_ge(s_maxed, n + 1)
                v.scalar_tensor_tensor(out=ngm[:, par, :, :], in0=mx[:, par, :, :], scalar=-SCALE, in1=lc[:, :, :],
                                       op0=ALU.mult, op1=ALU.add).then_inc(s_negm, 1)

            def o_lo(b, j):
                n, par = b * NH + j, j % 2
                if not has(n, 2):
                    return
                eng.wait_ge(s_oThi, n - 1)
                if pos(n - 3):
                    eng.wait_ge(s_heads_out, n - 3)
                v.tensor_tensor(otl[:, par, :], bOT, oth[:, par, :], ALU.subtract).then_inc(s_oTlo, 1)

            def p_lo(b, j):
                n, par = b * NH + j, (j + 1) % 2
                if not has(n, 1):
                    return
                eng.wait_ge(s_pThi, n)
                if pos(n - 2):
                    eng.wait_ge(s_pv, n - 2)
                v.tensor_tensor(ptl[:, par, :], bPT[:, 0:384], pth[:, par, :], ALU.subtract).then_inc(s_pTlo, 1)

            def combine(b, j):
                n, par = b * NH + j, j % 2
                if not has(n, 0):
                    return
                eng.wait_ge(s_exped, n + 1)
                if pos(n - 1):
                    eng.wait_ge(s_coef, n - 1)
                v.reciprocal(ri[:, par, :, :], rs[:, par, :, :]).then_inc(s_rsum_inv, 1)
                eng.wait_ge(s_rsum_inv, n + 1)
                v.scalar_tensor_tensor(out=al[:, par, 1, :], in0=rs[:, par, 0, :], scalar=sm[:, 9:10], in1=ri[:, par, 1, :],
                                       op0=ALU.mult, op1=ALU.mult).then_inc(s_coef, 1)
                eng.wait_ge(s_coef, n + 1)
                if pos(n - 1):
                    eng.wait_ge(s_pT, n - 1)
                for q in range(2):
                    c = slice(0, P) if q == 0 else slice(P, 3 * P)
                    last = v.scalar_tensor_tensor(out=pc[:, par, c], in0=ee[:, par, 1, c], scalar=al[:, par, 1, q:q + 1],
                                                  in1=ee[:, par, 0, c], op0=ALU.mult, op1=ALU.add)
                last.then_inc(s_pcomb, 1)
                if pos(n - 1):
                    eng.wait_ge(s_ocoef, n - 1)
                v.tensor_scalar(al[:, par, 0, :], ri[:, par, 0, :], rcp_c, 1.0 / WS, ALU.mult, ALU.mult).then_inc(s_oscale, 1)

            def mean_square(b, j, lag):
                n, par = b * NH + j, (j + lag) % 2
                if not has(n, lag):
                    return
                eng.wait_ge(s_sumsq, n - lag + 1)
                if pos(n - lag - 1):
                    eng.wait_ge(s_rms, n - lag - 1)
                v.tensor_scalar(ms[:, par, :], ss[:, par, :], 1.0 / VD, eps_c, ALU.mult, ALU.add).then_inc(s_meansq, 1)
                v.scalar_tensor_tensor(out=am[:, par, :], in0=ss[:, par, :], scalar=max_c, in1=al[:, par, 0, :],
                                       op0=ALU.is_lt, op1=ALU.mult).then_inc(s_omask, 1)

            def out_coef(b, j, lag):
                n, par = b * NH + j, (j + lag) % 2
                if not has(n, lag):
                    return
                eng.wait_ge(s_rms, n - lag + 1)
                if pos(n - lag - 1):
                    eng.wait_ge(s_onorm, n - lag - 1)
                eng.wait_ge(s_omask, n - lag + 1)
                v.tensor_tensor(rc[:, par, :], rm[:, par, :], am[:, par, :], ALU.mult).then_inc(s_ocoef, 1)

            def rows_out(b, j):
                if j % NH != 1 or (isinstance(b, int) and b * NH + j < NH):
                    return
                bb = b + j // NH
                eng.wait_ge(s_heads_out, bb * NH)
                eng.wait_ge(s_s_out, bb * 16)
                v.scalar_tensor_tensor(out=so.rearrange("p (q d) -> p q d", q=2), in0=bOUT.rearrange("p (q d) -> p q d", q=2),
                                       scalar=1.0 / WS, in1=ob_s[:, :].unsqueeze(1).to_broadcast([P, 2, D]),
                                       op0=ALU.mult, op1=ALU.add).then_inc(s_so_ready, 1)

            def beside(b, j):
                if not isinstance(b, int) or b > 0:
                    return
                if j == 1:
                    wq_lo(2)
                if j < XG:
                    t = slice(j * XT, (j + 1) * XT)
                    eng.wait_ge(s_xrow_ready, j + 1)
                    v.tensor_copy(XROWH[:, t, 1, 0:512], XROWH[:, t, 0, 0:512]).then_inc(s_copied, 1)
                if j == 1:
                    pad_slots()
                if j == 3:
                    tile_experts()

            def step(b, j):
                out_coef(b, j, 2)
                maxima(b, j)
                p_lo(b, j)
                o_lo(b, j)
                project_lo(b, j, 0)
                combine(b, j)
                mean_square(b, j, 1)
                project_lo(b, j, 1)
                beside(b, j)
                if isinstance(b, int) and b * NH + j == NN + 1:
                    xev(0, 0)
                    eng.sem_inc(s_wdlo, 1)
                    wd_lo(1)
                rows_out(b, j)

            eng.wait_ge(s_xT_out, 16 * (B - 1))
            steps(eng, step)

            wd_lo(2)
            wd_lo(3)

            def tile(t, j):
                i, par, last = t * 4 + j, j % 2, (j + 1) % 2
                if not isinstance(i, int) or i >= 1:
                    if pos(i):
                        eng.wait_ge(s_hhi, i)
                    if pos(i - 2):
                        eng.wait_ge(s_yp, i - 2)
                    v.tensor_tensor(hl[:, last, :], GUP[:, last, 0:768], hh[:, last, :], ALU.subtract).then_inc(s_hlo, 1)
                if not isinstance(i, int) or i + 1 < NS:
                    xev(i + 1, j + 1)
                if not isinstance(i, int) or i < NS:
                    eng.wait_ge(s_silu, i + 1)
                    if pos(i - 1):
                        eng.wait_ge(s_hTp, i - 1)
                    v.scalar_tensor_tensor(out=h32[:, par, 0:FF], in0=GUP[:, par, FF:GUW], scalar=HS / ES, in1=sg[:, par, 0:FF],
                                           op0=ALU.mult, op1=ALU.mult).then_inc(s_hmul, 1)
                if isinstance(i, int) and i == 0:
                    wd_lo(4)
                    wd_lo(5)
                if isinstance(i, int) and i == 1:
                    wd_lo(6)
                    wd_lo(7)
                if not isinstance(i, int) or i >= 1:
                    q = (j + 3) % 4
                    if pos(i):
                        eng.wait_ge(s_yp, i)
                    v.scalar_tensor_tensor(out=yy[:, q, :], in0=PS[:, 7, 0:D], scalar=xg[:, q, 257:258], in1=fb_s[:, :],
                                           op0=ALU.mult, op1=ALU.add).then_inc(s_yev, 1)

            tiles(eng, tile)

            def before_gate(b):
                t = slice(2 * b, 2 * b + 2)
                eng.wait_ge(s_fin_y_in[b], 16)
                v.tensor_tensor(FY[:, 0, t, :], FY[:, 0, t, :], FY[:, 1, t, :], ALU.add).then_inc(s_fin_add, 1)

            def after_gate(b):
                t = slice(2 * b, 2 * b + 2)
                eng.wait_ge(s_fin_silu, b + 1)
                v.tensor_tensor(FY[:, 1, t, :], FS[:, t, :], FY[:, 1, t, :], ALU.mult).then_inc(s_fin_mul, 1)

            eng.wait_ge(s_fin_s_in, 16)
            for b in range(NT // 2):
                before_gate(b)
                if b >= 1:
                    after_gate(b - 1)
            after_gate(NT // 2 - 1)
            t = slice(NT - 2, NT)
            eng.wait_ge(s_fin_x_in, 16)
            eng.wait_ge(s_fin_mul, NT // 2)
            eng.wait_ge(s_fin_done, NT // 2 - 1)
            v.tensor_tensor(FX[:, t, :], FX[:, t, :], FY[:, 1, t, :], ALU.add).then_inc(s_fin_done, 1)


def kernel(**inputs):
    import numpy as np
    import concourse.bacc as bacc
    from concourse.bass_utils import run_bass_kernel_spmd

    g = {k[3:]: np.asarray(a) for k, a in inputs.items()}
    c = np.ascontiguousarray
    wg = g["ffn_w_in_gate"].transpose(0, 2, 1).reshape(NE, DK, P, FF).transpose(0, 2, 1, 3)
    wu = g["ffn_w_in_up"].transpose(0, 2, 1).reshape(NE, DK, P, FF).transpose(0, 2, 1, 3)
    wd = np.zeros((NE, P, FB, D), np.float32)
    for b in range(FB):
        r = P if b < FB - 1 else FF - b * P
        wd[:, P - r:, b] = g["ffn_w_out"].transpose(0, 2, 1)[:, b * P:b * P + r]
    cols = np.concatenate([np.r_[q * 512:q * 512 + 512, 2048 + q * 256:2304 + q * 256, 3072 + q * 256:3328 + q * 256] for q in range(NG)])
    arrays = {
        "x": c(g["attn_hidden_states"].reshape(T, D)),
        "wqkv": c(g["attn_Wqkv_w"][cols].T.reshape(DK, P, 4096).transpose(1, 0, 2)),
        "qkb": c(g["attn_Wqkv_b"][:3072].reshape(24, P).T),
        "vb": c(g["attn_Wqkv_b"][3072:]),
        "lam_in": np.concatenate([g["attn_lambda_q1"], g["attn_lambda_k1"], g["attn_lambda_q2"], g["attn_lambda_k2"]]),
        "sub": c(g["attn_subln_w"].reshape(2, P).T),
        "wo": c(g["attn_out_w"].T.reshape(16, P, D).transpose(1, 0, 2).reshape(P, 16 * D)),
        "outb": c(g["attn_out_b"]),
        "gw": c(g["ffn_gate_w"].T.reshape(DK, P, NE).transpose(1, 0, 2)),
        "wgu": np.concatenate([wg, wu], axis=-1),
        "wd": wd,
        "fbias": c(g["ffn_bias"]),
    }
    nc = bacc.Bacc("TRN2", target_bir_lowering=False, num_devices=1)
    aps = {k: nc.dram_tensor(f"in_{k}", a.shape, mybir.dt.from_np(a.dtype), kind="ExternalInput").ap() for k, a in arrays.items()}
    out = nc.dram_tensor("out_0", (T, D), F32, kind="ExternalOutput").ap()
    build(nc, out=out, **aps)
    r = run_bass_kernel_spmd(nc, [{f"in_{k}": a for k, a in arrays.items()}], core_ids=[0])
    return r.results[0]["out_0"].reshape(B, S, D)
```
